# Optimizing a Trainium2 kernel written in Bass

```python
import numpy as np
import jax
import jax.numpy as jnp

def _softmax(x, axis=-1):
    return jax.nn.softmax(x, axis=axis)
def _gelu(x):
    return jax.nn.gelu(x, approximate=True)
def _silu(x):
    return jax.nn.silu(x)
def _sigmoid(x):
    return jax.nn.sigmoid(x)
def _layernorm(x, axis=-1, eps=1e-5):
    m = jnp.mean(x, axis=axis, keepdims=True)
    v = jnp.var(x, axis=axis, keepdims=True)
    return (x - m) / jnp.sqrt(v + eps)
def _scatter_add(tgt, idx, src, axis=0):
    return tgt.at[idx].add(src)
def _segment_sum(src, seg, n):
    return jax.ops.segment_sum(src, seg, n)

kernel_name = 'mk_conv_seq_d2_conv_nchw512_9f2b76'

def setup_inputs(seed: int = 0):
    np.random.seed(seed)
    _w = jnp.asarray
    def _rec_inputs():
        import jax
        import jax.numpy as jnp
        _gk = jax.random.key(seed)
        x = -7.109e-05 + 0.9999 * jax.random.normal(jax.random.fold_in(_gk, 1), (8, 512, 128, 128), jnp.float32)
        return x
    x = _rec_inputs()
    def _L0_conv_setup():
        import jax, jax.numpy as jnp
        import numpy as np
        B, CH, H, W = (8, 512, 128, 128)
        K, N = (8, 2)
        KM_ITERS, EM_ITERS = (10, 10)
        EPS = 1e-06

        def _kmeans_labels(xs):
            c = xs.shape[0]
            init_idx = jnp.round(jnp.linspace(0.0, c - 1.0, K)).astype(jnp.int32)
            cent = xs[init_idx]
            x2 = (xs ** 2).sum(1, keepdims=True)
            for _ in range(KM_ITERS):
                d = x2 - 2.0 * (xs @ cent.T) + (cent ** 2).sum(1)[None, :]
                labels = jnp.argmin(d, axis=1)
                oh = jax.nn.one_hot(labels, K, dtype=xs.dtype)
                cnt = oh.sum(0)
                new_cent = oh.T @ xs / jnp.maximum(cnt, 1.0)[:, None]
                cent = jnp.where((cnt > 0.0)[:, None], new_cent, cent)
            d = x2 - 2.0 * (xs @ cent.T) + (cent ** 2).sum(1)[None, :]
            return jnp.argmin(d, axis=1)

        def _gmm_fit(data):
            b, P, k = data.shape
            pick = jnp.round(jnp.linspace(0.0, P - 1.0, N)).astype(jnp.int32)
            mu = data[:, pick, :]
            var = jnp.broadcast_to(data.var(axis=1, keepdims=True) + EPS, mu.shape)
            wts = jnp.full((b, N), 1.0 / N, dtype=data.dtype)
            log2pi = jnp.log(2.0 * jnp.pi).astype(data.dtype)
            for _ in range(EM_ITERS):
                diff2 = ((data[:, :, None, :] - mu[:, None, :, :]) ** 2 / var[:, None, :, :]).sum(-1)
                logdet = jnp.log(var).sum(-1)
                logp = -0.5 * (diff2 + logdet[:, None, :] + k * log2pi) + jnp.log(wts)[:, None, :]
                resp = jax.nn.softmax(logp, axis=2)
                Nk = resp.sum(1)
                mu = jnp.einsum('bpn,bpk->bnk', resp, data) / Nk[..., None]
                ex2 = jnp.einsum('bpn,bpk->bnk', resp, data ** 2) / Nk[..., None]
                var = jnp.maximum(ex2 - mu ** 2 + EPS, EPS)
                wts = Nk / P
            return (mu, var)

        def _bilinear_up_x2(x):
            b, c, h, w = x.shape

            def coords(n_in, n_out):
                s = jnp.linspace(0.0, n_in - 1.0, n_out)
                i0 = jnp.floor(s).astype(jnp.int32)
                i1 = jnp.minimum(i0 + 1, n_in - 1)
                return (i0, i1, (s - i0).astype(x.dtype))
            y0, y1, fy = coords(h, 2 * h)
            x0, x1, fx = coords(w, 2 * w)
            rows = x[:, :, y0, :] * (1.0 - fy)[None, None, :, None] + x[:, :, y1, :] * fy[None, None, :, None]
            return rows[:, :, :, x0] * (1.0 - fx) + rows[:, :, :, x1] * fx

        def _forward(sx, w_down, w_conv, w_up):
            c2 = sx.shape[1] // 2
            x = jax.lax.conv_general_dilated(sx, w_down, window_strides=(2, 2), padding=((1, 1), (1, 1)), feature_group_count=c2, dimension_numbers=('NCHW', 'OIHW', 'NCHW'))
            b, c, h, w = x.shape
            xx = jax.lax.stop_gradient(x[0].reshape(c, h * w))
            mn = xx.min(axis=1, keepdims=True)
            mx = xx.max(axis=1, keepdims=True)
            xs = (xx - mn) / jnp.maximum(mx - mn, 1e-12)
            labels = _kmeans_labels(xs)
            oh = jax.nn.one_hot(labels, K, dtype=xx.dtype)
            cnt = oh.sum(0)
            cl_mean = oh.T @ xx / jnp.maximum(cnt, 1.0)[:, None]
            v22 = cl_mean.std(axis=1)
            order = jnp.argsort(v22)
            inv = jnp.argsort(order)
            slabel = inv[labels]
            soh = jax.nn.one_hot(slabel, K, dtype=x.dtype)
            scnt = soh.sum(0)
            v5 = jnp.einsum('bchw,ck->bkhw', x, soh / jnp.maximum(scnt, 1.0)[None, :])
            wa = jax.lax.stop_gradient(v5.reshape(b, K, h * w).transpose(0, 2, 1))
            mu, var = _gmm_fit(wa)
            v6 = mu.transpose(0, 2, 1)
            v66 = var.transpose(0, 2, 1)
            box = jnp.take_along_axis(v6, jnp.argsort(v66, axis=2), axis=2)
            y = jax.nn.sigmoid(jnp.einsum('bkn,kn->bk', box, w_conv))
            gate = y[:, slabel]
            pre_up = gate[:, :, None, None] * x + x
            up = jnp.repeat(pre_up, 2, axis=1) * w_up[None, :, None, None]
            return _bilinear_up_x2(up) + sx
        key = jax.random.key(seed)
        k1, k2, k3, k4 = jax.random.split(key, 4)
        sx = jax.random.normal(k1, (B, CH, H, W), dtype=jnp.float32)
        w_down = jax.random.normal(k2, (CH // 2, 2, 3, 3), dtype=jnp.float32) * 0.1
        w_conv = jax.random.normal(k3, (K, N), dtype=jnp.float32) * 0.5
        w_up = jax.random.normal(k4, (CH,), dtype=jnp.float32) * 0.1
        return {'sx': sx, 'w_down': w_down, 'w_conv': w_conv, 'w_up': w_up}
    _L0_conv_all = _L0_conv_setup()
    _L0_conv_in = {k: v for k, v in _L0_conv_all.items() if k in ('w_down', 'w_conv', 'w_up', )}
    del _L0_conv_all

    def _L1_conv_setup():
        import jax, jax.numpy as jnp
        import numpy as np
        B, C, H, W = (8, 512, 128, 128)
        OD = max(C // 8, 2)
        KS = (0, 8, 0, 8)

        def getP(Hs, Ws, k):
            ind_h = 2.0 * np.arange(Hs) + 1.0
            Dht = np.stack([np.sqrt(2.0) / np.sqrt(Hs) * np.cos(u * ind_h * np.pi / (2.0 * Hs)) for u in range(Hs)]).astype(np.float32)
            Dht[0, :] = 1.0 / np.sqrt(Hs)
            Dh = Dht.T[:, k[0]:k[1]]
            ind_w = 2.0 * np.arange(Ws) + 1.0
            Dvt = np.stack([np.sqrt(2.0) / np.sqrt(Hs) * np.cos(u * ind_w * np.pi / (2.0 * Ws)) for u in range(Ws)]).astype(np.float32)
            Dvt[0, :] = 1.0 / np.sqrt(Ws)
            Dv = Dvt.T[:, k[2]:k[3]]
            P = np.einsum('hu,wv->hwuv', Dh, Dv).reshape(Hs * Ws, (k[1] - k[0]) * (k[3] - k[2]))
            return jnp.asarray(P)
        P_CONST = getP(H, W, KS)
        key = jax.random.key(seed)
        ks = jax.random.split(key, 6)
        x = jax.random.normal(ks[0], (B, C, H, W), dtype=jnp.float32)
        Wq = jax.random.normal(ks[1], (OD, C), dtype=jnp.float32) * 0.05
        Wk = jax.random.normal(ks[2], (OD, C), dtype=jnp.float32) * 0.05
        Wv = jax.random.normal(ks[3], (C, C), dtype=jnp.float32) * 0.05
        out_bias = jax.random.normal(ks[4], (1, C, 1), dtype=jnp.float32) * 0.01
        gamma = jax.random.normal(ks[5], (1,), dtype=jnp.float32) * 0.5
        return {'x': x, 'Wq': Wq, 'Wk': Wk, 'Wv': Wv, 'out_bias': out_bias, 'gamma': gamma}
    _L1_conv_all = _L1_conv_setup()
    _L1_conv_in = {k: v for k, v in _L1_conv_all.items() if k in ('Wq', 'Wk', 'Wv', 'out_bias', 'gamma', )}
    del _L1_conv_all

    return {
        "x": x,
        "L0_conv_w_down": _L0_conv_in["w_down"],
        "L0_conv_w_conv": _L0_conv_in["w_conv"],
        "L0_conv_w_up": _L0_conv_in["w_up"],
        "L1_conv_Wq": _L1_conv_in["Wq"],
        "L1_conv_Wk": _L1_conv_in["Wk"],
        "L1_conv_Wv": _L1_conv_in["Wv"],
        "L1_conv_out_bias": _L1_conv_in["out_bias"],
        "L1_conv_gamma": _L1_conv_in["gamma"],
    }

def reference(x, L0_conv_w_down, L0_conv_w_conv, L0_conv_w_up, L1_conv_Wq, L1_conv_Wk, L1_conv_Wv, L1_conv_out_bias, L1_conv_gamma):
    import jax
    import jax.numpy as jnp
    def _L0_conv_ref(sx, w_down, w_conv, w_up):
        import jax, jax.numpy as jnp
        import numpy as np
        B, CH, H, W = (8, 512, 128, 128)
        K, N = (8, 2)
        KM_ITERS, EM_ITERS = (10, 10)
        EPS = 1e-06

        def _kmeans_labels(xs):
            c = xs.shape[0]
            init_idx = jnp.round(jnp.linspace(0.0, c - 1.0, K)).astype(jnp.int32)
            cent = xs[init_idx]
            x2 = (xs ** 2).sum(1, keepdims=True)
            for _ in range(KM_ITERS):
                d = x2 - 2.0 * (xs @ cent.T) + (cent ** 2).sum(1)[None, :]
                labels = jnp.argmin(d, axis=1)
                oh = jax.nn.one_hot(labels, K, dtype=xs.dtype)
                cnt = oh.sum(0)
                new_cent = oh.T @ xs / jnp.maximum(cnt, 1.0)[:, None]
                cent = jnp.where((cnt > 0.0)[:, None], new_cent, cent)
            d = x2 - 2.0 * (xs @ cent.T) + (cent ** 2).sum(1)[None, :]
            return jnp.argmin(d, axis=1)

        def _gmm_fit(data):
            b, P, k = data.shape
            pick = jnp.round(jnp.linspace(0.0, P - 1.0, N)).astype(jnp.int32)
            mu = data[:, pick, :]
            var = jnp.broadcast_to(data.var(axis=1, keepdims=True) + EPS, mu.shape)
            wts = jnp.full((b, N), 1.0 / N, dtype=data.dtype)
            log2pi = jnp.log(2.0 * jnp.pi).astype(data.dtype)
            for _ in range(EM_ITERS):
                diff2 = ((data[:, :, None, :] - mu[:, None, :, :]) ** 2 / var[:, None, :, :]).sum(-1)
                logdet = jnp.log(var).sum(-1)
                logp = -0.5 * (diff2 + logdet[:, None, :] + k * log2pi) + jnp.log(wts)[:, None, :]
                resp = jax.nn.softmax(logp, axis=2)
                Nk = resp.sum(1)
                mu = jnp.einsum('bpn,bpk->bnk', resp, data) / Nk[..., None]
                ex2 = jnp.einsum('bpn,bpk->bnk', resp, data ** 2) / Nk[..., None]
                var = jnp.maximum(ex2 - mu ** 2 + EPS, EPS)
                wts = Nk / P
            return (mu, var)

        def _bilinear_up_x2(x):
            b, c, h, w = x.shape

            def coords(n_in, n_out):
                s = jnp.linspace(0.0, n_in - 1.0, n_out)
                i0 = jnp.floor(s).astype(jnp.int32)
                i1 = jnp.minimum(i0 + 1, n_in - 1)
                return (i0, i1, (s - i0).astype(x.dtype))
            y0, y1, fy = coords(h, 2 * h)
            x0, x1, fx = coords(w, 2 * w)
            rows = x[:, :, y0, :] * (1.0 - fy)[None, None, :, None] + x[:, :, y1, :] * fy[None, None, :, None]
            return rows[:, :, :, x0] * (1.0 - fx) + rows[:, :, :, x1] * fx

        def _forward(sx, w_down, w_conv, w_up):
            c2 = sx.shape[1] // 2
            x = jax.lax.conv_general_dilated(sx, w_down, window_strides=(2, 2), padding=((1, 1), (1, 1)), feature_group_count=c2, dimension_numbers=('NCHW', 'OIHW', 'NCHW'))
            b, c, h, w = x.shape
            xx = jax.lax.stop_gradient(x[0].reshape(c, h * w))
            mn = xx.min(axis=1, keepdims=True)
            mx = xx.max(axis=1, keepdims=True)
            xs = (xx - mn) / jnp.maximum(mx - mn, 1e-12)
            labels = _kmeans_labels(xs)
            oh = jax.nn.one_hot(labels, K, dtype=xx.dtype)
            cnt = oh.sum(0)
            cl_mean = oh.T @ xx / jnp.maximum(cnt, 1.0)[:, None]
            v22 = cl_mean.std(axis=1)
            order = jnp.argsort(v22)
            inv = jnp.argsort(order)
            slabel = inv[labels]
            soh = jax.nn.one_hot(slabel, K, dtype=x.dtype)
            scnt = soh.sum(0)
            v5 = jnp.einsum('bchw,ck->bkhw', x, soh / jnp.maximum(scnt, 1.0)[None, :])
            wa = jax.lax.stop_gradient(v5.reshape(b, K, h * w).transpose(0, 2, 1))
            mu, var = _gmm_fit(wa)
            v6 = mu.transpose(0, 2, 1)
            v66 = var.transpose(0, 2, 1)
            box = jnp.take_along_axis(v6, jnp.argsort(v66, axis=2), axis=2)
            y = jax.nn.sigmoid(jnp.einsum('bkn,kn->bk', box, w_conv))
            gate = y[:, slabel]
            pre_up = gate[:, :, None, None] * x + x
            up = jnp.repeat(pre_up, 2, axis=1) * w_up[None, :, None, None]
            return _bilinear_up_x2(up) + sx
        return _forward(sx, w_down, w_conv, w_up)

    def _L1_conv_ref(x, Wq, Wk, Wv, out_bias, gamma):
        import jax, jax.numpy as jnp
        import numpy as np
        B, C, H, W = (8, 512, 128, 128)
        OD = max(C // 8, 2)
        KS = (0, 8, 0, 8)

        def getP(Hs, Ws, k):
            ind_h = 2.0 * np.arange(Hs) + 1.0
            Dht = np.stack([np.sqrt(2.0) / np.sqrt(Hs) * np.cos(u * ind_h * np.pi / (2.0 * Hs)) for u in range(Hs)]).astype(np.float32)
            Dht[0, :] = 1.0 / np.sqrt(Hs)
            Dh = Dht.T[:, k[0]:k[1]]
            ind_w = 2.0 * np.arange(Ws) + 1.0
            Dvt = np.stack([np.sqrt(2.0) / np.sqrt(Hs) * np.cos(u * ind_w * np.pi / (2.0 * Ws)) for u in range(Ws)]).astype(np.float32)
            Dvt[0, :] = 1.0 / np.sqrt(Ws)
            Dv = Dvt.T[:, k[2]:k[3]]
            P = np.einsum('hu,wv->hwuv', Dh, Dv).reshape(Hs * Ws, (k[1] - k[0]) * (k[3] - k[2]))
            return jnp.asarray(P)
        P_CONST = getP(H, W, KS)
        Bb, Cc, Hh, Ww = x.shape
        HW = Hh * Ww
        P = P_CONST
        PT = P.T
        x2 = x.reshape(Bb, Cc, HW)
        xP = jnp.einsum('bcn,nk->bck', x2, P)
        WqxP = jnp.einsum('oc,bck->bok', Wq, xP)
        WkxP = jnp.einsum('oc,bck->bok', Wk, xP)
        WvxP = jnp.einsum('vc,bck->bvk', Wv, xP)
        lamdq = jnp.linalg.norm(jnp.einsum('bok,kn->bon', WqxP, PT), axis=1, keepdims=True)
        lamdk = jnp.linalg.norm(jnp.einsum('bok,kn->bon', WkxP, PT), axis=1, keepdims=True).reshape(Bb, HW, 1)
        fatt = jnp.einsum('bok,bol->bkl', WkxP, WqxP)
        lamdkP = P[None] / lamdk
        PTlamdq = PT[None] / lamdq
        sum_lamdkP = jnp.sum(lamdkP, axis=1, keepdims=True)
        lamdv = HW + jnp.einsum('bil,bln->bin', jnp.einsum('bik,bkl->bil', sum_lamdkP, fatt), PTlamdq)
        A = jnp.einsum('kn,bnl->bkl', PT, lamdkP)
        out = jnp.einsum('bkl,bln->bkn', jnp.einsum('bkm,bml->bkl', A, fatt), PTlamdq)
        out = out + jnp.sum(PT, axis=1, keepdims=True)
        out = jnp.einsum('bvk,bkn->bvn', WvxP, out / lamdv)
        out = out + out_bias
        return gamma * out.reshape(Bb, Cc, Hh, Ww) + x

    def _gn(v, G=32, eps=1e-5):
        B_, C_, H_, W_ = v.shape
        g = v.reshape(B_, G, C_ // G, H_, W_)
        m = jnp.mean(g, axis=(2, 3, 4), keepdims=True)
        s = jnp.var(g, axis=(2, 3, 4), keepdims=True)
        return ((g - m) / jnp.sqrt(s + eps)).reshape(v.shape)

    def _ln_c(v, eps=1e-6):
        m = jnp.mean(v, axis=1, keepdims=True)
        s = jnp.var(v, axis=1, keepdims=True)
        return (v - m) / jnp.sqrt(s + eps)

    def _ln_t(v, eps=1e-5):
        m = jnp.mean(v, axis=-1, keepdims=True)
        s = jnp.var(v, axis=-1, keepdims=True)
        return (v - m) / jnp.sqrt(s + eps)

    def _to_tokens(v):
        B_, C_, H_, W_ = v.shape
        return v.reshape(B_, C_, H_ * W_).transpose(0, 2, 1)
    def _from_tokens(t, like):
        B_, C_, H_, W_ = like.shape
        return t.transpose(0, 2, 1).reshape(B_, C_, H_, W_)

    x = _L0_conv_ref(x, L0_conv_w_down, L0_conv_w_conv, L0_conv_w_up)
    x = _L1_conv_ref(x, L1_conv_Wq, L1_conv_Wk, L1_conv_Wv, L1_conv_out_bias, L1_conv_gamma)
    return x


_drawn_inputs = setup_inputs


def setup_inputs(seed=0):
    import zlib

    import numpy as np

    out = dict(_drawn_inputs(seed))
    spreads = {}
    factors = {'L0_conv_w_conv': 8.0,
     'L1_conv_Wq': 8.0,
     'L1_conv_Wk': 8.0,
     'L1_conv_Wv': 8.0,
     'L1_conv_out_bias': 8.0}
    for name, (base, spread) in spreads.items():
        noise = np.random.default_rng([zlib.crc32(name.encode()), seed]).standard_normal(out[name].shape)
        drawn = base * np.exp(spread * noise) if base else spread * noise
        out[name] = jnp.asarray(drawn.astype(out[name].dtype))
    for name, factor in factors.items():
        out[name] = (out[name] * factor).astype(out[name].dtype)
    return out
```

```python
import concourse.bass as bass
from concourse import mybir
from contextlib import ExitStack

F32 = mybir.dt.float32
ALU = mybir.AluOpType
ACT = mybir.ActivationFunctionType
AX = mybir.AxisListType

B, C, H, W = 8, 512, 128, 128
P = 128
T, S = 2, 2
TS = T * S
HD, WD = H // 2, W // 2
POS = HD * WD
NT = POS // P
K, N = 8, 2
ITERS = 10
EPS = 1e-6
UV, LOW = 64, 8
HW = H * W
BN = B * N
LOG2PI = 1.8378770664093453

CONST_COLS = [("ident", P), ("ones", P), ("dw8", LOW), ("dh_e", H), ("dw_e", W), ("p_sum", 1),
              ("bias_row", UV + 2), ("sel_mu", P), ("sel_ex", P), ("mask_x", BN), ("mask_x2", BN),
              ("mask_term", BN), ("block", BN), ("block_k", B), ("is_x2", 1), ("tie", K), ("before", K * K),
              ("pick0", T * K), ("rank", 1), ("mean", 1)]
CONST_AT, CONST_N = {}, 0
for _name, _width in CONST_COLS:
    CONST_AT[_name] = slice(CONST_N, CONST_N + _width)
    CONST_N += _width
SECOND_N = CONST_AT["sel_mu"].start


class Chain:

    def __init__(self, eng, sem, start=0):
        self.eng, self.sem, self.n = eng, sem, start

    def link(self, ins):
        self.n = self.n + 1
        ins.then_inc(self.sem, 1)
        self.eng.wait_ge(self.sem, self.n)


FREE = 1


def start_free(eng, sems):
    for sem in sems:
        eng.sem_inc(sem, FREE)


class Scope:

    def __init__(self, nc, name):
        self.nc, self.name, self.ctx = nc, name, ExitStack()

    def __enter__(self):
        self.ctx.__enter__()
        return self

    def __exit__(self, *e):
        return self.ctx.__exit__(*e)

    def sb(self, name, shape):
        return self.ctx.enter_context(self.nc.sbuf_tensor(f"{self.name}_{name}", shape, F32))

    def ps(self, name, shape):
        return self.ctx.enter_context(self.nc.psum_tensor(f"{self.name}_{name}", shape, F32))

    def sem(self, name):
        return self.ctx.enter_context(self.nc.semaphore(f"{self.name}_{name}"))


TAPS = [(s, dh, dw) for dw in (0, 1) for dh in (-1, 0, 1) for s in range(S)] + \
       [(s, dh, -1) for dh in (-1, 0, 1) for s in range(S)]
ROWS1 = 32
CH1 = H // ROWS1
TAPS_LEFT = len(TAPS) - 1
OUT1 = ROWS1 // 2
QUADS = S * ROWS1 // 4
SLOTS = 4


def tap_window(buf, tap, rows, row0=0):
    s, dh, dw = tap
    top = 1 + dh + 2 * row0
    left = dw if dw >= 0 else 1
    return buf[:, s, top:top + 2 * rows - 1:2, left:left + 2 * (WD - (dw < 0)) - 1:2]


def first_pass(nc, x, w_down, p_cols, consts, xd, xps):
    xv = x.rearrange("b (t g s) h w -> (b t) g s (h w)", t=T, s=S)
    with Scope(nc, "first") as sc:
        xt = [sc.sb(f"x{c}", [P, S, ROWS1 + 1, W]) for c in range(CH1)]
        p_sb = sc.sb("p", [P, H, UV])
        cst = sc.sb("const", [P, P])
        wd = sc.sb("wd", [P, T, S * 9])
        acc = [sc.sb(f"acc{i}", [P, OUT1, WD]) for i in range(CH1)]
        xT = [sc.sb(f"xT{i}", [P, 4, P]) for i in range(SLOTS)]
        tp = [sc.ps(f"tp{i}", [P, 4, P]) for i in range(SLOTS)]
        freq_ps = [sc.ps(f"freq{s}", [P, 512]) for s in range(S)]
        const_in = sc.sem("const_in")
        x_in = [sc.sem(f"x_in{c}") for c in range(CH1)]
        pe_read = [sc.sem(f"pe_read{c}") for c in range(CH1)]
        top_zero = sc.sem("top_zero")
        started = sc.sem("started")
        tapped = [sc.sem(f"tapped{c}") for c in range(2)]
        chunk_free = [sc.sem(f"chunk_free{c}") for c in range(CH1)]
        xd_out = [sc.sem(f"xd_out{i}") for i in range(CH1)]
        stored = [sc.sem(f"stored{i}") for i in range(CH1)]
        transposed = sc.sem("transposed")
        copied = [sc.sem(f"copied{i}") for i in range(SLOTS)]
        multiplied = [sc.sem(f"multiplied{i}") for i in range(SLOTS)]
        freq_done, freq_read = sc.sem("freq_done"), sc.sem("freq_read")
        ident = cst[:, :]
        quads = CH1 * QUADS

        with nc.Block() as block:
            @block.sync
            def _(sp):
                sp.dma_start(cst[:, :], consts[:, CONST_AT["ident"]]).then_inc(const_in, 16)
                sp.dma_start(wd[:, :, :], w_down.rearrange("(t g) s a b -> g t (s a b)", t=T)).then_inc(const_in, 16)
                sp.dma_start(p_sb[:, :, :], p_cols.rearrange("w (h k) -> w h k", k=UV)).then_inc(const_in, 16)
                with sp.Fori(0, B * T) as i:
                    for c in range(CH1):
                        sp.wait_ge(pe_read[c], i + FREE)
                        sp.wait_ge(chunk_free[c], i + FREE)
                        above = 1 if c == 0 else 0
                        sp.dma_start(xt[c][:, :, above:, :].rearrange("g s h w -> g s (h w)"),
                                     xv[i, :, :, (c * ROWS1 - 1 + above) * W:(c + 1) * ROWS1 * W]
                                     ).then_inc(x_in[c], 16)

            @block.gpsimd
            def _(pool):
                nc.gpsimd.memset(xt[0][:, :, 0, :], 0.0).then_inc(top_zero, 1)
                start_free(pool, stored)
                with pool.Fori(0, B * T) as i:
                    for c in range(CH1):
                        pool.wait_ge(tapped[c % 2], (i * (CH1 // 2) + c // 2 + 1) * TAPS_LEFT)
                        pool.dma_start(xd.rearrange("b t g n -> (b t) g n")[i, :, c * OUT1 * WD:(c + 1) * OUT1 * WD],
                                       acc[c][:, :, :].rearrange("g h w -> g (h w)")).then_inc(xd_out[c], 16)
                        pool.wait_ge(xd_out[c], i * 16 + 16)
                        pool.sem_inc(stored[c], 1)

            @block.vector
            def _(dve):
                dve.wait_ge(top_zero, 1)
                start_free(dve, chunk_free)
                with dve.Fori(0, B) as b:
                    for t in range(T):
                        for c0 in range(0, CH1, 2):
                            i = b * T + t
                            base = (i * (CH1 // 2) + c0 // 2) * TAPS_LEFT
                            for n, (s, dh, dw) in enumerate(TAPS[1:]):
                                for c in (c0, c0 + 1):
                                    if n == 0:
                                        dve.wait_ge(x_in[c], i * 16 + 16)
                                        dve.wait_ge(started, i * CH1 + c + 1)
                                    else:
                                        dve.wait_ge(tapped[c % 2], base + n)
                                    left = 1 if dw < 0 else 0
                                    k = s * 9 + (dh + 1) * 3 + dw + 1
                                    nc.vector.scalar_tensor_tensor(
                                        out=acc[c][:, :, left:], in0=tap_window(xt[c], (s, dh, dw), OUT1),
                                        scalar=wd[:, t, k:k + 1], in1=acc[c][:, :, left:],
                                        op0=ALU.mult, op1=ALU.add).then_inc(tapped[c % 2], 1)
                            for c in (c0, c0 + 1):
                                dve.wait_ge(tapped[c % 2], base + TAPS_LEFT)
                                dve.sem_inc(chunk_free[c], 1)

            @block.scalar
            def _(act):
                start_free(act, [freq_read, *copied])
                act.wait_ge(const_in, 48)
                act.wait_ge(top_zero, 1)
                s0, dh0, dw0 = TAPS[0]
                first_tap = s0 * 9 + (dh0 + 1) * 3 + dw0 + 1
                with act.Fori(0, B) as b:
                    for t in range(T):
                        i = b * T + t
                        for q in range(quads):
                            slot, c = q % SLOTS, q // QUADS
                            if q % QUADS == 0:
                                act.wait_ge(x_in[c], i * 16 + 16)
                                act.wait_ge(stored[c], i + FREE)
                                nc.scalar.activation(acc[c][:, :, :], tap_window(xt[c], TAPS[0], OUT1), ACT.Copy,
                                                     scale=wd[:, t, first_tap:first_tap + 1]).then_inc(started, 1)
                            act.wait_ge(transposed, i * quads + q + 1)
                            act.wait_ge(multiplied[slot], i * (quads // SLOTS) + q // SLOTS + FREE)
                            nc.scalar.activation(xT[slot][:, :, :], tp[slot][:, :, :],
                                                 ACT.Copy).then_inc(copied[slot], 1)
                        act.wait_ge(freq_done, i + 1)
                        for s in range(S):
                            nc.scalar.activation(xps[:, i, s, :], freq_ps[s][:, 0:UV], ACT.Copy
                                                 ).then_inc(freq_read, 1)

            @block.tensor
            def _(pe):
                pe.wait_ge(const_in, 48)
                pe.wait_ge(top_zero, 1)
                start_free(pe, [*multiplied, *pe_read])
                with pe.Fori(0, B) as b:
                    for t in range(T):
                        i = b * T + t

                        def transpose(q):
                            c, s, r = q // QUADS, q % QUADS // (QUADS // 2), q % (QUADS // 2) * 4
                            slot = q % SLOTS
                            if q % QUADS == 0:
                                pe.wait_ge(x_in[c], i * 16 + 16)
                            pe.wait_ge(copied[slot], i * (quads // SLOTS) + q // SLOTS + FREE)
                            for n in range(4):
                                last = nc.tensor.transpose(tp[slot][:, n, :], xt[c][:, s, 1 + r + n, :], ident)
                            last.then_inc(transposed, 1)

                        def multiply(q):
                            c, s, r = q // QUADS, q % QUADS // (QUADS // 2), q % (QUADS // 2) * 4
                            slot = q % SLOTS
                            if q == 0:
                                pe.wait_ge(freq_read, i * S + FREE)
                            pe.wait_ge(copied[slot], i * (quads // SLOTS) + q // SLOTS + 1 + FREE)
                            for n in range(4):
                                row = c * ROWS1 + r + n
                                last = nc.tensor.matmul(freq_ps[s][:, 0:UV], xT[slot][:, n, :], p_sb[:, row, :],
                                                        start=row == 0, stop=row == H - 1)
                            last.then_inc(multiplied[slot], 1)

                        for q in range(quads + 2):
                            if q < quads:
                                transpose(q)
                                if q % QUADS == QUADS - 1:
                                    pe.wait_ge(transposed, i * quads + q + 1)
                                    pe.sem_inc(pe_read[q // QUADS], 1)
                            if q >= 2:
                                multiply(q - 2)
                        pe.wait_ge(multiplied[(quads - 1) % SLOTS], (i + 1) * (quads // SLOTS) + FREE)
                        pe.sem_inc(freq_done, 1)


def cluster_pass(nc, consts, xd, wb_ohn, oh_t):
    ohn = wb_ohn
    with Scope(nc, "cluster") as sc:
        cst = sc.sb("const", [P, CONST_N])
        xx = sc.sb("xx", [P, T, POS])
        xsT = sc.sb("xsT", [P, NT, T, P])
        gram = sc.sb("gram", [P, T, T * P])
        square = sc.sb("square", [P, POS])
        hi, lo, den, inv = (sc.sb(n, [P, T]) for n in ("hi", "lo", "den", "inv"))
        x2 = sc.sb("x2", [P, T])
        wt = sc.sb("wt", [P, T, K])
        prod, dist, near, score, oh = (sc.sb(n, [P, T, K]) for n in ("prod", "dist", "near", "score", "oh"))
        low, best = sc.sb("low", [P, T]), sc.sb("best", [P, T])
        count, rc, empty = sc.sb("count", [P, K]), sc.sb("rc", [P, K]), sc.sb("empty", [P, K])
        rep = sc.sb("rep", [P, T, B * 2, K])
        tp = [sc.ps(f"tp{i}", [P, 4, P]) for i in range(2)]
        gram_ps = [sc.ps(f"gram{t}", [P, 512]) for t in range(T)]
        dot_ps = sc.ps("dot", [P, 512])
        c2_ps = sc.ps("c2", [P, 512])
        cnt_ps = sc.ps("cnt", [P, 512])
        data_in, normal, squared, transposed, copied = (
            sc.sem(n) for n in ("data_in", "normal", "squared", "transposed", "copied"))
        gram_made, gram_copied = sc.sem("gram_made"), sc.sem("gram_copied")
        dots, prods, c2s, labelled, counted, moved, chain_sem = (
            sc.sem(n) for n in ("dots", "prods", "c2s", "labelled", "counted", "moved", "chain"))
        replicated, rep_t, rep_copied = sc.sem("replicated"), sc.sem("rep_t"), sc.sem("rep_copied")
        ident, ones = cst[:, CONST_AT["ident"]], cst[:, CONST_AT["ones"]]
        groups = NT // 2

        with nc.Block() as block:
            @block.sync
            def _(sp):
                sp.dma_start(cst[:, :], consts).then_inc(data_in, 16)
                sp.dma_start(xx[:, :, :], xd[0].rearrange("t g n -> g t n")).then_inc(data_in, 16)
                sp.wait_ge(data_in, 32)

            @block.vector
            def _(dve):
                ch = Chain(dve, chain_sem)
                dve.wait_ge(data_in, 32)
                ch.link(nc.vector.tensor_reduce(hi[:, :], xx[:, :, :], AX.X, ALU.max))
                ch.link(nc.vector.tensor_reduce(lo[:, :], xx[:, :, :], AX.X, ALU.min))
                ch.link(nc.vector.tensor_tensor(den[:, :], hi[:, :], lo[:, :], ALU.subtract))
                ch.link(nc.vector.tensor_scalar(den[:, :], den[:, :], 1e-12, None, ALU.max))
                ch.link(nc.vector.reciprocal(inv[:, :], den[:, :]))
                for t in range(T):
                    nc.vector.tensor_scalar(xx[:, t, :], xx[:, t, :], lo[:, t:t + 1], inv[:, t:t + 1],
                                            ALU.subtract, ALU.mult).then_inc(normal, 1)
                nc.vector.tensor_copy(wt[:, :, :].rearrange("p t k -> p (t k)"),
                                      cst[:, CONST_AT["pick0"]]).then_inc(moved, 1)
                dve.wait_ge(moved, 1)
                dve.wait_ge(squared, T)
                first = 5
                per = 13
                with dve.Fori(0, ITERS + 1) as i:
                    ch = Chain(dve, chain_sem, i * per + first)
                    dve.wait_ge(dots, i + 1)
                    dv = dot_ps[:, 0:T * K].rearrange("p (t k) -> p t k", t=T)
                    nc.vector.tensor_tensor(prod[:, :, :], wt[:, :, :], dv, ALU.mult).then_inc(prods, 1)
                    for t in range(T):
                        ch.link(nc.vector.tensor_scalar(dist[:, t, :], dv[:, t, :], -2.0, x2[:, t:t + 1],
                                                        ALU.mult, ALU.add))
                    dve.wait_ge(c2s, i + 1)
                    ch.link(nc.vector.tensor_tensor(dist[:, :, :], dist[:, :, :],
                                                    c2_ps[:, 0:K].unsqueeze(1).broadcast_to([P, T, K]), ALU.add))
                    ch.link(nc.vector.tensor_reduce(low[:, :], dist[:, :, :], AX.X, ALU.min))
                    ch.link(nc.vector.tensor_tensor(near[:, :, :], dist[:, :, :],
                                                    low[:, :].unsqueeze(2).broadcast_to([P, T, K]), ALU.is_le))
                    ch.link(nc.vector.tensor_tensor(
                        score[:, :, :], near[:, :, :],
                        cst[:, CONST_AT["tie"]].unsqueeze(1).broadcast_to([P, T, K]), ALU.mult))
                    ch.link(nc.vector.tensor_reduce(best[:, :], score[:, :, :], AX.X, ALU.max))
                    nc.vector.tensor_tensor(oh[:, :, :], score[:, :, :],
                                            best[:, :].unsqueeze(2).broadcast_to([P, T, K]),
                                            ALU.is_equal).then_inc(labelled, 1)
                    dve.wait_ge(labelled, i + 1)
                    dve.wait_ge(counted, i + 1)
                    ch.link(nc.vector.tensor_scalar(count[:, :], cnt_ps[:, 0:K], 1.0, None, ALU.max))
                    ch.link(nc.vector.reciprocal(rc[:, :], count[:, :]))
                    ch.link(nc.vector.tensor_scalar(empty[:, :], cnt_ps[:, 0:K], 0.0, None, ALU.is_equal))
                    ch.link(nc.vector.tensor_tensor(ohn[:, :, :], oh[:, :, :],
                                                    rc[:, :].unsqueeze(1).broadcast_to([P, T, K]), ALU.mult))
                    ch.link(nc.vector.tensor_tensor(wt[:, :, :], wt[:, :, :],
                                                    empty[:, :].unsqueeze(1).broadcast_to([P, T, K]), ALU.mult))
                    ch.link(nc.vector.tensor_tensor(wt[:, :, :], wt[:, :, :], ohn[:, :, :], ALU.add))
                    dve.sem_inc(moved, 1)
                for t in range(T):
                    nc.vector.tensor_copy(rep[:, t, :, :], oh[:, t, :].unsqueeze(1).broadcast_to([P, B * 2, K])
                                          ).then_inc(replicated, 1)

            @block.scalar
            def _(act):
                for t in range(T):
                    act.wait_ge(normal, t + 1)
                    if t:
                        act.wait_ge(squared, t)
                    nc.scalar.activation(square[:, :], xx[:, t, :], ACT.Square,
                                         accum_out=x2[:, t:t + 1]).then_inc(squared, 1)
                for n in range(groups):
                    act.wait_ge(transposed, n + 1)
                    nc.scalar.activation(xsT[:, 2 * n:2 * n + 2, :, :].rearrange("p a t g -> p (a t) g"),
                                         tp[n % 2][:, :, :], ACT.Copy).then_inc(copied, 1)
                for t in range(T):
                    act.wait_ge(gram_made, t + 1)
                    nc.scalar.activation(gram[:, t, :], gram_ps[t][:, 0:T * P], ACT.Copy).then_inc(gram_copied, 1)
                for t in range(T):
                    act.wait_ge(rep_t, t + 1)
                    nc.scalar.activation(oh_t[:, t, :], tp[t][:, 0, :], ACT.Copy).then_inc(rep_copied, 1)
                act.wait_ge(rep_copied, T)

            @block.tensor
            def _(pe):
                pe.wait_ge(data_in, 32)
                pe.wait_ge(normal, T)
                for n in range(groups):
                    if n >= 2:
                        pe.wait_ge(copied, n - 1)
                    for a in range(2):
                        for t in range(T):
                            at = (2 * n + a) * P
                            last = nc.tensor.transpose(tp[n % 2][:, 2 * a + t, :], xx[:, t, at:at + P], ident)
                    last.then_inc(transposed, 1)
                pe.wait_ge(copied, groups)
                for t in range(T):
                    for n in range(NT):
                        last = nc.tensor.matmul(gram_ps[t][:, 0:T * P], xsT[:, n, t, :],
                                                xsT[:, n, :, :].rearrange("p t g -> p (t g)"),
                                                start=n == 0, stop=n == NT - 1)
                    last.then_inc(gram_made, 1)
                pe.wait_ge(gram_copied, T)
                with pe.Fori(0, ITERS + 1) as i:
                    pe.wait_ge(moved, i + 1)
                    for t in range(T):
                        for t2 in range(T):
                            last = nc.tensor.matmul(dot_ps[:, t * K:(t + 1) * K], gram[:, t2, t * P:(t + 1) * P],
                                                    wt[:, t2, :], start=t2 == 0, stop=t2 == T - 1)
                    last.then_inc(dots, 1)
                    pe.wait_ge(prods, i + 1)
                    for t in range(T):
                        last = nc.tensor.matmul(c2_ps[:, 0:K], ones, prod[:, t, :], start=t == 0, stop=t == T - 1)
                    last.then_inc(c2s, 1)
                    pe.wait_ge(labelled, i + 1)
                    for t in range(T):
                        last = nc.tensor.matmul(cnt_ps[:, 0:K], ones, oh[:, t, :], start=t == 0, stop=t == T - 1)
                    last.then_inc(counted, 1)
                for t in range(T):
                    pe.wait_ge(replicated, t + 1)
                    nc.tensor.transpose(tp[t][:, 0, :], rep[:, t, :, :].rearrange("p a k -> p (a k)"),
                                        ident).then_inc(rep_t, 1)


def average_pass(nc, consts, q_cols, xd, ohn, feat, xpu):
    with Scope(nc, "average") as sc:
        cst = sc.sb("const", [P, P])
        q_sb = sc.sb("q", [P, NT, UV])
        dbuf = [[sc.sb(f"xd{a}_{t}", [P, POS]) for t in range(T)] for a in range(2)]
        dT = [sc.sb(f"dT{i}", [P, 4, P]) for i in range(SLOTS)]
        tp = [sc.ps(f"tp{i}", [P, 4, P]) for i in range(SLOTS)]
        mean_ps = [sc.ps(f"mean{a}", [P, NT, K]) for a in range(2)]
        freq_ps = [sc.ps(f"freq{a}", [P, T, UV]) for a in range(2)]
        const_in = sc.sem("const_in")
        d_in = [[sc.sem(f"d_in{a}_{t}") for t in range(T)] for a in range(2)]
        batch_done = [sc.sem(f"batch_done{a}") for a in range(2)]
        transposed, averaged, freq_done = (sc.sem(n) for n in ("transposed", "averaged", "freq_done"))
        mean_read, freq_read = ([sc.sem(f"{n}{a}") for a in range(2)] for n in ("mean_read", "freq_read"))
        copied = [sc.sem(f"copied{i}") for i in range(SLOTS)]
        multiplied = [sc.sem(f"multiplied{i}") for i in range(SLOTS)]
        ident = cst[:, :]
        per = NT // 4
        quads = T * per
        turns = quads // SLOTS

        with nc.Block() as block:
            @block.sync
            def _(sp):
                sp.dma_start(cst[:, :], consts[:, CONST_AT["ident"]]).then_inc(const_in, 16)
                sp.dma_start(q_sb[:, :, :], q_cols.rearrange("p (n k) -> p n k", k=UV)).then_inc(const_in, 16)
                with sp.Fori(0, B // 2) as h:
                    for a in range(2):
                        sp.wait_ge(batch_done[a], h + FREE)
                        for t in range(T):
                            sp.dma_start(dbuf[a][t][:, :], xd[h * 2 + a, t, :, :]).then_inc(d_in[a][t], 16)

            @block.tensor
            def _(pe):
                pe.wait_ge(const_in, 32)
                start_free(pe, [*batch_done, *multiplied])
                with pe.Fori(0, B // 2) as h:
                    for a in range(2):
                        b = h * 2 + a
                        d = dbuf[a]

                        def transpose(q):
                            t, n0, slot = q // per, q % per * 4, q % SLOTS
                            if q % per == 0:
                                pe.wait_ge(d_in[a][t], h * 16 + 16)
                            pe.wait_ge(copied[slot], b * turns + q // SLOTS + FREE)
                            for n in range(4):
                                last = nc.tensor.transpose(tp[slot][:, n, :], d[t][:, (n0 + n) * P:(n0 + n + 1) * P],
                                                           ident)
                            last.then_inc(transposed, 1)

                        def multiply(q):
                            t, n0, slot = q // per, q % per * 4, q % SLOTS
                            if q == 0:
                                pe.wait_ge(freq_read[a], h + FREE)
                            pe.wait_ge(copied[slot], b * turns + q // SLOTS + 1 + FREE)
                            for n in range(4):
                                last = nc.tensor.matmul(freq_ps[a][:, t, :], dT[slot][:, n, :], q_sb[:, n0 + n, :],
                                                        start=n0 + n == 0, stop=n0 + n == NT - 1)
                            last.then_inc(multiplied[slot], 1)
                            if q == quads - 1:
                                pe.wait_ge(multiplied[slot], b * turns + turns + FREE)
                                pe.sem_inc(freq_done, 1)

                        for q in range(quads + 2):
                            if q < quads:
                                transpose(q)
                            if q >= 2:
                                multiply(q - 2)
                        pe.wait_ge(mean_read[a], h + FREE)
                        for n in range(NT):
                            for t in range(T):
                                last = nc.tensor.matmul(mean_ps[a][:, n, :], d[t][:, n * P:(n + 1) * P],
                                                        ohn[:, t, :], start=t == 0, stop=t == T - 1)
                        last.then_inc(averaged, 1)
                        pe.wait_ge(averaged, b + 1)
                        pe.sem_inc(batch_done[a], 1)

            @block.scalar
            def _(act):
                start_free(act, [*freq_read, *copied])
                with act.Fori(0, B // 2) as h:
                    for a in range(2):
                        b = h * 2 + a
                        for q in range(quads):
                            slot = q % SLOTS
                            act.wait_ge(transposed, b * quads + q + 1)
                            act.wait_ge(multiplied[slot], b * turns + q // SLOTS + FREE)
                            nc.scalar.activation(dT[slot][:, :, :], tp[slot][:, :, :], ACT.Copy
                                                 ).then_inc(copied[slot], 1)
                        act.wait_ge(freq_done, b + 1)
                        nc.scalar.activation(xpu[:, :, :].rearrange("p (b t) k -> p b t k", t=T)[:, b, :, :],
                                             freq_ps[a][:, :, :], ACT.Copy).then_inc(freq_read[a], 1)

            @block.vector
            def _(dve):
                start_free(dve, mean_read)
                with dve.Fori(0, B // 2) as h:
                    for a in range(2):
                        b = h * 2 + a
                        dve.wait_ge(averaged, b + 1)
                        nc.vector.tensor_copy(feat[:, :, :].rearrange("p n (b f k) -> p n b f k", b=B, f=2)[:, :, b, 0, :],
                                              mean_ps[a][:, :, :]).then_inc(mean_read[a], 1)


def mixture_pass(nc, consts, w_conv, w_up, feat, oh_t, xps, xpu, coef):
    with Scope(nc, "mix") as sc:
        cst = sc.sb("const", [P, CONST_N])
        wc = sc.sb("wc", [K, N])
        wu = sc.sb("wu", [P, T, S])
        ft = sc.sb("ft", [P, NT, P])
        mean_b = sc.sb("mean_b", [P, B, K])
        red0, red, red2 = (sc.sb(n, [P, B, 2, K]) for n in ("red0", "red", "red2"))
        mean_c, var_c = sc.sb("mean_c", [P, 1]), sc.sb("var_c", [P, 1])
        order, less, rank = sc.sb("order", [P, K, K]), sc.sb("less", [P, K, K]), sc.sb("rank", [P, K])
        var0 = sc.sb("var0", [P, K])
        ranked = sc.sb("ranked", [K, B * 2, K])
        wp = sc.sb("wp", [P, N])
        ms, mu, mu2, var, iv, quad, lnv, w1, w2, wmat, term, lnw, wb, cs, rs, rn = (
            sc.sb(n, [P, BN]) for n in ("ms", "mu", "mu2", "var", "iv", "quad", "lnv", "w1", "w2", "wmat", "term",
                                        "lnw", "wb", "cs", "rs", "rn"))
        logit, resp = sc.sb("logit", [P, NT, BN]), sc.sb("resp", [P, NT, BN])
        top, tot, inv = (sc.sb(n, [P, NT, B]) for n in ("top", "tot", "inv"))
        mud, vard, muc = sc.sb("mud", [P, N]), sc.sb("vard", [P, N]), sc.sb("muc", [P, N])
        c0, c1, box0, box1, ya, yb, ye, y = (sc.sb(n, [P, 1]) for n in ("c0", "c1", "box0", "box1", "ya", "yb",
                                                                      "ye", "y"))
        low = sc.sb("low", [P, B * T, UV])
        ymat, one_gate = sc.sb("ymat", [P, B]), sc.sb("one_gate", [P, T, B])
        tp = [sc.ps(f"tp{i}", [P, 4, P]) for i in range(2)]
        a_ps, b_ps, l_ps, m_ps, n_ps, c_ps = (sc.ps(n, [P, 512]) for n in ("a", "b", "l", "m", "n", "c"))
        const_in, chain_sem = sc.sem("const_in"), sc.sem("chain")
        sums, mean_made, centred, squared, spread_sum, spread_made, order_made, picked = (
            sc.sem(n) for n in ("sums", "mean_made", "centred", "squared", "spread_sum", "spread_made",
                                "order_made", "picked"))
        transposed, copied, means, params, weights, logs, logged, terms, scores, shifted, exped, resps, moments, \
            masses, ready = (sc.sem(n) for n in ("transposed", "copied", "means", "params", "weights", "logs",
                                                 "logged", "terms", "scores", "shifted", "exped", "resps",
                                                 "moments", "masses", "ready"))
        gated, sig, sig_in = sc.sem("gated"), sc.sem("sig"), sc.sem("sig_in")
        y_made, act_chain = sc.sem("y_made"), sc.sem("act_chain")

        def k(name):
            return cst[:, CONST_AT[name]]

        fv = feat[:, :, :].rearrange("p n (b f k) -> p n b f k", b=B, f=2)
        groups = NT // 4

        with nc.Block() as block:
            @block.sync
            def _(sp):
                sp.dma_start(cst[:, :], consts).then_inc(const_in, 16)
                sp.dma_start(wc[:, :], w_conv).then_inc(const_in, 16)
                sp.dma_start(wu[:, :, :], w_up.rearrange("(t g s) -> g t s", t=T, s=S)).then_inc(const_in, 16)

            def parameters(pe, i):
                pe.wait_ge(ready, i + 1)
                nc.tensor.matmul(a_ps[:, 0:BN], k("sel_mu"), ms[:, :], start=True, stop=True)
                nc.tensor.matmul(b_ps[:, 0:BN], k("sel_ex"), ms[:, :], start=True, stop=True).then_inc(means, 1)

            def dve_parameters(dve, ch, i):
                dve.wait_ge(means, i + 1)
                ch.link(nc.vector.tensor_copy(mu[:, :], a_ps[:, 0:BN]))
                ch.link(nc.vector.tensor_tensor(mu2[:, :], mu[:, :], mu[:, :], ALU.mult))
                ch.link(nc.vector.tensor_tensor(var[:, :], b_ps[:, 0:BN], mu2[:, :], ALU.subtract))
                ch.link(nc.vector.tensor_scalar(var[:, :], var[:, :], EPS, EPS, ALU.add, ALU.max))

            @block.tensor
            def _(pe):
                pe.wait_ge(const_in, 48)
                pe.wait_ge(sums, 1)
                nc.tensor.matmul(a_ps[:, 0:P], k("ones"), red0[:, :, :, :].rearrange("p b f k -> p (b f k)"),
                                 start=True, stop=True)
                nc.tensor.matmul(b_ps[:, 0:1], red0[:, :, :, :].rearrange("p b f k -> p (b f k)"), k("mean"),
                                 start=True, stop=True).then_inc(mean_made, 1)
                pe.wait_ge(spread_sum, 1)
                nc.tensor.matmul(m_ps[:, 0:P], k("ones"), red2[:, :, :, :].rearrange("p b f k -> p (b f k)"),
                                 start=True, stop=True)
                nc.tensor.matmul(n_ps[:, 0:1], red2[:, :, :, :].rearrange("p b f k -> p (b f k)"), k("mean"),
                                 start=True, stop=True).then_inc(spread_made, 1)
                for n in range(groups):
                    if n >= 2:
                        pe.wait_ge(copied, n - 1)
                    for j in range(4):
                        last = nc.tensor.transpose(tp[n % 2][:, j, :], feat[:, 4 * n + j, :], k("ident"))
                    last.then_inc(transposed, 1)
                pe.wait_ge(order_made, 1)
                nc.tensor.matmul(c_ps[:, 0:N], ranked[:, :, :].rearrange("r a k -> r (a k)"), wc[:, :],
                                 start=True, stop=True).then_inc(picked, 1)
                with pe.Fori(0, ITERS) as i:
                    parameters(pe, i)
                    pe.wait_ge(terms, i + 1)
                    nc.tensor.matmul(c_ps[:, 0:BN], k("ones"), term[:, :], start=True, stop=True).then_inc(logs, 1)
                    pe.wait_ge(weights, i + 1)
                    for n in range(NT):
                        last = nc.tensor.matmul(l_ps[:, n * BN:(n + 1) * BN], ft[:, n, :], wmat[:, :],
                                                start=True, stop=True)
                    last.then_inc(scores, 1)
                    pe.wait_ge(resps, i + 1)
                    nc.tensor.matmul(n_ps[:, 0:BN], k("ones"), rs[:, :], start=True, stop=True).then_inc(masses, 1)
                    for n in range(NT):
                        last = nc.tensor.matmul(m_ps[:, 0:BN], feat[:, n, :], resp[:, n, :],
                                                start=n == 0, stop=n == NT - 1)
                    last.then_inc(moments, 1)
                parameters(pe, ITERS)
                pe.wait_ge(y_made, 1)
                for t in range(T):
                    last = nc.tensor.matmul(l_ps[:, t * B:(t + 1) * B], oh_t[:, t, :], ymat[:, :],
                                            start=True, stop=True)
                last.then_inc(gated, 1)

            @block.scalar
            def _(act):
                act.wait_ge(centred, 1)
                nc.scalar.activation(fv[:, :, :, 1, :], fv[:, :, :, 0, :], ACT.Square).then_inc(squared, 1)
                for n in range(groups):
                    act.wait_ge(transposed, n + 1)
                    nc.scalar.activation(ft[:, 4 * n:4 * n + 4, :], tp[n % 2][:, :, :], ACT.Copy).then_inc(copied, 1)
                with act.Fori(0, ITERS) as i:
                    act.wait_ge(params, i + 1)
                    nc.scalar.activation(lnv[:, :], var[:, :], ACT.Ln).then_inc(act_chain, 1)
                    nc.scalar.activation(lnw[:, :], wb[:, :], ACT.Ln).then_inc(logged, 1)
                    act.wait_ge(shifted, i + 1)
                    nc.scalar.activation(logit[:, :, :], logit[:, :, :], ACT.Exp).then_inc(exped, 1)
                act.wait_ge(sig_in, 1)
                nc.scalar.activation(ye[:, :], yb[:, :], ACT.Exp, scale=-1.0).then_inc(sig, 1)

            @block.vector
            def _(dve):
                ch = Chain(dve, chain_sem)
                dve.wait_ge(const_in, 48)
                for f in range(2):
                    ch.link(nc.vector.tensor_reduce(red0[:, :, f, :],
                                                    fv[:, :, :, 0, :].rearrange("p n b k -> p b k n"), AX.X, ALU.add))
                dve.sem_inc(sums, 1)
                dve.wait_ge(mean_made, 1)
                av = a_ps[:, 0:P].rearrange("p (b f k) -> p b f k", b=B, f=2)
                ch.link(nc.vector.tensor_scalar(mean_b[:, :, :], av[:, :, 0, :], 1.0 / POS, None, ALU.mult))
                ch.link(nc.vector.tensor_copy(mean_c[:, :], b_ps[:, 0:1]))
                for b in range(B):
                    ch.link(nc.vector.tensor_tensor(fv[:, :, b, 0, :], fv[:, :, b, 0, :],
                                                    mean_b[:, b, :].unsqueeze(1).broadcast_to([P, NT, K]),
                                                    ALU.subtract))
                dve.sem_inc(centred, 1)
                dve.wait_ge(squared, 1)
                ch.link(nc.vector.tensor_reduce(red2[:, :, :, :].rearrange("p b f k -> p (b f k)"),
                                                feat[:, :, :].rearrange("p n c -> p c n"), AX.X, ALU.add))
                dve.sem_inc(spread_sum, 1)
                dve.wait_ge(spread_made, 1)
                ch.link(nc.vector.tensor_tensor(var_c[:, :], n_ps[:, 0:1], k("is_x2"), ALU.mult))
                mv = m_ps[:, 0:P].rearrange("p (b f k) -> p b f k", b=B, f=2)
                ch.link(nc.vector.tensor_copy(var0[:, :], mv[:, 0, 1, :]))
                mine = var0[:, :].unsqueeze(2).broadcast_to([P, K, K])
                other = var0[:, :].unsqueeze(1).broadcast_to([P, K, K])
                ch.link(nc.vector.tensor_tensor(less[:, :, :], other, mine, ALU.is_lt))
                ch.link(nc.vector.tensor_tensor(order[:, :, :], other, mine, ALU.is_equal))
                ch.link(nc.vector.tensor_tensor(order[:, :, :], order[:, :, :],
                                                k("before").rearrange("p (a c) -> p a c", a=K), ALU.mult))
                ch.link(nc.vector.tensor_tensor(less[:, :, :], less[:, :, :], order[:, :, :], ALU.add))
                ch.link(nc.vector.tensor_reduce(rank[:, :], less[:, :, :], AX.X, ALU.add))
                ch.link(nc.vector.tensor_scalar(ranked[:, :, :],
                                                rank[0:K, :].unsqueeze(1).broadcast_to([K, B * 2, K]),
                                                cst[0:K, CONST_AT["rank"]], None, ALU.is_equal))
                dve.sem_inc(order_made, 1)
                dve.wait_ge(picked, 1)
                ch.link(nc.vector.tensor_copy(wp[:, :], c_ps[:, 0:N]))
                dve.wait_ge(copied, groups)
                msv = ms[:, :].rearrange("p (b n) -> p b n", n=N)
                for n, (tile, pos) in enumerate(((0, 0), (NT - 1, P - 1))):
                    ch.link(nc.vector.tensor_tensor(msv[:, :, n], ft[:, tile, pos:pos + 1].broadcast_to([P, B]),
                                                    var_c[:, 0:1].broadcast_to([P, B]), ALU.add))
                ch.link(nc.vector.memset(wb[:, :], 1.0 / N))
                dve.sem_inc(ready, 1)
                first = ch.n
                lv = logit[:, :, :].rearrange("p n (b c) -> p n b c", c=N)
                per = 23
                with dve.Fori(0, ITERS) as i:
                    ch = Chain(dve, chain_sem, i * per + first)
                    dve_parameters(dve, ch, i)
                    dve.sem_inc(params, 1)
                    ch.link(nc.vector.reciprocal(iv[:, :], var[:, :]))
                    ch.link(nc.vector.tensor_tensor(w1[:, :], mu[:, :], iv[:, :], ALU.mult))
                    ch.link(nc.vector.tensor_tensor(w2[:, :], iv[:, :], k("mask_x2"), ALU.mult))
                    ch.link(nc.vector.tensor_tensor(wmat[:, :], w1[:, :], k("mask_x"), ALU.mult))
                    ch.link(nc.vector.tensor_tensor(wmat[:, :], wmat[:, :], w2[:, :], ALU.add))
                    dve.sem_inc(weights, 1)
                    ch.link(nc.vector.tensor_tensor(quad[:, :], mu2[:, :], iv[:, :], ALU.mult))
                    dve.wait_ge(act_chain, i + 1)
                    ch.link(nc.vector.tensor_tensor(quad[:, :], quad[:, :], lnv[:, :], ALU.add))
                    ch.link(nc.vector.tensor_tensor(term[:, :], quad[:, :], k("mask_term"), ALU.mult))
                    dve.sem_inc(terms, 1)
                    dve.wait_ge(logs, i + 1)
                    dve.wait_ge(logged, i + 1)
                    ch.link(nc.vector.scalar_tensor_tensor(out=cs[:, :], in0=lnw[:, :], scalar=-0.5 * K * LOG2PI,
                                                           in1=c_ps[:, 0:BN], op0=ALU.add, op1=ALU.add))
                    dve.wait_ge(scores, i + 1)
                    ch.link(nc.vector.tensor_tensor(logit[:, :, :],
                                                    l_ps[:, :].rearrange("p (n c) -> p n c", c=BN),
                                                    cs[:, :].unsqueeze(1).broadcast_to([P, NT, BN]), ALU.add))
                    ch.link(nc.vector.tensor_tensor(top[:, :, :], lv[:, :, :, 0], lv[:, :, :, 1], ALU.max))
                    ch.link(nc.vector.tensor_tensor(lv, lv, top[:, :, :].unsqueeze(3).broadcast_to([P, NT, B, N]),
                                                    ALU.subtract))
                    dve.sem_inc(shifted, 1)
                    dve.wait_ge(exped, i + 1)
                    ch.link(nc.vector.tensor_tensor(tot[:, :, :], lv[:, :, :, 0], lv[:, :, :, 1], ALU.add))
                    ch.link(nc.vector.reciprocal(inv[:, :, :], tot[:, :, :]))
                    ch.link(nc.vector.tensor_tensor(
                        resp[:, :, :].rearrange("p n (b c) -> p n b c", c=N), lv,
                        inv[:, :, :].unsqueeze(3).broadcast_to([P, NT, B, N]), ALU.mult))
                    ch.link(nc.vector.tensor_reduce(rs[:, :], resp[:, :, :].rearrange("p n c -> p c n"),
                                                    AX.X, ALU.add))
                    dve.sem_inc(resps, 1)
                    dve.wait_ge(masses, i + 1)
                    ch.link(nc.vector.reciprocal(rn[:, :], n_ps[:, 0:BN]))
                    ch.link(nc.vector.tensor_scalar(wb[:, :], n_ps[:, 0:BN], 1.0 / POS, None, ALU.mult))
                    dve.wait_ge(moments, i + 1)
                    ch.link(nc.vector.tensor_tensor(ms[:, :], m_ps[:, 0:BN], rn[:, :], ALU.mult))
                    assert isinstance(per, int)
                    dve.sem_inc(ready, 1)
                ch = Chain(dve, chain_sem, ITERS * per + first)
                dve_parameters(dve, ch, ITERS)
                for src, dst in ((mu, mud), (var, vard)):
                    ch.link(nc.vector.tensor_tensor(w1[:, :], src[:, :], k("block"), ALU.mult))
                    ch.link(nc.vector.tensor_reduce(dst[:, :], w1[:, :].rearrange("p (b n) -> p n b", n=N),
                                                    AX.X, ALU.add))
                ch.link(nc.vector.tensor_scalar(muc[:, :], mud[:, :], mean_c[:, 0:1], None, ALU.add))
                ch.link(nc.vector.tensor_tensor(c0[:, :], vard[:, 0:1], vard[:, 1:2], ALU.is_le))
                ch.link(nc.vector.tensor_scalar(c1[:, :], c0[:, :], -1.0, 1.0, ALU.mult, ALU.add))
                for box, a, b in ((box0, c0, c1), (box1, c1, c0)):
                    ch.link(nc.vector.tensor_tensor(ya[:, :], muc[:, 0:1], a[:, :], ALU.mult))
                    ch.link(nc.vector.tensor_tensor(yb[:, :], muc[:, 1:2], b[:, :], ALU.mult))
                    ch.link(nc.vector.tensor_tensor(box[:, :], ya[:, :], yb[:, :], ALU.add))
                ch.link(nc.vector.tensor_tensor(ya[:, :], box0[:, :], wp[:, 0:1], ALU.mult))
                ch.link(nc.vector.tensor_tensor(yb[:, :], box1[:, :], wp[:, 1:2], ALU.mult))
                ch.link(nc.vector.tensor_tensor(yb[:, :], ya[:, :], yb[:, :], ALU.add))
                dve.sem_inc(sig_in, 1)
                dve.wait_ge(sig, 1)
                ch.link(nc.vector.tensor_scalar(ye[:, :], ye[:, :], 1.0, None, ALU.add))
                ch.link(nc.vector.reciprocal(y[:, :], ye[:, :]))
                ch.link(nc.vector.tensor_scalar(ymat[:, :], k("block_k"), y[:, 0:1], None, ALU.mult))
                dve.sem_inc(y_made, 1)
                dve.wait_ge(gated, 1)
                ch.link(nc.vector.tensor_scalar(one_gate[:, :, :].rearrange("p t b -> p (t b)"), l_ps[:, 0:T * B],
                                                1.0, None, ALU.add))
                for t in range(T):
                    ch.link(nc.vector.tensor_tensor(
                        coef[:, :, t, :], one_gate[:, t, :].unsqueeze(2).broadcast_to([P, B, S]),
                        wu[:, t, :].unsqueeze(1).broadcast_to([P, B, S]), ALU.mult))
                cv = coef[:, :, :, :].rearrange("p b t s -> p (b t) s")
                for s in range(S):
                    ch.link(nc.vector.tensor_tensor(low[:, :, :], xpu[:, :, :],
                                                    cv[:, :, s].unsqueeze(2).broadcast_to([P, B * T, UV]), ALU.mult))
                    ch.link(nc.vector.tensor_tensor(xps[:, :, s, :], xps[:, :, s, :], low[:, :, :], ALU.add))


ROWS2 = 8
CH2 = H // ROWS2
DROWS = ROWS2 // 2
RING = 9
ZR = UV + 2
XBUF = 4
PIECES = 16


def pair_of(h):
    return 0 if h == 0 else min((h - 1) // 2, HD - 2)


def runs(h0, rows):
    found = []
    for h in range(h0, h0 + rows):
        if found and found[-1][0] == pair_of(h):
            found[-1][2] += 1
        else:
            found.append([pair_of(h), h, 1])
    return found
def second_pass(nc, x, p_cols, r_cols, up_cols, consts, wqk, wv, bias, gamma, xd, xps, coef, out):
    xv = x.rearrange("b (t g s) h w -> b t g s (h w)", t=T, s=S)
    ov = out.rearrange("b (t g s) h w -> b t g s (h w)", t=T, s=S)
    with Scope(nc, "second") as sc:
        cst = sc.sb("const", [P, SECOND_N])
        p_sb = sc.sb("p", [P, H, UV])
        r_sb = sc.sb("r", [UV, H * LOW])
        up = sc.sb("up", [P, H, W])
        wqk_sb, wv_sb = sc.sb("wqk", [P, TS, P]), sc.sb("wv", [P, TS, C])
        gam = sc.sb("gam", [P, 1])
        xt = [sc.sb(f"x{i}", [P, S, ROWS2, W]) for i in range(XBUF)]
        dd = [sc.sb(f"dd{i}", [P, T, DROWS + 1, WD]) for i in range(2)]
        ring = [sc.sb(f"ring{i}", [P, T, S, P]) for i in range(RING)]
        zt = [sc.sb(f"zt{i}", [P, ROWS2, ZR]) for i in range(2)]
        z = [sc.sb(f"z{i}", [ZR, ROWS2, W]) for i in range(2)]
        xp = sc.sb("xp", [P, TS, UV])
        qk = sc.sb("qk", [UV, 2, UV])
        vx = sc.sb("vx", [UV + 1, C])
        grams = sc.sb("grams", [UV, 4, UV])
        work = sc.sb("work", [P, H // 2, LOW])
        m1 = work[0:UV, :, :]
        lam2, lam = sc.sb("lam2", [P, 2, H]), sc.sb("lam", [P, 2, H])
        rk, den = sc.sb("rk", [P, H]), sc.sb("den", [P, H])
        pk = [sc.sb(f"pk{i}", [P, H // PIECES, UV]) for i in range(2)]
        a_sb, mx, ms = sc.sb("a", [UV, UV]), sc.sb("mx", [UV + 1, ZR]), sc.sb("ms", [UV, H])
        vt = sc.sb("vt", [ZR, C])
        rr = sc.sb("rr", [P, 2, H])
        crow = sc.sb("crow", [P, T, S, P])
        dg = crow[:, :, :, :].rearrange("p t s g -> p (t s) g")
        ob = [sc.ps(f"o{i}", [P, 4, W]) for i in range(4)]
        tp = [sc.ps(f"tp{i}", [P, 4, P]) for i in range(2)]
        st = sc.ps("st", [P, 1024])

        const_in = sc.sem("const_in")
        x_in = [sc.sem(f"x_in{i}") for i in range(XBUF)]
        y_out = [sc.sem(f"y_out{i}") for i in range(XBUF)]
        stored = [sc.sem(f"stored{i}") for i in range(XBUF)]
        dd_in = [sc.sem(f"dd_in{i}") for i in range(2)]
        ones_set = sc.sem("ones_set")
        pairs_t, rows_t = sc.sem("pairs_t"), sc.sem("rows_t")
        pairs_copied = [sc.sem(f"pairs_copied{i}") for i in range(2)]
        rows_copied = [sc.sem(f"rows_copied{i}") for i in range(2)]
        zt_made, filled, added_all = sc.sem("zt_made"), sc.sem("filled"), sc.sem("added_all")
        added = [sc.sem(f"added{i}") for i in range(4)]
        chain_sem = sc.sem("chain")
        (xp_made, qk_made, qk_copied, g_made, g_copied, half_made, half_taken, lam_made, lam2_made, root_made,
         pk_made, pk_used, a_made, a_copied, m_made, mx_made, v_made, vt_made, r_made, dg_made, crow_made,
         crow_copied) = (sc.sem(n) for n in (
             "xp_made", "qk_made", "qk_copied", "g_made", "g_copied", "half_made", "half_taken", "lam_made",
             "lam2_made", "root_made", "pk_made", "pk_used", "a_made", "a_copied", "m_made", "mx_made", "v_made",
             "vt_made", "r_made", "dg_made", "crow_made", "crow_copied"))

        def k(name, rows=P):
            return cst[0:rows, CONST_AT[name]]

        half = H * LOW // 2
        rows_pk = H // PIECES

        with nc.Block() as block:
            @block.sync
            def _(sp):
                for dst, src in ((cst[:, :], consts[:, 0:SECOND_N]), (p_sb[:, :, :], p_cols.rearrange("w (h k) -> w h k", k=UV)),
                                 (r_sb[:, :], r_cols), (up[:, :, :], up_cols.rearrange("p (h w) -> p h w", w=W)),
                                 (wqk_sb[:, :, :], wqk), (wv_sb[:, :, :], wv), (vx[UV:UV + 1, :], bias),
                                 (gam[:, :], gamma.rearrange("(a b) -> a b", b=1).broadcast_to([P, 1]))):
                    sp.dma_start(dst, src).then_inc(const_in, 16)
                with sp.Fori(0, B) as b:
                    for m in range(CH2):
                        slot = m % 2
                        sp.wait_ge(pairs_copied[1], b * CH2 + max(m - 1, 0) + FREE)
                        n = min(DROWS + 1, HD - m * DROWS)
                        sp.dma_start(dd[slot][:, :, 0:n, :].rearrange("g t h w -> g t (h w)"),
                                     xd[b].rearrange("t g n -> g t n")[:, :, m * DROWS * WD:(m * DROWS + n) * WD]
                                     ).then_inc(dd_in[slot], 16)
                        for t in range(T):
                            i = (m * T + t) % XBUF
                            sp.wait_ge(stored[i], b * (CH2 * T // XBUF) + (m * T + t) // XBUF + FREE)
                            sp.dma_start(xt[i][:, :, :, :].rearrange("g s h w -> g s (h w)"),
                                         xv[b, t, :, :, m * ROWS2 * W:(m + 1) * ROWS2 * W]).then_inc(x_in[i], 16)

            @block.gpsimd
            def _(pool):
                start_free(pool, stored)
                with pool.Fori(0, B) as b:
                    for m in range(CH2):
                        for t in range(T):
                            i = (m * T + t) % XBUF
                            pool.wait_ge(added_all, (b * CH2 + m) * T + t + 1)
                            pool.dma_start(ov[b, t, :, :, m * ROWS2 * W:(m + 1) * ROWS2 * W],
                                           xt[i][:, :, :, :].rearrange("g s h w -> g s (h w)")).then_inc(y_out[i], 16)
                            pool.wait_ge(y_out[i], (b * (CH2 * T // XBUF) + (m * T + t) // XBUF) * 16 + 16)
                            pool.sem_inc(stored[i], 1)

            @block.tensor
            def _(pe):
                pe.wait_ge(const_in, 128)
                pe.wait_ge(ones_set, 6)
                start_free(pe, [filled])

                def attention(b):
                    pe.wait_ge(xp_made, b + 1)
                    for j in range(2):
                        for n in range(TS):
                            nc.tensor.matmul(st[0:UV, j * UV:(j + 1) * UV], wqk_sb[:, n, j * UV:(j + 1) * UV],
                                             xp[:, n, :], start=n == 0, stop=n == TS - 1)
                    for n in range(TS):
                        last = nc.tensor.matmul(st[0:UV, 512:1024], xp[:, n, :], wv_sb[:, n, :],
                                                start=n == 0, stop=n == TS - 1)
                    last.then_inc(qk_made, 1)
                    pe.wait_ge(qk_copied, b + 1)
                    nc.tensor.matmul(st[:, UV:2 * UV], qk[:, :, :].rearrange("p a k -> p (a k)"), qk[:, 0, :],
                                     start=True, stop=True)
                    nc.tensor.matmul(st[0:UV, 2 * UV:3 * UV], qk[:, 1, :], qk[:, 1, :], start=True, stop=True)
                    nc.tensor.matmul(st[0:UV, 0:UV], qk[:, 1, :], qk[:, 0, :], start=True, stop=True
                                     ).then_inc(g_made, 1)
                    pe.wait_ge(g_copied, b + 1)
                    for j in range(2):
                        for a in range(2):
                            if j or a:
                                pe.wait_ge(lam2_made, b * 4 + j * 2 + a)
                            nc.tensor.matmul(st[:, 0:half], grams[:, j + 1:j + 3, :].rearrange("p a k -> p (a k)"),
                                             r_sb[:, a * half:(a + 1) * half],
                                             start=True, stop=True).then_inc(half_made, 1)
                            pe.wait_ge(half_taken, b * 4 + j * 2 + a + 1)
                            nc.tensor.matmul(st[:, half:2 * half], k("dw_e", UV), m1.rearrange("p h v -> p (h v)"),
                                             start=True, stop=True).then_inc(lam_made, 1)
                    pe.wait_ge(lam2_made, b * 4 + 4)
                    for e in range(PIECES):
                        pe.wait_ge(pk_made, b * PIECES + e + 1)
                        for n in range(rows_pk):
                            row = e * rows_pk + n
                            last = nc.tensor.matmul(st[0:UV, 0:UV], p_sb[:, row, :], pk[e % 2][:, n, :],
                                                    start=row == 0, stop=row == H - 1)
                        last.then_inc(pk_used, 1)
                    pe.wait_ge(a_copied, b + 1)
                    nc.tensor.matmul(st[:, 512 + UV:512 + UV + 1], grams[:, 0:2, :].rearrange("p a k -> p (a k)"),
                                     a_sb[:, 0:1], start=True, stop=True)
                    nc.tensor.matmul(st[0:UV, 512:512 + UV], a_sb[:, :], grams[:, 0, :], start=True, stop=True
                                     ).then_inc(m_made, 1)
                    pe.wait_ge(mx_made, b + 1)
                    nc.tensor.matmul(st[0:ZR, 0:C], mx[:, :], vx[:, :], start=True, stop=True)
                    nc.tensor.matmul(st[:, 512:512 + H], k("dw_e", UV), ms[:, :], start=True, stop=True
                                     ).then_inc(v_made, 1)
                    pe.wait_ge(vt_made, b + 1)
                    pe.wait_ge(dg_made, b + 1)
                    nc.tensor.matmul(st[:, 0:TS * P], k("ones"), crow[:, :, :, :].rearrange("p t s g -> p (t s g)"),
                                     start=True, stop=True).then_inc(crow_made, 1)

                def produce(b, m):
                    j = b * CH2 + m
                    pe.wait_ge(dd_in[m % 2], (b * (CH2 // 2) + m // 2) * 16 + 16)
                    for a in range(2):
                        pe.wait_ge(rows_copied[a], j + FREE)
                        for n in range(2):
                            kk = m * DROWS + 2 * a + n
                            if kk > HD - 2:
                                continue
                            r = 2 * a + n
                            for t in range(T):
                                last = nc.tensor.transpose(
                                    tp[a][:, n * T + t, :],
                                    dd[m % 2][:, t, r:r + 2, :].rearrange("g h w -> g (h w)"), k("ident"))
                        last.then_inc(pairs_t, 1)
                    pe.wait_ge(zt_made, j + 1)
                    for a in range(2):
                        pe.wait_ge(pairs_copied[a], j + 1 + FREE)
                        for n in range(4):
                            last = nc.tensor.transpose(tp[a][0:ZR, n, :], zt[m % 2][:, 4 * a + n, :], k("ident"))
                        last.then_inc(rows_t, 1)

                def combine(b, m):
                    j = b * CH2 + m
                    pe.wait_ge(rows_copied[0], j + 1 + FREE)
                    pe.wait_ge(rows_copied[1], j + 1 + FREE)
                    for t in range(T):
                        for s in range(S):
                            for a in range(2):
                                bank = ob[s * 2 + a]
                                pe.wait_ge(added[s * 2 + a], j * T + t + FREE)
                                nc.tensor.matmul(bank[:, :, :].rearrange("p h w -> p (h w)"),
                                                 vt[:, (t * S + s) * P:(t * S + s + 1) * P],
                                                 z[m % 2][:, 4 * a:4 * a + 4, :].rearrange("p h w -> p (h w)"),
                                                 start=True, stop=False)
                                h0 = m * ROWS2 + 4 * a
                                parts = runs(h0, 4)
                                for kk, h, n in parts:
                                    last = nc.tensor.matmul(
                                        bank[:, h - h0:h - h0 + n, :].rearrange("p h w -> p (h w)"),
                                        ring[kk % RING][:, t, s, :],
                                        up[:, h:h + n, :].rearrange("p h w -> p (h w)"),
                                        start=False, stop=h + n == h0 + 4)
                                last.then_inc(filled, 1)

                with pe.Fori(0, B) as b:
                    attention(b)
                    pe.wait_ge(crow_copied, b + 1)
                    produce(b, 0)
                    for m in range(CH2):
                        if m < CH2 - 1:
                            produce(b, m + 1)
                        combine(b, m)

            @block.scalar
            def _(act):
                act.wait_ge(const_in, 128)
                start_free(act, rows_copied)

                def attention(b):
                    act.wait_ge(qk_made, b + 1)
                    nc.scalar.activation(qk[:, :, :].rearrange("p a k -> p (a k)"), st[0:UV, 0:2 * UV], ACT.Copy)
                    nc.scalar.activation(vx[0:UV, :], st[0:UV, 512:1024], ACT.Copy).then_inc(qk_copied, 1)
                    act.wait_ge(g_made, b + 1)
                    nc.scalar.activation(grams[:, 0:3, :].rearrange("p a k -> p (a k)"), st[0:UV, 0:3 * UV],
                                         ACT.Copy).then_inc(g_copied, 1)
                    act.wait_ge(lam2_made, b * 4 + 4)
                    nc.scalar.activation(lam[:, :, :], lam2[:, :, :], ACT.Sqrt).then_inc(root_made, 1)
                    act.wait_ge(pk_used, (b + 1) * PIECES)
                    nc.scalar.activation(a_sb[:, :], st[0:UV, 0:UV], ACT.Copy).then_inc(a_copied, 1)
                    act.wait_ge(filled, b * CH2 * 8 + FREE)
                    act.wait_ge(v_made, b + 1)
                    nc.scalar.activation(vt[:, :], st[0:ZR, 0:C], ACT.Copy, scale=gam[0:ZR, 0:1]).then_inc(vt_made, 1)
                    act.wait_ge(pairs_copied[1], b * CH2 + FREE)
                    act.wait_ge(crow_made, b + 1)
                    nc.scalar.activation(crow[:, :, :, :].rearrange("p t s g -> p (t s g)"), st[:, 0:TS * P],
                                         ACT.Copy).then_inc(crow_copied, 1)

                with act.Fori(0, B) as b:
                    attention(b)
                    for m in range(CH2):
                        j = b * CH2 + m
                        act.wait_ge(filled, (b * CH2 + max(m - 1, 0)) * 8 + FREE)
                        for a in range(2):
                            act.wait_ge(rows_t, j * 2 + a + 1)
                            nc.scalar.activation(z[m % 2][:, 4 * a:4 * a + 4, :], tp[a][0:ZR, :, :],
                                                 ACT.Copy).then_inc(rows_copied[a], 1)

            @block.vector
            def _(dve):
                nc.vector.memset(mx[:, :], 0.0).then_inc(ones_set, 1)
                nc.vector.memset(grams[:, 3, :], 0.0).then_inc(ones_set, 1)
                for i in range(2):
                    nc.vector.memset(zt[i][:, :, ZR - 1:ZR], 1.0).then_inc(ones_set, 1)
                start_free(dve, [*pairs_copied, *added])
                dve.wait_ge(ones_set, 4)
                dve.wait_ge(const_in, 128)
                nc.vector.tensor_copy(mx[0:UV, UV:UV + 1], k("p_sum", UV)).then_inc(ones_set, 1)
                nc.vector.tensor_copy(mx[UV:UV + 1, :], cst[UV:UV + 1, CONST_AT["bias_row"]]).then_inc(ones_set, 1)

                def attention(b, ch):
                    nc.vector.tensor_copy(xp[:, :, :].rearrange("p (t s) k -> p t s k", t=T),
                                          xps[:, :, :, :].rearrange("p (b t) s k -> p b t s k", t=T)[:, b, :, :, :]
                                          ).then_inc(xp_made, 1)
                    for n in range(TS):
                        ins = nc.vector.tensor_scalar(dg[:, n, :], k("ident"), coef[:, b, n // S, n % S:n % S + 1],
                                                      None, ALU.mult)
                        if n < TS - 1:
                            ch.link(ins)
                        else:
                            ins.then_inc(dg_made, 1)
                    for j in range(2):
                        for a in range(2):
                            n = b * 4 + j * 2 + a + 1
                            rows = slice(a * H // 2, (a + 1) * H // 2)
                            dve.wait_ge(half_made, n)
                            nc.vector.tensor_tensor(
                                m1, st[0:UV, 0:half].rearrange("p (h v) -> p h v", v=LOW),
                                k("dh_e", UV)[:, rows].unsqueeze(2).broadcast_to([UV, H // 2, LOW]),
                                ALU.mult).then_inc(half_taken, 1)
                            dve.wait_ge(lam_made, n)
                            ch.link(nc.vector.tensor_tensor(
                                work[:, :, :], st[:, half:2 * half].rearrange("p (h v) -> p h v", v=LOW),
                                k("dw8").unsqueeze(1).broadcast_to([P, H // 2, LOW]), ALU.mult))
                            nc.vector.tensor_reduce(lam2[:, j, rows], work[:, :, :], AX.X,
                                                    ALU.add).then_inc(lam2_made, 1)
                            dve.wait_ge(lam2_made, n)
                    dve.wait_ge(root_made, b + 1)
                    ch.link(nc.vector.reciprocal(rk[:, :], lam[:, 1, :]))
                    for e in range(PIECES):
                        if e >= 2:
                            dve.wait_ge(pk_used, b * PIECES + e - 1)
                        rows = slice(e * rows_pk, (e + 1) * rows_pk)
                        nc.vector.tensor_tensor(pk[e % 2][:, :, :], p_sb[:, rows, :],
                                                rk[:, rows].unsqueeze(2).broadcast_to([P, rows_pk, UV]),
                                                ALU.mult).then_inc(pk_made, 1)
                    dve.wait_ge(m_made, b + 1)
                    ch.link(nc.vector.tensor_copy(mx[0:UV, 0:UV], st[0:UV, 512:512 + UV]))
                    nc.vector.tensor_scalar(ms[:, :], k("dh_e", UV), st[0:UV, 512 + UV:512 + UV + 1], float(P),
                                            ALU.mult, ALU.mult).then_inc(mx_made, 1)
                    dve.wait_ge(v_made, b + 1)
                    ch.link(nc.vector.scalar_tensor_tensor(out=den[:, :], in0=lam[:, 0, :], scalar=float(HW),
                                                           in1=st[:, 512:512 + H], op0=ALU.mult, op1=ALU.add))
                    ch.link(nc.vector.reciprocal(rr[:, 0, :], den[:, :]))
                    ch.link(nc.vector.tensor_tensor(rr[:, 1, :], lam[:, 0, :], rr[:, 0, :], ALU.mult))
                    dve.wait_ge(crow_copied, b + 1)
                    return ch

                def produce(b, m):
                    j = b * CH2 + m
                    rows = slice(m * ROWS2, (m + 1) * ROWS2)
                    dve.wait_ge(rows_copied[1], b * CH2 + max(m - 1, 0) + FREE)
                    nc.vector.tensor_copy(zt[m % 2][:, :, UV:UV + 1], rr[:, 1, rows].unsqueeze(2))
                    nc.vector.tensor_tensor(zt[m % 2][:, :, 0:UV], p_sb[:, rows, :],
                                            rr[:, 0, rows].unsqueeze(2).broadcast_to([P, ROWS2, UV]),
                                            ALU.mult).then_inc(zt_made, 1)
                    for a in range(2):
                        dve.wait_ge(pairs_t, j * 2 + a + 1)
                        for n in range(2):
                            kk = m * DROWS + 2 * a + n
                            if kk > HD - 2:
                                continue
                            last = nc.vector.tensor_tensor(
                                ring[kk % RING][:, :, :, :],
                                tp[a][:, n * T:(n + 1) * T, :].unsqueeze(2).broadcast_to([P, T, S, P]),
                                crow[:, :, :, :], ALU.mult)
                        last.then_inc(pairs_copied[a], 1)

                with dve.Fori(0, B) as b:
                    ch = Chain(dve, chain_sem, b * 12)
                    attention(b, ch)
                    produce(b, 0)
                    for m in range(CH2):
                        if m < CH2 - 1:
                            produce(b, m + 1)
                        for t in range(T):
                            u = (b * CH2 + m) * T + t
                            i = (m * T + t) % XBUF
                            dve.wait_ge(x_in[i], (b * (CH2 * T // XBUF) + (m * T + t) // XBUF) * 16 + 16)
                            for s in range(S):
                                for a in range(2):
                                    dve.wait_ge(filled, u * 4 + s * 2 + a + 1 + FREE)
                                    ins = nc.vector.tensor_tensor(xt[i][:, s, 4 * a:4 * a + 4, :],
                                                                  ob[s * 2 + a][:, :, :],
                                                                  xt[i][:, s, 4 * a:4 * a + 4, :], ALU.add)
                                    ins.then_inc(added[s * 2 + a], 1)
                            for q in range(4):
                                dve.wait_ge(added[q], u + 1 + FREE)
                            dve.sem_inc(added_all, 1)


def program(nc, x, w_down, w_conv, w_up, wqk, wv, bias, gamma, consts, p_cols, q_cols, r_cols, up_cols, out):
    xd = nc.dram_tensor("downsampled", (B, T, P, POS), F32, kind="Internal").ap()
    with Scope(nc, "all") as sc:
        xps = sc.sb("xps", [P, B * T, S, UV])
        coef = sc.sb("coef", [P, B, T, S])
        first_pass(nc, x, w_down, p_cols, consts, xd, xps)
        with Scope(nc, "gates") as sg:
            xpu = sg.sb("xpu", [P, B * T, UV])
            ohn = sg.sb("ohn", [P, T, K])
            oh_t = sg.sb("oh_t", [P, T, P])
            feat = sg.sb("feat", [P, NT, P])
            cluster_pass(nc, consts, xd, ohn, oh_t)
            average_pass(nc, consts, q_cols, xd, ohn, feat, xpu)
            mixture_pass(nc, consts, w_conv, w_up, feat, oh_t, xps, xpu, coef)
        second_pass(nc, x, p_cols, r_cols, up_cols, consts, wqk, wv, bias, gamma, xd, xps, coef, out)


def shape_constants():
    import numpy as np

    f = np.float32
    ind = 2.0 * np.arange(H) + 1.0
    d = np.stack([np.sqrt(2.0) / np.sqrt(H) * np.cos(u * ind * np.pi / (2.0 * H)) for u in range(LOW)]).astype(f)
    d[0, :] = 1.0 / np.sqrt(H)
    d = d.T
    p = (d[:, None, :, None] * d[None, :, None, :]).astype(f)
    p_cols = p.transpose(1, 0, 2, 3).reshape(W, H * UV)
    s = np.linspace(0.0, HD - 1.0, H).astype(f)
    i0 = np.floor(s).astype(int)
    i1 = np.minimum(i0 + 1, HD - 1)
    fr = (s - i0.astype(f)).astype(f)
    inter = np.zeros((H, HD), f)
    for h in range(H):
        inter[h, i0[h]] += f(1) - fr[h]
        inter[h, i1[h]] += fr[h]
    du = inter.astype(np.float64).T @ d.astype(np.float64)
    q = (du[:, None, :, None] * du[None, :, None, :]).astype(f).reshape(NT, P, UV)
    q_cols = q.transpose(1, 0, 2).reshape(P, NT * UV)
    up = np.zeros((2, HD, H, W), f)
    for h in range(H):
        for r in range(2):
            up[r, :, h, :] = inter[h, pair_of(h) + r] * inter.T
    up_cols = up.reshape(P, H * W)
    r = np.zeros((LOW, LOW, H, LOW), f)
    for v in range(LOW):
        r[:, v, :, v] = d.T
    r_cols = r.reshape(UV, H * LOW)

    row = np.arange(P)
    rb, rf, rk = row // 16, row // 8 % 2, row % 8
    col_b = np.arange(BN) // N
    block = (rb[:, None] == col_b[None, :]).astype(f)
    picks = np.round(np.linspace(0.0, C // 2 - 1.0, K)).astype(int)
    wide = {
        "ident": np.eye(P), "ones": np.ones((P, P)),
        "sel_mu": row[:, None] == (rb * 16 + rk)[None, :], "sel_ex": row[:, None] == (rb * 16 + 8 + rk)[None, :],
        "mask_x": block * (rf == 0)[:, None], "mask_x2": -0.5 * block * (rf == 1)[:, None],
        "mask_term": -0.5 * block * (rf == 0)[:, None], "block": block,
        "block_k": (rb[:, None] == np.arange(B)[None, :]) & (rf == 0)[:, None],
        "is_x2": (rf == 1)[:, None], "tie": np.tile(np.arange(K, 0, -1), (P, 1)),
        "before": np.tile((np.arange(K)[None, :] < np.arange(K)[:, None]).reshape(1, -1), (P, 1)),
        "pick0": (row[:, None, None] + P * np.arange(T)[None, :, None] == picks[None, None, :]).reshape(P, T * K),
        "dw8": d, "dh_e": np.concatenate([np.repeat(d.T, LOW, 0)] * 2), "dw_e": np.concatenate([d.T] * (P // LOW)),
        "p_sum": np.concatenate([p.sum((0, 1), dtype=np.float64).reshape(UV, 1)] * 2),
        "bias_row": np.tile(np.arange(ZR) == ZR - 1, (P, 1)), "rank": row[:, None],
        "mean": np.full((P, 1), 1.0 / POS),
    }
    consts = np.concatenate([np.asarray(wide[n]).astype(f).reshape(P, w) for n, w in CONST_COLS], 1)
    return {"consts": consts, "p_cols": p_cols, "q_cols": q_cols, "r_cols": r_cols, "up_cols": up_cols}


def kernel(x, L0_conv_w_down, L0_conv_w_conv, L0_conv_w_up, L1_conv_Wq, L1_conv_Wk, L1_conv_Wv, L1_conv_out_bias,
           L1_conv_gamma):
    import numpy as np
    import concourse.bacc as bacc
    from concourse.bass_utils import run_bass_kernel_spmd

    def by_group(w):
        return np.asarray(w).reshape(-1, T, P, S).transpose(2, 1, 3, 0).reshape(P, TS, -1)

    wv = by_group(L1_conv_Wv).reshape(P, TS, T, P, S).transpose(0, 1, 2, 4, 3).reshape(P, TS, C)
    arrays = {
        "x": x, "w_down": L0_conv_w_down, "w_conv": L0_conv_w_conv, "w_up": L0_conv_w_up,
        "wqk": np.concatenate([by_group(L1_conv_Wq), by_group(L1_conv_Wk)], 2), "wv": wv,
        "bias": np.asarray(L1_conv_out_bias).reshape(T, P, S).transpose(0, 2, 1).reshape(1, C),
        "gamma": L1_conv_gamma, **shape_constants(),
    }
    arrays = {f"in_{n}": np.ascontiguousarray(a) for n, a in arrays.items()}
    nc = bacc.Bacc("TRN2", target_bir_lowering=False, num_devices=1)
    args = {n[3:]: nc.dram_tensor(n, a.shape, mybir.dt.from_np(a.dtype), kind="ExternalInput").ap()
            for n, a in arrays.items()}
    out = nc.dram_tensor("out", (B, C, H, W), F32, kind="ExternalOutput").ap()
    program(nc, out=out, **args)
    r = run_bass_kernel_spmd(nc, [arrays], core_ids=[0])
    return r.results[0]["out"]
```

```python
import concourse.bass as bass
from concourse import mybir
from contextlib import ExitStack

F32 = mybir.dt.float32
ALU = mybir.AluOpType
ACT = mybir.ActivationFunctionType
AX = mybir.AxisListType

B, C, H, W = 8, 512, 128, 128
P = 128
T, S = 2, 2
TS = T * S
HD, WD = H // 2, W // 2
POS = HD * WD
NT = POS // P
K, N = 8, 2
ITERS = 10
EPS = 1e-6
UV, LOW = 64, 8
HW = H * W
BN = B * N
LOG2PI = 1.8378770664093453

CONST_COLS = [("ident", P), ("ones", P), ("dw8", LOW), ("dh_e", H), ("dw_e", W), ("p_sum", 1),
              ("p_row", UV), ("sel_mu", P), ("sel_ex", P), ("mask_x", BN), ("mask_x2", BN),
              ("mask_term", BN), ("block", BN), ("block_k", B), ("is_x2", 1), ("tie", K), ("before", K * K),
              ("pick0", T * K), ("rank", 1), ("mean", 1)]
CONST_AT, CONST_N = {}, 0
for _name, _width in CONST_COLS:
    CONST_AT[_name] = slice(CONST_N, CONST_N + _width)
    CONST_N += _width
SECOND_N = CONST_AT["sel_mu"].start


class Chain:

    def __init__(self, eng, sem, start=0):
        self.eng, self.sem, self.n = eng, sem, start

    def link(self, ins):
        self.n = self.n + 1
        ins.then_inc(self.sem, 1)
        self.eng.wait_ge(self.sem, self.n)


FREE = 1


def start_free(eng, sems):
    for sem in sems:
        eng.sem_inc(sem, FREE)


class Scope:

    def __init__(self, nc, name):
        self.nc, self.name, self.ctx = nc, name, ExitStack()

    def __enter__(self):
        self.ctx.__enter__()
        return self

    def __exit__(self, *e):
        return self.ctx.__exit__(*e)

    def sb(self, name, shape):
        return self.ctx.enter_context(self.nc.sbuf_tensor(f"{self.name}_{name}", shape, F32))

    def ps(self, name, shape):
        return self.ctx.enter_context(self.nc.psum_tensor(f"{self.name}_{name}", shape, F32))

    def sem(self, name):
        return self.ctx.enter_context(self.nc.semaphore(f"{self.name}_{name}"))


TAPS = [(s, dh, dw) for dw in (0, 1) for dh in (-1, 0, 1) for s in range(S)] + \
       [(s, dh, -1) for dh in (-1, 0, 1) for s in range(S)]
ROWS1 = 32
CH1 = H // ROWS1
TAPS_LEFT = len(TAPS) - 1
OUT1 = ROWS1 // 2
QUADS = S * ROWS1 // 4
SLOTS = 4


def tap_window(buf, tap, rows, row0=0):
    s, dh, dw = tap
    top = 1 + dh + 2 * row0
    left = dw if dw >= 0 else 1
    return buf[:, s, top:top + 2 * rows - 1:2, left:left + 2 * (WD - (dw < 0)) - 1:2]


def first_pass(nc, x, w_down, p_cols, consts, xd, xps):
    xv = x.rearrange("b (t g s) h w -> (b t) g s (h w)", t=T, s=S)
    with Scope(nc, "first") as sc:
        xt = [sc.sb(f"x{c}", [P, S, ROWS1 + 1, W]) for c in range(CH1)]
        p_sb = sc.sb("p", [P, H, UV])
        cst = sc.sb("const", [P, P])
        wd = sc.sb("wd", [P, T, S * 9])
        acc = [sc.sb(f"acc{i}", [P, OUT1, WD]) for i in range(CH1)]
        xT = [sc.sb(f"xT{i}", [P, 4, P]) for i in range(SLOTS)]
        tp = [sc.ps(f"tp{i}", [P, 4, P]) for i in range(SLOTS)]
        freq_ps = [sc.ps(f"freq{s}", [P, 512]) for s in range(S)]
        const_in = sc.sem("const_in")
        x_in = [sc.sem(f"x_in{c}") for c in range(CH1)]
        pe_read = [sc.sem(f"pe_read{c}") for c in range(CH1)]
        top_zero = sc.sem("top_zero")
        started = sc.sem("started")
        tapped = [sc.sem(f"tapped{c}") for c in range(2)]
        chunk_free = [sc.sem(f"chunk_free{c}") for c in range(CH1)]
        xd_out = [sc.sem(f"xd_out{i}") for i in range(CH1)]
        stored = [sc.sem(f"stored{i}") for i in range(CH1)]
        transposed = sc.sem("transposed")
        copied = [sc.sem(f"copied{i}") for i in range(SLOTS)]
        multiplied = [sc.sem(f"multiplied{i}") for i in range(SLOTS)]
        freq_done, freq_read = sc.sem("freq_done"), sc.sem("freq_read")
        ident = cst[:, :]
        quads = CH1 * QUADS

        with nc.Block() as block:
            @block.sync
            def _(sp):
                sp.dma_start(cst[:, :], consts[:, CONST_AT["ident"]]).then_inc(const_in, 16)
                sp.dma_start(wd[:, :, :], w_down.rearrange("(t g) s a b -> g t (s a b)", t=T)).then_inc(const_in, 16)
                sp.dma_start(p_sb[:, :, :], p_cols.rearrange("w (h k) -> w h k", k=UV)).then_inc(const_in, 16)
                with sp.Fori(0, B * T) as i:
                    for c in range(CH1):
                        sp.wait_ge(pe_read[c], i + FREE)
                        sp.wait_ge(chunk_free[c], i + FREE)
                        above = 1 if c == 0 else 0
                        sp.dma_start(xt[c][:, :, above:, :].rearrange("g s h w -> g s (h w)"),
                                     xv[i, :, :, (c * ROWS1 - 1 + above) * W:(c + 1) * ROWS1 * W]
                                     ).then_inc(x_in[c], 16)

            @block.gpsimd
            def _(pool):
                nc.gpsimd.memset(xt[0][:, :, 0, :], 0.0).then_inc(top_zero, 1)
                start_free(pool, stored)
                with pool.Fori(0, B * T) as i:
                    for c in range(CH1):
                        pool.wait_ge(tapped[c % 2], (i * (CH1 // 2) + c // 2 + 1) * TAPS_LEFT)
                        pool.dma_start(xd.rearrange("b t g n -> (b t) g n")[i, :, c * OUT1 * WD:(c + 1) * OUT1 * WD],
                                       acc[c][:, :, :].rearrange("g h w -> g (h w)")).then_inc(xd_out[c], 16)
                        pool.wait_ge(xd_out[c], i * 16 + 16)
                        pool.sem_inc(stored[c], 1)

            @block.vector
            def _(dve):
                dve.wait_ge(top_zero, 1)
                start_free(dve, chunk_free)
                with dve.Fori(0, B) as b:
                    for t in range(T):
                        for c0 in range(0, CH1, 2):
                            i = b * T + t
                            base = (i * (CH1 // 2) + c0 // 2) * TAPS_LEFT
                            for n, (s, dh, dw) in enumerate(TAPS[1:]):
                                for c in (c0, c0 + 1):
                                    if n == 0:
                                        dve.wait_ge(x_in[c], i * 16 + 16)
                                        dve.wait_ge(started, i * CH1 + c + 1)
                                    else:
                                        dve.wait_ge(tapped[c % 2], base + n)
                                    left = 1 if dw < 0 else 0
                                    k = s * 9 + (dh + 1) * 3 + dw + 1
                                    nc.vector.scalar_tensor_tensor(
                                        out=acc[c][:, :, left:], in0=tap_window(xt[c], (s, dh, dw), OUT1),
                                        scalar=wd[:, t, k:k + 1], in1=acc[c][:, :, left:],
                                        op0=ALU.mult, op1=ALU.add).then_inc(tapped[c % 2], 1)
                            for c in (c0, c0 + 1):
                                dve.wait_ge(tapped[c % 2], base + TAPS_LEFT)
                                dve.sem_inc(chunk_free[c], 1)

            @block.scalar
            def _(act):
                start_free(act, [freq_read, *copied])
                act.wait_ge(const_in, 48)
                act.wait_ge(top_zero, 1)
                s0, dh0, dw0 = TAPS[0]
                first_tap = s0 * 9 + (dh0 + 1) * 3 + dw0 + 1
                with act.Fori(0, B) as b:
                    for t in range(T):
                        i = b * T + t
                        for q in range(quads):
                            slot, c = q % SLOTS, q // QUADS
                            if q % QUADS == 0:
                                act.wait_ge(x_in[c], i * 16 + 16)
                                act.wait_ge(stored[c], i + FREE)
                                nc.scalar.activation(acc[c][:, :, :], tap_window(xt[c], TAPS[0], OUT1), ACT.Copy,
                                                     scale=wd[:, t, first_tap:first_tap + 1]).then_inc(started, 1)
                            act.wait_ge(transposed, i * quads + q + 1)
                            act.wait_ge(multiplied[slot], i * (quads // SLOTS) + q // SLOTS + FREE)
                            nc.scalar.activation(xT[slot][:, :, :], tp[slot][:, :, :],
                                                 ACT.Copy).then_inc(copied[slot], 1)
                        act.wait_ge(freq_done, i + 1)
                        for s in range(S):
                            nc.scalar.activation(xps[:, i, s, :], freq_ps[s][:, 0:UV], ACT.Copy
                                                 ).then_inc(freq_read, 1)

            @block.tensor
            def _(pe):
                pe.wait_ge(const_in, 48)
                pe.wait_ge(top_zero, 1)
                start_free(pe, [*multiplied, *pe_read])
                with pe.Fori(0, B) as b:
                    for t in range(T):
                        i = b * T + t

                        def transpose(q):
                            c, s, r = q // QUADS, q % QUADS // (QUADS // 2), q % (QUADS // 2) * 4
                            slot = q % SLOTS
                            if q % QUADS == 0:
                                pe.wait_ge(x_in[c], i * 16 + 16)
                            pe.wait_ge(copied[slot], i * (quads // SLOTS) + q // SLOTS + FREE)
                            for n in range(4):
                                last = nc.tensor.transpose(tp[slot][:, n, :], xt[c][:, s, 1 + r + n, :], ident)
                            last.then_inc(transposed, 1)

                        def multiply(q):
                            c, s, r = q // QUADS, q % QUADS // (QUADS // 2), q % (QUADS // 2) * 4
                            slot = q % SLOTS
                            if q == 0:
                                pe.wait_ge(freq_read, i * S + FREE)
                            pe.wait_ge(copied[slot], i * (quads // SLOTS) + q // SLOTS + 1 + FREE)
                            for n in range(4):
                                row = c * ROWS1 + r + n
                                last = nc.tensor.matmul(freq_ps[s][:, 0:UV], xT[slot][:, n, :], p_sb[:, row, :],
                                                        start=row == 0, stop=row == H - 1)
                            last.then_inc(multiplied[slot], 1)

                        for q in range(quads + 2):
                            if q < quads:
                                transpose(q)
                                if q % QUADS == QUADS - 1:
                                    pe.wait_ge(transposed, i * quads + q + 1)
                                    pe.sem_inc(pe_read[q // QUADS], 1)
                            if q >= 2:
                                multiply(q - 2)
                        pe.wait_ge(multiplied[(quads - 1) % SLOTS], (i + 1) * (quads // SLOTS) + FREE)
                        pe.sem_inc(freq_done, 1)


def cluster_pass(nc, consts, xd, wb_ohn, oh_t):
    ohn = wb_ohn
    with Scope(nc, "cluster") as sc:
        cst = sc.sb("const", [P, CONST_N])
        xx = sc.sb("xx", [P, T, POS])
        xsT = sc.sb("xsT", [P, NT, T, P])
        gram = sc.sb("gram", [P, T, T * P])
        square = sc.sb("square", [P, POS])
        hi, lo, den, inv = (sc.sb(n, [P, T]) for n in ("hi", "lo", "den", "inv"))
        x2 = sc.sb("x2", [P, T])
        wt = sc.sb("wt", [P, T, K])
        prod, dist, near, score, oh = (sc.sb(n, [P, T, K]) for n in ("prod", "dist", "near", "score", "oh"))
        low, best = sc.sb("low", [P, T]), sc.sb("best", [P, T])
        count, rc, empty = sc.sb("count", [P, K]), sc.sb("rc", [P, K]), sc.sb("empty", [P, K])
        rep = sc.sb("rep", [P, T, B * 2, K])
        tp = [sc.ps(f"tp{i}", [P, 4, P]) for i in range(2)]
        gram_ps = [sc.ps(f"gram{t}", [P, 512]) for t in range(T)]
        dot_ps = sc.ps("dot", [P, 512])
        c2_ps = sc.ps("c2", [P, 512])
        cnt_ps = sc.ps("cnt", [P, 512])
        data_in, normal, squared, transposed, copied = (
            sc.sem(n) for n in ("data_in", "normal", "squared", "transposed", "copied"))
        gram_made, gram_copied = sc.sem("gram_made"), sc.sem("gram_copied")
        dots, prods, c2s, labelled, counted, moved, chain_sem = (
            sc.sem(n) for n in ("dots", "prods", "c2s", "labelled", "counted", "moved", "chain"))
        replicated, rep_t, rep_copied = sc.sem("replicated"), sc.sem("rep_t"), sc.sem("rep_copied")
        ident, ones = cst[:, CONST_AT["ident"]], cst[:, CONST_AT["ones"]]
        groups = NT // 2

        with nc.Block() as block:
            @block.sync
            def _(sp):
                sp.dma_start(cst[:, :], consts).then_inc(data_in, 16)
                sp.dma_start(xx[:, :, :], xd[0].rearrange("t g n -> g t n")).then_inc(data_in, 16)
                sp.wait_ge(data_in, 32)

            @block.vector
            def _(dve):
                ch = Chain(dve, chain_sem)
                dve.wait_ge(data_in, 32)
                ch.link(nc.vector.tensor_reduce(hi[:, :], xx[:, :, :], AX.X, ALU.max))
                ch.link(nc.vector.tensor_reduce(lo[:, :], xx[:, :, :], AX.X, ALU.min))
                ch.link(nc.vector.tensor_tensor(den[:, :], hi[:, :], lo[:, :], ALU.subtract))
                ch.link(nc.vector.tensor_scalar(den[:, :], den[:, :], 1e-12, None, ALU.max))
                ch.link(nc.vector.reciprocal(inv[:, :], den[:, :]))
                for t in range(T):
                    nc.vector.tensor_scalar(xx[:, t, :], xx[:, t, :], lo[:, t:t + 1], inv[:, t:t + 1],
                                            ALU.subtract, ALU.mult).then_inc(normal, 1)
                nc.vector.tensor_copy(wt[:, :, :].rearrange("p t k -> p (t k)"),
                                      cst[:, CONST_AT["pick0"]]).then_inc(moved, 1)
                dve.wait_ge(moved, 1)
                dve.wait_ge(squared, T)
                first = 5
                per = 13
                with dve.Fori(0, ITERS + 1) as i:
                    ch = Chain(dve, chain_sem, i * per + first)
                    dve.wait_ge(dots, i + 1)
                    dv = dot_ps[:, 0:T * K].rearrange("p (t k) -> p t k", t=T)
                    nc.vector.tensor_tensor(prod[:, :, :], wt[:, :, :], dv, ALU.mult).then_inc(prods, 1)
                    for t in range(T):
                        ch.link(nc.vector.tensor_scalar(dist[:, t, :], dv[:, t, :], -2.0, x2[:, t:t + 1],
                                                        ALU.mult, ALU.add))
                    dve.wait_ge(c2s, i + 1)
                    ch.link(nc.vector.tensor_tensor(dist[:, :, :], dist[:, :, :],
                                                    c2_ps[:, 0:K].unsqueeze(1).broadcast_to([P, T, K]), ALU.add))
                    ch.link(nc.vector.tensor_reduce(low[:, :], dist[:, :, :], AX.X, ALU.min))
                    ch.link(nc.vector.tensor_tensor(near[:, :, :], dist[:, :, :],
                                                    low[:, :].unsqueeze(2).broadcast_to([P, T, K]), ALU.is_le))
                    ch.link(nc.vector.tensor_tensor(
                        score[:, :, :], near[:, :, :],
                        cst[:, CONST_AT["tie"]].unsqueeze(1).broadcast_to([P, T, K]), ALU.mult))
                    ch.link(nc.vector.tensor_reduce(best[:, :], score[:, :, :], AX.X, ALU.max))
                    nc.vector.tensor_tensor(oh[:, :, :], score[:, :, :],
                                            best[:, :].unsqueeze(2).broadcast_to([P, T, K]),
                                            ALU.is_equal).then_inc(labelled, 1)
                    dve.wait_ge(labelled, i + 1)
                    dve.wait_ge(counted, i + 1)
                    ch.link(nc.vector.tensor_scalar(count[:, :], cnt_ps[:, 0:K], 1.0, None, ALU.max))
                    ch.link(nc.vector.reciprocal(rc[:, :], count[:, :]))
                    ch.link(nc.vector.tensor_scalar(empty[:, :], cnt_ps[:, 0:K], 0.0, None, ALU.is_equal))
                    ch.link(nc.vector.tensor_tensor(ohn[:, :, :], oh[:, :, :],
                                                    rc[:, :].unsqueeze(1).broadcast_to([P, T, K]), ALU.mult))
                    ch.link(nc.vector.tensor_tensor(wt[:, :, :], wt[:, :, :],
                                                    empty[:, :].unsqueeze(1).broadcast_to([P, T, K]), ALU.mult))
                    ch.link(nc.vector.tensor_tensor(wt[:, :, :], wt[:, :, :], ohn[:, :, :], ALU.add))
                    dve.sem_inc(moved, 1)
                for t in range(T):
                    nc.vector.tensor_copy(rep[:, t, :, :], oh[:, t, :].unsqueeze(1).broadcast_to([P, B * 2, K])
                                          ).then_inc(replicated, 1)

            @block.scalar
            def _(act):
                for t in range(T):
                    act.wait_ge(normal, t + 1)
                    if t:
                        act.wait_ge(squared, t)
                    nc.scalar.activation(square[:, :], xx[:, t, :], ACT.Square,
                                         accum_out=x2[:, t:t + 1]).then_inc(squared, 1)
                for n in range(groups):
                    act.wait_ge(transposed, n + 1)
                    nc.scalar.activation(xsT[:, 2 * n:2 * n + 2, :, :].rearrange("p a t g -> p (a t) g"),
                                         tp[n % 2][:, :, :], ACT.Copy).then_inc(copied, 1)
                for t in range(T):
                    act.wait_ge(gram_made, t + 1)
                    nc.scalar.activation(gram[:, t, :], gram_ps[t][:, 0:T * P], ACT.Copy).then_inc(gram_copied, 1)
                for t in range(T):
                    act.wait_ge(rep_t, t + 1)
                    nc.scalar.activation(oh_t[:, t, :], tp[t][:, 0, :], ACT.Copy).then_inc(rep_copied, 1)
                act.wait_ge(rep_copied, T)

            @block.tensor
            def _(pe):
                pe.wait_ge(data_in, 32)
                pe.wait_ge(normal, T)
                for n in range(groups):
                    if n >= 2:
                        pe.wait_ge(copied, n - 1)
                    for a in range(2):
                        for t in range(T):
                            at = (2 * n + a) * P
                            last = nc.tensor.transpose(tp[n % 2][:, 2 * a + t, :], xx[:, t, at:at + P], ident)
                    last.then_inc(transposed, 1)
                pe.wait_ge(copied, groups)
                for t in range(T):
                    for n in range(NT):
                        last = nc.tensor.matmul(gram_ps[t][:, 0:T * P], xsT[:, n, t, :],
                                                xsT[:, n, :, :].rearrange("p t g -> p (t g)"),
                                                start=n == 0, stop=n == NT - 1)
                    last.then_inc(gram_made, 1)
                pe.wait_ge(gram_copied, T)
                with pe.Fori(0, ITERS + 1) as i:
                    pe.wait_ge(moved, i + 1)
                    for t in range(T):
                        for t2 in range(T):
                            last = nc.tensor.matmul(dot_ps[:, t * K:(t + 1) * K], gram[:, t2, t * P:(t + 1) * P],
                                                    wt[:, t2, :], start=t2 == 0, stop=t2 == T - 1)
                    last.then_inc(dots, 1)
                    pe.wait_ge(prods, i + 1)
                    for t in range(T):
                        last = nc.tensor.matmul(c2_ps[:, 0:K], ones, prod[:, t, :], start=t == 0, stop=t == T - 1)
                    last.then_inc(c2s, 1)
                    pe.wait_ge(labelled, i + 1)
                    for t in range(T):
                        last = nc.tensor.matmul(cnt_ps[:, 0:K], ones, oh[:, t, :], start=t == 0, stop=t == T - 1)
                    last.then_inc(counted, 1)
                for t in range(T):
                    pe.wait_ge(replicated, t + 1)
                    nc.tensor.transpose(tp[t][:, 0, :], rep[:, t, :, :].rearrange("p a k -> p (a k)"),
                                        ident).then_inc(rep_t, 1)


def average_pass(nc, consts, q_cols, xd, ohn, feat, xpu):
    with Scope(nc, "average") as sc:
        cst = sc.sb("const", [P, P])
        q_sb = sc.sb("q", [P, NT, UV])
        dbuf = [[sc.sb(f"xd{a}_{t}", [P, POS]) for t in range(T)] for a in range(2)]
        dT = [sc.sb(f"dT{i}", [P, 4, P]) for i in range(SLOTS)]
        tp = [sc.ps(f"tp{i}", [P, 4, P]) for i in range(SLOTS)]
        mean_ps = [sc.ps(f"mean{a}", [P, NT, K]) for a in range(2)]
        freq_ps = [sc.ps(f"freq{a}", [P, T, UV]) for a in range(2)]
        const_in = sc.sem("const_in")
        d_in = [[sc.sem(f"d_in{a}_{t}") for t in range(T)] for a in range(2)]
        batch_done = [sc.sem(f"batch_done{a}") for a in range(2)]
        transposed, averaged, freq_done = (sc.sem(n) for n in ("transposed", "averaged", "freq_done"))
        mean_read, freq_read = ([sc.sem(f"{n}{a}") for a in range(2)] for n in ("mean_read", "freq_read"))
        copied = [sc.sem(f"copied{i}") for i in range(SLOTS)]
        multiplied = [sc.sem(f"multiplied{i}") for i in range(SLOTS)]
        ident = cst[:, :]
        per = NT // 4
        quads = T * per
        turns = quads // SLOTS

        with nc.Block() as block:
            @block.sync
            def _(sp):
                sp.dma_start(cst[:, :], consts[:, CONST_AT["ident"]]).then_inc(const_in, 16)
                sp.dma_start(q_sb[:, :, :], q_cols.rearrange("p (n k) -> p n k", k=UV)).then_inc(const_in, 16)
                with sp.Fori(0, B // 2) as h:
                    for a in range(2):
                        sp.wait_ge(batch_done[a], h + FREE)
                        for t in range(T):
                            sp.dma_start(dbuf[a][t][:, :], xd[h * 2 + a, t, :, :]).then_inc(d_in[a][t], 16)

            @block.tensor
            def _(pe):
                pe.wait_ge(const_in, 32)
                start_free(pe, [*batch_done, *multiplied])
                with pe.Fori(0, B // 2) as h:
                    for a in range(2):
                        b = h * 2 + a
                        d = dbuf[a]

                        def transpose(q):
                            t, n0, slot = q // per, q % per * 4, q % SLOTS
                            if q % per == 0:
                                pe.wait_ge(d_in[a][t], h * 16 + 16)
                            pe.wait_ge(copied[slot], b * turns + q // SLOTS + FREE)
                            for n in range(4):
                                last = nc.tensor.transpose(tp[slot][:, n, :], d[t][:, (n0 + n) * P:(n0 + n + 1) * P],
                                                           ident)
                            last.then_inc(transposed, 1)

                        def multiply(q):
                            t, n0, slot = q // per, q % per * 4, q % SLOTS
                            if q == 0:
                                pe.wait_ge(freq_read[a], h + FREE)
                            pe.wait_ge(copied[slot], b * turns + q // SLOTS + 1 + FREE)
                            for n in range(4):
                                last = nc.tensor.matmul(freq_ps[a][:, t, :], dT[slot][:, n, :], q_sb[:, n0 + n, :],
                                                        start=n0 + n == 0, stop=n0 + n == NT - 1)
                            last.then_inc(multiplied[slot], 1)
                            if q == quads - 1:
                                pe.wait_ge(multiplied[slot], b * turns + turns + FREE)
                                pe.sem_inc(freq_done, 1)

                        for q in range(quads + 2):
                            if q < quads:
                                transpose(q)
                            if q >= 2:
                                multiply(q - 2)
                        pe.wait_ge(mean_read[a], h + FREE)
                        for n in range(NT):
                            for t in range(T):
                                last = nc.tensor.matmul(mean_ps[a][:, n, :], d[t][:, n * P:(n + 1) * P],
                                                        ohn[:, t, :], start=t == 0, stop=t == T - 1)
                        last.then_inc(averaged, 1)
                        pe.wait_ge(averaged, b + 1)
                        pe.sem_inc(batch_done[a], 1)

            @block.scalar
            def _(act):
                start_free(act, [*freq_read, *copied])
                with act.Fori(0, B // 2) as h:
                    for a in range(2):
                        b = h * 2 + a
                        for q in range(quads):
                            slot = q % SLOTS
                            act.wait_ge(transposed, b * quads + q + 1)
                            act.wait_ge(multiplied[slot], b * turns + q // SLOTS + FREE)
                            nc.scalar.activation(dT[slot][:, :, :], tp[slot][:, :, :], ACT.Copy
                                                 ).then_inc(copied[slot], 1)
                        act.wait_ge(freq_done, b + 1)
                        nc.scalar.activation(xpu[:, :, :].rearrange("p (b t) k -> p b t k", t=T)[:, b, :, :],
                                             freq_ps[a][:, :, :], ACT.Copy).then_inc(freq_read[a], 1)

            @block.vector
            def _(dve):
                start_free(dve, mean_read)
                with dve.Fori(0, B // 2) as h:
                    for a in range(2):
                        b = h * 2 + a
                        dve.wait_ge(averaged, b + 1)
                        nc.vector.tensor_copy(feat[:, :, :].rearrange("p n (b f k) -> p n b f k", b=B, f=2)[:, :, b, 0, :],
                                              mean_ps[a][:, :, :]).then_inc(mean_read[a], 1)


def mixture_pass(nc, consts, w_conv, w_up, feat, oh_t, xps, xpu, coef):
    with Scope(nc, "mix") as sc:
        cst = sc.sb("const", [P, CONST_N])
        wc = sc.sb("wc", [K, N])
        wu = sc.sb("wu", [P, T, S])
        ft = sc.sb("ft", [P, NT, P])
        mean_b = sc.sb("mean_b", [P, B, K])
        red0, red, red2 = (sc.sb(n, [P, B, 2, K]) for n in ("red0", "red", "red2"))
        mean_c, var_c = sc.sb("mean_c", [P, 1]), sc.sb("var_c", [P, 1])
        order, less, rank = sc.sb("order", [P, K, K]), sc.sb("less", [P, K, K]), sc.sb("rank", [P, K])
        var0 = sc.sb("var0", [P, K])
        ranked = sc.sb("ranked", [K, B * 2, K])
        wp = sc.sb("wp", [P, N])
        ms, mu, mu2, var, iv, quad, lnv, w1, w2, wmat, term, lnw, wb, cs, rs, rn = (
            sc.sb(n, [P, BN]) for n in ("ms", "mu", "mu2", "var", "iv", "quad", "lnv", "w1", "w2", "wmat", "term",
                                        "lnw", "wb", "cs", "rs", "rn"))
        logit, resp = sc.sb("logit", [P, NT, BN]), sc.sb("resp", [P, NT, BN])
        top, tot, inv = (sc.sb(n, [P, NT, B]) for n in ("top", "tot", "inv"))
        mud, vard, muc = sc.sb("mud", [P, N]), sc.sb("vard", [P, N]), sc.sb("muc", [P, N])
        c0, c1, box0, box1, ya, yb, ye, y = (sc.sb(n, [P, 1]) for n in ("c0", "c1", "box0", "box1", "ya", "yb",
                                                                      "ye", "y"))
        low = sc.sb("low", [P, B * T, UV])
        ymat, one_gate = sc.sb("ymat", [P, B]), sc.sb("one_gate", [P, T, B])
        tp = [sc.ps(f"tp{i}", [P, 4, P]) for i in range(2)]
        a_ps, b_ps, l_ps, m_ps, n_ps, c_ps = (sc.ps(n, [P, 512]) for n in ("a", "b", "l", "m", "n", "c"))
        const_in, chain_sem = sc.sem("const_in"), sc.sem("chain")
        sums, mean_made, centred, squared, spread_sum, spread_made, order_made, picked = (
            sc.sem(n) for n in ("sums", "mean_made", "centred", "squared", "spread_sum", "spread_made",
                                "order_made", "picked"))
        transposed, copied, means, params, weights, logs, logged, terms, scores, shifted, exped, resps, moments, \
            masses, ready = (sc.sem(n) for n in ("transposed", "copied", "means", "params", "weights", "logs",
                                                 "logged", "terms", "scores", "shifted", "exped", "resps",
                                                 "moments", "masses", "ready"))
        gated, sig, sig_in = sc.sem("gated"), sc.sem("sig"), sc.sem("sig_in")
        y_made, act_chain = sc.sem("y_made"), sc.sem("act_chain")

        def k(name):
            return cst[:, CONST_AT[name]]

        fv = feat[:, :, :].rearrange("p n (b f k) -> p n b f k", b=B, f=2)
        groups = NT // 4

        with nc.Block() as block:
            @block.sync
            def _(sp):
                sp.dma_start(cst[:, :], consts).then_inc(const_in, 16)
                sp.dma_start(wc[:, :], w_conv).then_inc(const_in, 16)
                sp.dma_start(wu[:, :, :], w_up.rearrange("(t g s) -> g t s", t=T, s=S)).then_inc(const_in, 16)

            def parameters(pe, i):
                pe.wait_ge(ready, i + 1)
                nc.tensor.matmul(a_ps[:, 0:BN], k("sel_mu"), ms[:, :], start=True, stop=True)
                nc.tensor.matmul(b_ps[:, 0:BN], k("sel_ex"), ms[:, :], start=True, stop=True).then_inc(means, 1)

            def dve_parameters(dve, ch, i):
                dve.wait_ge(means, i + 1)
                ch.link(nc.vector.tensor_copy(mu[:, :], a_ps[:, 0:BN]))
                ch.link(nc.vector.tensor_tensor(mu2[:, :], mu[:, :], mu[:, :], ALU.mult))
                ch.link(nc.vector.tensor_tensor(var[:, :], b_ps[:, 0:BN], mu2[:, :], ALU.subtract))
                ch.link(nc.vector.tensor_scalar(var[:, :], var[:, :], EPS, EPS, ALU.add, ALU.max))

            @block.tensor
            def _(pe):
                pe.wait_ge(const_in, 48)
                pe.wait_ge(sums, 1)
                nc.tensor.matmul(a_ps[:, 0:P], k("ones"), red0[:, :, :, :].rearrange("p b f k -> p (b f k)"),
                                 start=True, stop=True)
                nc.tensor.matmul(b_ps[:, 0:1], red0[:, :, :, :].rearrange("p b f k -> p (b f k)"), k("mean"),
                                 start=True, stop=True).then_inc(mean_made, 1)
                pe.wait_ge(spread_sum, 1)
                nc.tensor.matmul(m_ps[:, 0:P], k("ones"), red2[:, :, :, :].rearrange("p b f k -> p (b f k)"),
                                 start=True, stop=True)
                nc.tensor.matmul(n_ps[:, 0:1], red2[:, :, :, :].rearrange("p b f k -> p (b f k)"), k("mean"),
                                 start=True, stop=True).then_inc(spread_made, 1)
                for n in range(groups):
                    if n >= 2:
                        pe.wait_ge(copied, n - 1)
                    for j in range(4):
                        last = nc.tensor.transpose(tp[n % 2][:, j, :], feat[:, 4 * n + j, :], k("ident"))
                    last.then_inc(transposed, 1)
                pe.wait_ge(order_made, 1)
                nc.tensor.matmul(c_ps[:, 0:N], ranked[:, :, :].rearrange("r a k -> r (a k)"), wc[:, :],
                                 start=True, stop=True).then_inc(picked, 1)
                with pe.Fori(0, ITERS) as i:
                    parameters(pe, i)
                    pe.wait_ge(terms, i + 1)
                    nc.tensor.matmul(c_ps[:, 0:BN], k("ones"), term[:, :], start=True, stop=True).then_inc(logs, 1)
                    pe.wait_ge(weights, i + 1)
                    for n in range(NT):
                        last = nc.tensor.matmul(l_ps[:, n * BN:(n + 1) * BN], ft[:, n, :], wmat[:, :],
                                                start=True, stop=True)
                    last.then_inc(scores, 1)
                    pe.wait_ge(resps, i + 1)
                    nc.tensor.matmul(n_ps[:, 0:BN], k("ones"), rs[:, :], start=True, stop=True).then_inc(masses, 1)
                    for n in range(NT):
                        last = nc.tensor.matmul(m_ps[:, 0:BN], feat[:, n, :], resp[:, n, :],
                                                start=n == 0, stop=n == NT - 1)
                    last.then_inc(moments, 1)
                parameters(pe, ITERS)
                pe.wait_ge(y_made, 1)
                for t in range(T):
                    last = nc.tensor.matmul(l_ps[:, t * B:(t + 1) * B], oh_t[:, t, :], ymat[:, :],
                                            start=True, stop=True)
                last.then_inc(gated, 1)

            @block.scalar
            def _(act):
                act.wait_ge(centred, 1)
                nc.scalar.activation(fv[:, :, :, 1, :], fv[:, :, :, 0, :], ACT.Square).then_inc(squared, 1)
                for n in range(groups):
                    act.wait_ge(transposed, n + 1)
                    nc.scalar.activation(ft[:, 4 * n:4 * n + 4, :], tp[n % 2][:, :, :], ACT.Copy).then_inc(copied, 1)
                with act.Fori(0, ITERS) as i:
                    act.wait_ge(params, i + 1)
                    nc.scalar.activation(lnv[:, :], var[:, :], ACT.Ln).then_inc(act_chain, 1)
                    nc.scalar.activation(lnw[:, :], wb[:, :], ACT.Ln).then_inc(logged, 1)
                    act.wait_ge(shifted, i + 1)
                    nc.scalar.activation(logit[:, :, :], logit[:, :, :], ACT.Exp).then_inc(exped, 1)
                act.wait_ge(sig_in, 1)
                nc.scalar.activation(ye[:, :], yb[:, :], ACT.Exp, scale=-1.0).then_inc(sig, 1)

            @block.vector
            def _(dve):
                ch = Chain(dve, chain_sem)
                dve.wait_ge(const_in, 48)
                for f in range(2):
                    ch.link(nc.vector.tensor_reduce(red0[:, :, f, :],
                                                    fv[:, :, :, 0, :].rearrange("p n b k -> p b k n"), AX.X, ALU.add))
                dve.sem_inc(sums, 1)
                dve.wait_ge(mean_made, 1)
                av = a_ps[:, 0:P].rearrange("p (b f k) -> p b f k", b=B, f=2)
                ch.link(nc.vector.tensor_scalar(mean_b[:, :, :], av[:, :, 0, :], 1.0 / POS, None, ALU.mult))
                ch.link(nc.vector.tensor_copy(mean_c[:, :], b_ps[:, 0:1]))
                for b in range(B):
                    ch.link(nc.vector.tensor_tensor(fv[:, :, b, 0, :], fv[:, :, b, 0, :],
                                                    mean_b[:, b, :].unsqueeze(1).broadcast_to([P, NT, K]),
                                                    ALU.subtract))
                dve.sem_inc(centred, 1)
                dve.wait_ge(squared, 1)
                ch.link(nc.vector.tensor_reduce(red2[:, :, :, :].rearrange("p b f k -> p (b f k)"),
                                                feat[:, :, :].rearrange("p n c -> p c n"), AX.X, ALU.add))
                dve.sem_inc(spread_sum, 1)
                dve.wait_ge(spread_made, 1)
                ch.link(nc.vector.tensor_tensor(var_c[:, :], n_ps[:, 0:1], k("is_x2"), ALU.mult))
                mv = m_ps[:, 0:P].rearrange("p (b f k) -> p b f k", b=B, f=2)
                ch.link(nc.vector.tensor_copy(var0[:, :], mv[:, 0, 1, :]))
                mine = var0[:, :].unsqueeze(2).broadcast_to([P, K, K])
                other = var0[:, :].unsqueeze(1).broadcast_to([P, K, K])
                ch.link(nc.vector.tensor_tensor(less[:, :, :], other, mine, ALU.is_lt))
                ch.link(nc.vector.tensor_tensor(order[:, :, :], other, mine, ALU.is_equal))
                ch.link(nc.vector.tensor_tensor(order[:, :, :], order[:, :, :],
                                                k("before").rearrange("p (a c) -> p a c", a=K), ALU.mult))
                ch.link(nc.vector.tensor_tensor(less[:, :, :], less[:, :, :], order[:, :, :], ALU.add))
                ch.link(nc.vector.tensor_reduce(rank[:, :], less[:, :, :], AX.X, ALU.add))
                ch.link(nc.vector.tensor_scalar(ranked[:, :, :],
                                                rank[0:K, :].unsqueeze(1).broadcast_to([K, B * 2, K]),
                                                cst[0:K, CONST_AT["rank"]], None, ALU.is_equal))
                dve.sem_inc(order_made, 1)
                dve.wait_ge(picked, 1)
                ch.link(nc.vector.tensor_copy(wp[:, :], c_ps[:, 0:N]))
                dve.wait_ge(copied, groups)
                msv = ms[:, :].rearrange("p (b n) -> p b n", n=N)
                for n, (tile, pos) in enumerate(((0, 0), (NT - 1, P - 1))):
                    ch.link(nc.vector.tensor_tensor(msv[:, :, n], ft[:, tile, pos:pos + 1].broadcast_to([P, B]),
                                                    var_c[:, 0:1].broadcast_to([P, B]), ALU.add))
                ch.link(nc.vector.memset(wb[:, :], 1.0 / N))
                dve.sem_inc(ready, 1)
                first = ch.n
                lv = logit[:, :, :].rearrange("p n (b c) -> p n b c", c=N)
                per = 23
                with dve.Fori(0, ITERS) as i:
                    ch = Chain(dve, chain_sem, i * per + first)
                    dve_parameters(dve, ch, i)
                    dve.sem_inc(params, 1)
                    ch.link(nc.vector.reciprocal(iv[:, :], var[:, :]))
                    ch.link(nc.vector.tensor_tensor(w1[:, :], mu[:, :], iv[:, :], ALU.mult))
                    ch.link(nc.vector.tensor_tensor(w2[:, :], iv[:, :], k("mask_x2"), ALU.mult))
                    ch.link(nc.vector.tensor_tensor(wmat[:, :], w1[:, :], k("mask_x"), ALU.mult))
                    ch.link(nc.vector.tensor_tensor(wmat[:, :], wmat[:, :], w2[:, :], ALU.add))
                    dve.sem_inc(weights, 1)
                    ch.link(nc.vector.tensor_tensor(quad[:, :], mu2[:, :], iv[:, :], ALU.mult))
                    dve.wait_ge(act_chain, i + 1)
                    ch.link(nc.vector.tensor_tensor(quad[:, :], quad[:, :], lnv[:, :], ALU.add))
                    ch.link(nc.vector.tensor_tensor(term[:, :], quad[:, :], k("mask_term"), ALU.mult))
                    dve.sem_inc(terms, 1)
                    dve.wait_ge(logs, i + 1)
                    dve.wait_ge(logged, i + 1)
                    ch.link(nc.vector.scalar_tensor_tensor(out=cs[:, :], in0=lnw[:, :], scalar=-0.5 * K * LOG2PI,
                                                           in1=c_ps[:, 0:BN], op0=ALU.add, op1=ALU.add))
                    dve.wait_ge(scores, i + 1)
                    ch.link(nc.vector.tensor_tensor(logit[:, :, :],
                                                    l_ps[:, :].rearrange("p (n c) -> p n c", c=BN),
                                                    cs[:, :].unsqueeze(1).broadcast_to([P, NT, BN]), ALU.add))
                    ch.link(nc.vector.tensor_tensor(top[:, :, :], lv[:, :, :, 0], lv[:, :, :, 1], ALU.max))
                    ch.link(nc.vector.tensor_tensor(lv, lv, top[:, :, :].unsqueeze(3).broadcast_to([P, NT, B, N]),
                                                    ALU.subtract))
                    dve.sem_inc(shifted, 1)
                    dve.wait_ge(exped, i + 1)
                    ch.link(nc.vector.tensor_tensor(tot[:, :, :], lv[:, :, :, 0], lv[:, :, :, 1], ALU.add))
                    ch.link(nc.vector.reciprocal(inv[:, :, :], tot[:, :, :]))
                    ch.link(nc.vector.tensor_tensor(
                        resp[:, :, :].rearrange("p n (b c) -> p n b c", c=N), lv,
                        inv[:, :, :].unsqueeze(3).broadcast_to([P, NT, B, N]), ALU.mult))
                    ch.link(nc.vector.tensor_reduce(rs[:, :], resp[:, :, :].rearrange("p n c -> p c n"),
                                                    AX.X, ALU.add))
                    dve.sem_inc(resps, 1)
                    dve.wait_ge(masses, i + 1)
                    ch.link(nc.vector.reciprocal(rn[:, :], n_ps[:, 0:BN]))
                    ch.link(nc.vector.tensor_scalar(wb[:, :], n_ps[:, 0:BN], 1.0 / POS, None, ALU.mult))
                    dve.wait_ge(moments, i + 1)
                    ch.link(nc.vector.tensor_tensor(ms[:, :], m_ps[:, 0:BN], rn[:, :], ALU.mult))
                    assert isinstance(per, int)
                    dve.sem_inc(ready, 1)
                ch = Chain(dve, chain_sem, ITERS * per + first)
                dve_parameters(dve, ch, ITERS)
                for src, dst in ((mu, mud), (var, vard)):
                    ch.link(nc.vector.tensor_tensor(w1[:, :], src[:, :], k("block"), ALU.mult))
                    ch.link(nc.vector.tensor_reduce(dst[:, :], w1[:, :].rearrange("p (b n) -> p n b", n=N),
                                                    AX.X, ALU.add))
                ch.link(nc.vector.tensor_scalar(muc[:, :], mud[:, :], mean_c[:, 0:1], None, ALU.add))
                ch.link(nc.vector.tensor_tensor(c0[:, :], vard[:, 0:1], vard[:, 1:2], ALU.is_le))
                ch.link(nc.vector.tensor_scalar(c1[:, :], c0[:, :], -1.0, 1.0, ALU.mult, ALU.add))
                for box, a, b in ((box0, c0, c1), (box1, c1, c0)):
                    ch.link(nc.vector.tensor_tensor(ya[:, :], muc[:, 0:1], a[:, :], ALU.mult))
                    ch.link(nc.vector.tensor_tensor(yb[:, :], muc[:, 1:2], b[:, :], ALU.mult))
                    ch.link(nc.vector.tensor_tensor(box[:, :], ya[:, :], yb[:, :], ALU.add))
                ch.link(nc.vector.tensor_tensor(ya[:, :], box0[:, :], wp[:, 0:1], ALU.mult))
                ch.link(nc.vector.tensor_tensor(yb[:, :], box1[:, :], wp[:, 1:2], ALU.mult))
                ch.link(nc.vector.tensor_tensor(yb[:, :], ya[:, :], yb[:, :], ALU.add))
                dve.sem_inc(sig_in, 1)
                dve.wait_ge(sig, 1)
                ch.link(nc.vector.tensor_scalar(ye[:, :], ye[:, :], 1.0, None, ALU.add))
                ch.link(nc.vector.reciprocal(y[:, :], ye[:, :]))
                ch.link(nc.vector.tensor_scalar(ymat[:, :], k("block_k"), y[:, 0:1], None, ALU.mult))
                dve.sem_inc(y_made, 1)
                dve.wait_ge(gated, 1)
                ch.link(nc.vector.tensor_scalar(one_gate[:, :, :].rearrange("p t b -> p (t b)"), l_ps[:, 0:T * B],
                                                1.0, None, ALU.add))
                for t in range(T):
                    ch.link(nc.vector.tensor_tensor(
                        coef[:, :, t, :], one_gate[:, t, :].unsqueeze(2).broadcast_to([P, B, S]),
                        wu[:, t, :].unsqueeze(1).broadcast_to([P, B, S]), ALU.mult))
                cv = coef[:, :, :, :].rearrange("p b t s -> p (b t) s")
                for s in range(S):
                    ch.link(nc.vector.tensor_tensor(low[:, :, :], xpu[:, :, :],
                                                    cv[:, :, s].unsqueeze(2).broadcast_to([P, B * T, UV]), ALU.mult))
                    ch.link(nc.vector.tensor_tensor(xps[:, :, s, :], xps[:, :, s, :], low[:, :, :], ALU.add))


ROWS2 = 8
CH2 = H // ROWS2
DROWS = ROWS2 // 2
HALO = DROWS + 2
HALF = ROWS2 // 2
UNITS = H // HALF
PAIRS = HALF // 2
FILLS = PAIRS + 1
BANKS = TS
XBUF = 4
PIECES = 16
PKBUF = 4
SET_UP = 5

CHUNK_LEAD = 2
FILL_LEAD = 2 * FILLS + 1
UNIT_LEAD = BANKS + 1


def second_pass(nc, x, p_cols, r_cols, inter_cols, consts, wqk, wv, bias, gamma, xd, xps, coef, out):
    xv = x.rearrange("b (t g s) h w -> b t g s (h w)", t=T, s=S)
    ov = out.rearrange("b (t g s) h w -> b t g s (h w)", t=T, s=S)
    with Scope(nc, "second") as sc:
        cst = sc.sb("const", [P, SECOND_N])
        inter = sc.sb("inter", [P, W + 4 * HD])
        p_sb = sc.sb("p", [P, H, UV])
        r_sb = sc.sb("r", [UV, H * LOW])
        wqk_sb, wv_sb = sc.sb("wqk", [P, TS, P]), sc.sb("wv", [P, TS, C])
        gam = sc.sb("gam", [P, 1])
        xt = [sc.sb(f"x{i}", [P, T, S, HALF, W]) for i in range(XBUF)]
        dd = [sc.sb(f"dd{i}", [P, T, HALO, WD]) for i in range(2)]
        mid = [sc.sb(f"mid{i}", [P, T, ROWS2, WD]) for i in range(2)]
        part = sc.sb("part", [P, T, ROWS2, WD])
        scaled_rows = [sc.sb(f"scaled{i}", [P, T, S, ROWS2, WD]) for i in range(2)]
        zt = [sc.sb(f"zt{i}", [P, ROWS2, UV]) for i in range(2)]
        left = [sc.sb(f"left{i}", [P, HALF, TS, P]) for i in range(2)]
        right = [sc.sb(f"right{i}", [P, HALF, W]) for i in range(2)]
        xp = sc.sb("xp", [P, TS, UV])
        qk = sc.sb("qk", [UV, 2, UV])
        vx = sc.sb("vx", [UV + 1, C])
        grams = sc.sb("grams", [UV, 4, UV])
        work, m1 = sc.sb("work", [P, H // 2, LOW]), sc.sb("m1", [UV, H // 2, LOW])
        lam2, lam = sc.sb("lam2", [P, 2, H]), sc.sb("lam", [P, 2, H])
        rk, den, rr = sc.sb("rk", [P, H]), sc.sb("den", [P, H]), sc.sb("rr", [P, H])
        pk = [sc.sb(f"pk{i}", [P, H // PIECES, UV]) for i in range(PKBUF)]
        a_sb, a_free, mx = sc.sb("a", [UV, UV]), sc.sb("a_free", [UV, UV]), sc.sb("mx", [UV, P])
        ms = sc.sb("ms", [UV, H])
        vt = sc.sb("vt", [P, C])
        gain, shift = sc.sb("gain", [P, TS]), sc.sb("shift", [P, TS])
        ob = [sc.ps(f"o{i}", [P, HALF, W]) for i in range(BANKS)]
        tp = [sc.ps(f"tp{i}", [P, 4, P]) for i in range(2)]
        st = sc.ps("st", [P, 1024])

        const_in = sc.sem("const_in")
        x_in = [sc.sem(f"x_in{i}") for i in range(XBUF)]
        y_out = [sc.sem(f"y_out{i}") for i in range(XBUF)]
        stored = [sc.sem(f"stored{i}") for i in range(XBUF)]
        dd_in = [sc.sem(f"dd_in{i}") for i in range(2)]
        set_up, weighted, interpolated, scaled = (sc.sem(n) for n in ("set_up", "weighted", "interpolated", "scaled"))
        zt_made, transposed, multiplied = sc.sem("zt_made"), sc.sem("transposed"), sc.sem("multiplied")
        copied = [sc.sem(f"copied{i}") for i in range(2)]
        added = [sc.sem(f"added{i}") for i in range(BANKS)]
        chain_sem = sc.sem("chain")
        (xp_made, qk_made, qk_copied, g_made, g_copied, half_made, half_taken, lam_made, lam2_made, root_made,
         pk_made, pk_used, a_made, a_copied, a_freed, m_made, mx_made, v_made, vt_made, factors_made) = (
            sc.sem(n) for n in (
                "xp_made", "qk_made", "qk_copied", "g_made", "g_copied", "half_made", "half_taken", "lam_made",
                "lam2_made", "root_made", "pk_made", "pk_used", "a_made", "a_copied", "a_freed", "m_made",
                "mx_made", "v_made", "vt_made", "factors_made"))

        def k(name, rows=P):
            return cst[0:rows, CONST_AT[name]]

        half = H * LOW // 2
        rows_pk = H // PIECES
        row_w = inter[:, W:].rearrange("p (k i) -> p k i", k=4)
        hi, lo = slice(UV, P), slice(0, UV)

        def chunk_of(u):
            return u // 2

        def batches(eng, step, prologue=None):
            if prologue:
                prologue()
            with eng.Fori(0, B - 1) as b:
                for u in range(UNITS):
                    step(b, u, True)
            for u in range(UNITS):
                step(B - 1, u, False)

        with nc.Block() as block:
            @block.sync
            def _(sp):
                def load_rows(b, m):
                    slot, n = m % 2, m % CH2
                    sp.wait_ge(interpolated, b * CH2 + m + CHUNK_LEAD - 1)
                    batch = b + m // CH2
                    rows = xd[batch].rearrange("t g n -> g t n")
                    first, last = max(n * DROWS - 1, 0), min(n * DROWS + DROWS + 1, HD)
                    at = first - (n * DROWS - 1)
                    if n == 0:
                        sp.dma_start(dd[slot][:, :, 0, :], rows[:, :, 0:WD]).then_inc(dd_in[slot], 16)
                    if n == CH2 - 1:
                        sp.dma_start(dd[slot][:, :, HALO - 1, :], rows[:, :, (HD - 1) * WD:HD * WD]
                                     ).then_inc(dd_in[slot], 16)
                    sp.dma_start(dd[slot][:, :, at:at + last - first, :].rearrange("g t h w -> g t (h w)"),
                                 rows[:, :, first * WD:last * WD]).then_inc(dd_in[slot], 16)

                for dst, src in ((cst[:, :], consts[:, 0:SECOND_N]), (inter[:, :], inter_cols),
                                 (r_sb[:, :], r_cols), (wqk_sb[:, :, :], wqk), (wv_sb[:, :, :], wv),
                                 (vx[UV:UV + 1, :], bias),
                                 (gam[:, :], gamma.rearrange("(a b) -> a b", b=1).broadcast_to([P, 1])),
                                 (p_sb[:, :, :], p_cols.rearrange("w (h k) -> w h k", k=UV))):
                    sp.dma_start(dst, src).then_inc(const_in, 16)

                def step(b, u, more):
                    if u % 2 == 0 and (more or chunk_of(u) < CH2 - 1):
                        load_rows(b, chunk_of(u) + 1)
                    i = u % XBUF
                    sp.wait_ge(stored[i], b * (UNITS // XBUF) + u // XBUF + FREE)
                    for t in range(T):
                        sp.dma_start(xt[i][:, t, :, :, :].rearrange("g s h w -> g s (h w)"),
                                     xv[b, t, :, :, u * HALF * W:(u + 1) * HALF * W]).then_inc(x_in[i], 16)

                batches(sp, step, lambda: load_rows(0, 0))

            @block.gpsimd
            def _(pool):
                start_free(pool, stored)
                with pool.Fori(0, B) as b:
                    for u in range(UNITS):
                        i = u % XBUF
                        pool.wait_ge(added[BANKS - 1], b * UNITS + u + 1 + FREE)
                        for t in range(T):
                            pool.dma_start(ov[b, t, :, :, u * HALF * W:(u + 1) * HALF * W],
                                           xt[i][:, t, :, :, :].rearrange("g s h w -> g s (h w)")
                                           ).then_inc(y_out[i], 16)
                        pool.wait_ge(y_out[i], (b * (UNITS // XBUF) + u // XBUF) * T * 16 + T * 16)
                        pool.sem_inc(stored[i], 1)

            @block.tensor
            def _(pe):
                pe.wait_ge(const_in, 128)
                pe.wait_ge(set_up, SET_UP)
                pe.sem_inc(transposed, FILL_LEAD)
                pe.sem_inc(multiplied, UNIT_LEAD)

                def qkv(q, first):
                    if not first:
                        pe.wait_ge(vt_made, q)
                        pe.wait_ge(factors_made, q)
                    pe.wait_ge(xp_made, q + 1)
                    for n in range(TS):
                        last = nc.tensor.matmul(st[0:UV, 512:1024], xp[:, n, :], wv_sb[:, n, :],
                                                start=n == 0, stop=n == TS - 1)
                    for j in range(2):
                        for n in range(TS):
                            last = nc.tensor.matmul(st[0:UV, j * UV:(j + 1) * UV], wqk_sb[:, n, j * UV:(j + 1) * UV],
                                                    xp[:, n, :], start=n == 0, stop=n == TS - 1)
                    last.then_inc(qk_made, 1)

                def gram(q):
                    pe.wait_ge(qk_copied, q + 1)
                    nc.tensor.matmul(st[:, UV:2 * UV], qk[:, :, :].rearrange("p a k -> p (a k)"), qk[:, 0, :],
                                     start=True, stop=True)
                    nc.tensor.matmul(st[0:UV, 2 * UV:3 * UV], qk[:, 1, :], qk[:, 1, :], start=True, stop=True)
                    nc.tensor.matmul(st[0:UV, 0:UV], qk[:, 1, :], qk[:, 0, :], start=True, stop=True
                                     ).then_inc(g_made, 1)

                def norm_rows(q, n):
                    j, a = n // 2, n % 2
                    if n == 0:
                        pe.wait_ge(g_copied, q + 1)
                    nc.tensor.matmul(st[:, 0:half], grams[:, j + 1:j + 3, :].rearrange("p a k -> p (a k)"),
                                     r_sb[:, a * half:(a + 1) * half], start=True, stop=True).then_inc(half_made, 1)

                def norm_columns(q, n):
                    pe.wait_ge(half_taken, q * 4 + n + 1)
                    nc.tensor.matmul(st[:, half:2 * half], k("dw_e", UV), m1[:, :, :].rearrange("p h v -> p (h v)"),
                                     start=True, stop=True).then_inc(lam_made, 1)

                def over_positions(q, e):
                    pe.wait_ge(pk_made, q * PIECES + e + 1)
                    for n in range(rows_pk):
                        row = e * rows_pk + n
                        last = nc.tensor.matmul(st[0:UV, 0:UV], p_sb[:, row, :], pk[e % PKBUF][:, n, :],
                                                start=row == 0, stop=row == H - 1)
                    last.then_inc(pk_used, 1)

                def small_products(q):
                    pe.wait_ge(a_freed, q + 1)
                    nc.tensor.matmul(st[:, 512 + UV:512 + UV + 1], grams[:, 0:2, :].rearrange("p a k -> p (a k)"),
                                     a_sb[:, 0:1], start=True, stop=True)
                    nc.tensor.matmul(st[0:UV, 512:512 + UV], a_free[:, :], grams[:, 0, :], start=True, stop=True
                                     ).then_inc(m_made, 1)

                def values(q):
                    pe.wait_ge(mx_made, q + 1)
                    nc.tensor.matmul(st[:, 0:C], mx[:, :], vx[0:UV, :], start=True, stop=True)
                    nc.tensor.matmul(st[:, 512:512 + H], k("dw_e", UV), ms[:, :], start=True, stop=True)
                    for n in range(TS):
                        last = nc.tensor.matmul(st[:, 512 + H + n:512 + H + n + 1], vx[:, n * P:(n + 1) * P],
                                                k("p_sum", UV + 1), start=True, stop=True)
                    last.then_inc(v_made, 1)

                def stage(q, u, first=False):
                    if u == 1:
                        qkv(q, first)
                    elif u == 3:
                        gram(q)
                    elif u in (5, 7, 9, 11, 13):
                        n = (u - 5) // 2
                        if n > 0:
                            norm_columns(q, n - 1)
                        if n < 4:
                            norm_rows(q, n)
                    elif 17 <= u < 17 + PIECES // 2:
                        over_positions(q, 2 * (u - 17))
                        over_positions(q, 2 * (u - 17) + 1)
                    elif u == 27:
                        small_products(q)
                    elif u == 29:
                        values(q)

                def fill(b, u, n):
                    m, a = chunk_of(u), u % 2
                    c, slot = m % 2, (a * FILLS + n) % 2
                    if n == 0 and a == 0:
                        pe.wait_ge(scaled, b * CH2 + m + 1 + CHUNK_LEAD)
                        pe.wait_ge(zt_made, b * CH2 + m + 1)
                    pe.wait_ge(copied[slot], b * CH2 * FILLS + m * FILLS + (a * FILLS + n) // 2 + FREE)
                    for i in range(TS if n < PAIRS else PAIRS):
                        if n < PAIRS:
                            r = a * HALF + 2 * n
                            src = scaled_rows[c][:, i // S, i % S, r:r + 2, :]
                        else:
                            r = a * HALF + 2 * i
                            src = zt[c][:, r:r + 2, :]
                        last = nc.tensor.transpose(tp[slot][:, i, :], src.rearrange("p h w -> p (h w)"), k("ident"))
                    last.then_inc(transposed, 1)

                def multiply(b, u, n):
                    m, a = chunk_of(u), u % 2
                    if n == 0:
                        pe.wait_ge(copied[0], b * CH2 * FILLS + m * FILLS + (a * FILLS + FILLS + 1) // 2 + FREE)
                        pe.wait_ge(copied[1], b * CH2 * FILLS + m * FILLS + (a * FILLS + FILLS) // 2 + FREE)
                    pe.wait_ge(added[n], b * UNITS + u + FREE)
                    for r in range(HALF):
                        last = nc.tensor.matmul(ob[n][:, r, :], left[a][:, r, n, :], right[a][:, r, :],
                                                start=True, stop=True)
                    last.then_inc(multiplied, 1)

                def prologue():
                    for u in range(UNITS):
                        stage(0, u, True)
                    for n in range(FILLS):
                        fill(0, 0, n)

                def step(b, u, more):
                    for n in range(BANKS):
                        multiply(b, u, n)
                        if n < FILLS and (more or u < UNITS - 1):
                            fill(b, u + 1, n)
                    if more:
                        stage(b + 1, u)

                batches(pe, step, prologue)

            @block.scalar
            def _(act):
                act.wait_ge(const_in, 128)
                start_free(act, copied)
                act.sem_inc(scaled, CHUNK_LEAD)

                def stage(q, u):
                    if u == 2:
                        act.wait_ge(qk_made, q + 1)
                        nc.scalar.activation(qk[:, :, :].rearrange("p a k -> p (a k)"), st[0:UV, 0:2 * UV], ACT.Copy)
                        nc.scalar.activation(vx[0:UV, :], st[0:UV, 512:1024], ACT.Copy).then_inc(qk_copied, 1)
                    elif u == 4:
                        act.wait_ge(g_made, q + 1)
                        nc.scalar.activation(grams[:, 0:3, :].rearrange("p a k -> p (a k)"), st[0:UV, 0:3 * UV],
                                             ACT.Copy).then_inc(g_copied, 1)
                    elif u == 15:
                        act.wait_ge(lam2_made, q * 4 + 4)
                        nc.scalar.activation(lam[:, :, :], lam2[:, :, :], ACT.Sqrt).then_inc(root_made, 1)
                    elif u == 25:
                        act.wait_ge(pk_used, q * PIECES + PIECES)
                        nc.scalar.activation(a_sb[:, :], st[0:UV, 0:UV], ACT.Copy).then_inc(a_copied, 1)
                    elif u == 30:
                        act.wait_ge(v_made, q + 1)
                        nc.scalar.activation(vt[:, :], st[:, 0:C], ACT.Copy, scale=gam[:, 0:1]).then_inc(vt_made, 1)

                def scale(b, m):
                    c = m % 2
                    act.wait_ge(interpolated, b * CH2 + m + 1 + CHUNK_LEAD)
                    act.wait_ge(transposed, (b * CH2 + m) * 2 * FILLS - 2 * FILLS + FILL_LEAD)
                    for t in range(T):
                        for s in range(S):
                            n = t * S + s
                            last = nc.scalar.activation(scaled_rows[c][:, t, s, :, :], mid[c][:, t, :, :], ACT.Identity,
                                                        scale=gain[:, n:n + 1], bias=shift[:, n:n + 1])
                    last.then_inc(scaled, 1)

                def copy(b, u):
                    m, a = chunk_of(u), u % 2
                    act.wait_ge(multiplied, (b * UNITS + u) * BANKS - BANKS + UNIT_LEAD)
                    if u % UNITS < 2:
                        act.wait_ge(vt_made, b + u // UNITS + 1)
                        for rows, e in ((lo, 0), (hi, 1)):
                            nc.scalar.activation(left[a][rows, e:HALF:2, :, :].rearrange("p h n g -> p h (n g)"),
                                                 vt[rows, :].unsqueeze(1).broadcast_to([UV, PAIRS, C]), ACT.Copy)
                    for n in range(FILLS):
                        slot = (a * FILLS + n) % 2
                        act.wait_ge(transposed, (b * CH2 + m) * 2 * FILLS + a * FILLS + n + 1 + FILL_LEAD)
                        if n < PAIRS:
                            nc.scalar.activation(left[a][lo, 2 * n + 1, :, :], tp[slot][lo, :, :], ACT.Copy)
                            nc.scalar.activation(left[a][hi, 2 * n, :, :], tp[slot][hi, :, :], ACT.Copy
                                                 ).then_inc(copied[slot], 1)
                        else:
                            nc.scalar.activation(right[a][lo, 0:HALF:2, :], tp[slot][lo, 0:PAIRS, :], ACT.Copy)
                            nc.scalar.activation(right[a][hi, 1:HALF:2, :], tp[slot][hi, 0:PAIRS, :], ACT.Copy
                                                 ).then_inc(copied[slot], 1)

                def prologue():
                    for u in range(UNITS):
                        stage(0, u)
                    scale(0, 0)
                    copy(0, 0)

                def step(b, u, more):
                    if more:
                        stage(b + 1, u)
                    if more or u < UNITS - 1:
                        copy(b, u + 1)
                    if u % 2 == 0 and (more or chunk_of(u) < CH2 - 1):
                        scale(b, chunk_of(u) + 1)

                batches(act, step, prologue)

            @block.vector
            def _(dve):
                nc.vector.memset(grams[:, 3, :], 0.0).then_inc(set_up, 1)
                start_free(dve, added)
                dve.sem_inc(interpolated, CHUNK_LEAD)
                dve.wait_ge(const_in, 128)
                for i in range(2):
                    for rows, e in ((hi, 0), (lo, 1)):
                        nc.vector.tensor_copy(right[i][rows, e:HALF:2, :],
                                              inter[rows, 0:W].unsqueeze(1).broadcast_to([UV, PAIRS, W])
                                              ).then_inc(set_up, 1)
                dve.wait_ge(set_up, SET_UP)

                def take_rows(q, n):
                    rows = slice(n % 2 * H // 2, (n % 2 + 1) * H // 2)
                    dve.wait_ge(half_made, q * 4 + n + 1)
                    nc.vector.tensor_tensor(
                        m1[:, :, :], st[0:UV, 0:half].rearrange("p (h v) -> p h v", v=LOW),
                        k("dh_e", UV)[:, rows].unsqueeze(2).broadcast_to([UV, H // 2, LOW]), ALU.mult
                    ).then_inc(half_taken, 1)

                def take_columns(q, n, ch):
                    rows = slice(n % 2 * H // 2, (n % 2 + 1) * H // 2)
                    if n > 0:
                        dve.wait_ge(lam2_made, q * 4 + n)
                    dve.wait_ge(lam_made, q * 4 + n + 1)
                    ch.link(nc.vector.tensor_tensor(
                        work[:, :, :], st[:, half:2 * half].rearrange("p (h v) -> p h v", v=LOW),
                        k("dw8").unsqueeze(1).broadcast_to([P, H // 2, LOW]), ALU.mult))
                    nc.vector.tensor_reduce(lam2[:, n // 2, rows], work[:, :, :], AX.X, ALU.add
                                            ).then_inc(lam2_made, 1)

                def over_lam(q, e):
                    rows = slice(e * rows_pk, (e + 1) * rows_pk)
                    if e >= PKBUF:
                        dve.wait_ge(pk_used, q * PIECES + e - PKBUF + 1)
                    nc.vector.tensor_tensor(pk[e % PKBUF][:, :, :], p_sb[:, rows, :],
                                            rk[:, rows].unsqueeze(2).broadcast_to([P, rows_pk, UV]),
                                            ALU.mult).then_inc(pk_made, 1)

                def stage(b, ahead, u, ch):
                    q = b + ahead
                    if u == 0:
                        if ahead:
                            dve.wait_ge(qk_made, q)
                        nc.vector.tensor_copy(xp[:, :, :].rearrange("p (t s) k -> p t s k", t=T),
                                              xps[:, :, :, :].rearrange("p (b t) s k -> p b t s k", t=T)[:, q, :, :, :]
                                              ).then_inc(xp_made, 1)
                    elif u in (6, 8, 10, 12, 14):
                        n = (u - 6) // 2
                        if n > 0:
                            take_columns(q, n - 1, ch)
                        if n < 4:
                            take_rows(q, n)
                    elif 16 <= u < 16 + PIECES // 2:
                        if u == 16:
                            dve.wait_ge(root_made, q + 1)
                            ch.link(nc.vector.reciprocal(rk[:, :], lam[:, 1, :]))
                        over_lam(q, 2 * (u - 16))
                        over_lam(q, 2 * (u - 16) + 1)
                    elif u == 26:
                        dve.wait_ge(a_copied, q + 1)
                        nc.vector.scalar_tensor_tensor(out=a_free[:, :], in0=k("p_row", UV), scalar=a_sb[:, 0:1],
                                                       in1=a_sb[:, :], op0=ALU.mult, op1=ALU.add
                                                       ).then_inc(a_freed, 1)
                    elif u == 28:
                        dve.wait_ge(m_made, q + 1)
                        nc.vector.tensor_copy(mx[:, :].rearrange("p (e k) -> p e k", e=2),
                                              st[0:UV, 512:512 + UV].unsqueeze(1).broadcast_to([UV, 2, UV]))
                        nc.vector.tensor_scalar(ms[:, :], k("dh_e", UV), st[0:UV, 512 + UV:512 + UV + 1], float(P),
                                                ALU.mult, ALU.mult).then_inc(mx_made, 1)
                    elif u == 30:
                        dve.wait_ge(v_made, q + 1)
                        ch.link(nc.vector.scalar_tensor_tensor(out=den[:, :], in0=lam[:, 0, :], scalar=float(HW),
                                                               in1=st[:, 512:512 + H], op0=ALU.mult, op1=ALU.add))
                        dve.wait_ge(scaled, q * CH2 + CHUNK_LEAD)
                        nc.vector.tensor_copy(gain[:, :].rearrange("p (t s) -> p t s", t=T), coef[:, q, :, :])
                        nc.vector.tensor_scalar(shift[:, :], st[:, 512 + H:512 + H + TS], gam[:, 0:1], None, ALU.mult)
                        ch.link(nc.vector.reciprocal(rr[:, :], den[:, :]))
                        dve.sem_inc(factors_made, 1)

                def interpolate(b, m):
                    c, n = m % 2, m % CH2
                    if c == 0:
                        loads = (m // CH2) * (CH2 // 2 + 1) + n // 2 + 2
                    else:
                        loads = n // 2 + 1 + (n == CH2 - 1)
                    dve.wait_ge(dd_in[c], b * (CH2 // 2 + 1) * 16 + loads * 16)
                    dve.wait_ge(scaled, b * CH2 + m + CHUNK_LEAD - 1)
                    dve.wait_ge(interpolated, b * CH2 + m + CHUNK_LEAD)
                    for e in range(2):
                        for r, buf in enumerate((mid[c], part)):
                            last = nc.vector.tensor_tensor(
                                buf[:, :, :, :].rearrange("p t (i e) w -> p t i e w", e=2)[:, :, :, 1 - e, :],
                                dd[c][:, :, e + r:e + r + DROWS, :],
                                row_w[:, 2 * e + r, n * DROWS:(n + 1) * DROWS].unsqueeze(1).unsqueeze(3)
                                .broadcast_to([P, T, DROWS, WD]), ALU.mult)
                    last.then_inc(weighted, 1)
                    dve.wait_ge(transposed, (b * CH2 + m) * 2 * FILLS - 2 * FILLS + FILL_LEAD)
                    rows = slice(n * ROWS2, (n + 1) * ROWS2)
                    nc.vector.tensor_tensor(zt[c][:, :, :], p_sb[:, rows, :],
                                            rr[:, rows].unsqueeze(2).broadcast_to([P, ROWS2, UV]),
                                            ALU.mult).then_inc(zt_made, 1)
                    dve.wait_ge(weighted, b * CH2 + m + 1)
                    nc.vector.tensor_tensor(mid[c][:, :, :, :], mid[c][:, :, :, :], part[:, :, :, :], ALU.add
                                            ).then_inc(interpolated, 1)

                def add(b, u):
                    i = u % XBUF
                    dve.wait_ge(x_in[i], (b * (UNITS // XBUF) + u // XBUF) * T * 16 + T * 16)
                    for n in range(BANKS):
                        dve.wait_ge(multiplied, (b * UNITS + u) * BANKS + n + 1 + UNIT_LEAD)
                        nc.vector.tensor_tensor(xt[i][:, n // S, n % S, :, :], ob[n][:, :, :],
                                                xt[i][:, n // S, n % S, :, :], ALU.add).then_inc(added[n], 1)

                links = 7

                def prologue():
                    ch = Chain(dve, chain_sem)
                    for u in range(UNITS):
                        stage(0, 0, u, ch)
                    assert ch.n == links
                    interpolate(0, 0)

                chains = {}

                def step(b, u, more):
                    if more:
                        if u == 0:
                            chains[0] = Chain(dve, chain_sem, b * links + links)
                        stage(b, 1, u, chains[0])
                    if u % 2 == 0 and (more or chunk_of(u) < CH2 - 1):
                        interpolate(b, chunk_of(u) + 1)
                    add(b, u)

                batches(dve, step, prologue)


def program(nc, x, w_down, w_conv, w_up, wqk, wv, bias, gamma, consts, p_cols, q_cols, r_cols, inter_cols, out):
    xd = nc.dram_tensor("downsampled", (B, T, P, POS), F32, kind="Internal").ap()
    with Scope(nc, "all") as sc:
        xps = sc.sb("xps", [P, B * T, S, UV])
        coef = sc.sb("coef", [P, B, T, S])
        first_pass(nc, x, w_down, p_cols, consts, xd, xps)
        with Scope(nc, "gates") as sg:
            xpu = sg.sb("xpu", [P, B * T, UV])
            ohn = sg.sb("ohn", [P, T, K])
            oh_t = sg.sb("oh_t", [P, T, P])
            feat = sg.sb("feat", [P, NT, P])
            cluster_pass(nc, consts, xd, ohn, oh_t)
            average_pass(nc, consts, q_cols, xd, ohn, feat, xpu)
            mixture_pass(nc, consts, w_conv, w_up, feat, oh_t, xps, xpu, coef)
        second_pass(nc, x, p_cols, r_cols, inter_cols, consts, wqk, wv, bias, gamma, xd, xps, coef, out)


def shape_constants():
    import numpy as np

    f = np.float32
    ind = 2.0 * np.arange(H) + 1.0
    d = np.stack([np.sqrt(2.0) / np.sqrt(H) * np.cos(u * ind * np.pi / (2.0 * H)) for u in range(LOW)]).astype(f)
    d[0, :] = 1.0 / np.sqrt(H)
    d = d.T
    p = (d[:, None, :, None] * d[None, :, None, :]).astype(f)
    p_cols = p.transpose(1, 0, 2, 3).reshape(W, H * UV)
    s = np.linspace(0.0, HD - 1.0, H).astype(f)
    i0 = np.floor(s).astype(int)
    i1 = np.minimum(i0 + 1, HD - 1)
    fr = (s - i0.astype(f)).astype(f)
    inter = np.zeros((H, HD), f)
    for h in range(H):
        inter[h, i0[h]] += f(1) - fr[h]
        inter[h, i1[h]] += fr[h]
    du = inter.astype(np.float64).T @ d.astype(np.float64)
    q = (du[:, None, :, None] * du[None, :, None, :]).astype(f).reshape(NT, P, UV)
    q_cols = q.transpose(1, 0, 2).reshape(P, NT * UV)
    above = [0.0] + [inter[2 * i, i - 1] for i in range(1, HD)]
    below = [inter[2 * i, i] for i in range(HD)]
    here = [inter[2 * i + 1, i] for i in range(HD)]
    under = [inter[2 * i + 1, i + 1] for i in range(HD - 1)] + [0.0]
    inter_cols = np.concatenate([np.concatenate([inter.T] * 2)] +
                                [np.tile(np.asarray(v, f), (P, 1)) for v in (above, below, here, under)], 1)
    r = np.zeros((LOW, LOW, H, LOW), f)
    for v in range(LOW):
        r[:, v, :, v] = d.T
    r_cols = r.reshape(UV, H * LOW)

    row = np.arange(P)
    rb, rf, rk = row // 16, row // 8 % 2, row % 8
    col_b = np.arange(BN) // N
    block = (rb[:, None] == col_b[None, :]).astype(f)
    picks = np.round(np.linspace(0.0, C // 2 - 1.0, K)).astype(int)
    p_sum = p.sum((0, 1), dtype=np.float64).reshape(UV)
    wide = {
        "ident": np.eye(P), "ones": np.ones((P, P)),
        "sel_mu": row[:, None] == (rb * 16 + rk)[None, :], "sel_ex": row[:, None] == (rb * 16 + 8 + rk)[None, :],
        "mask_x": block * (rf == 0)[:, None], "mask_x2": -0.5 * block * (rf == 1)[:, None],
        "mask_term": -0.5 * block * (rf == 0)[:, None], "block": block,
        "block_k": (rb[:, None] == np.arange(B)[None, :]) & (rf == 0)[:, None],
        "is_x2": (rf == 1)[:, None], "tie": np.tile(np.arange(K, 0, -1), (P, 1)),
        "before": np.tile((np.arange(K)[None, :] < np.arange(K)[:, None]).reshape(1, -1), (P, 1)),
        "pick0": (row[:, None, None] + P * np.arange(T)[None, :, None] == picks[None, None, :]).reshape(P, T * K),
        "dw8": d, "dh_e": np.concatenate([np.repeat(d.T, LOW, 0)] * 2), "dw_e": np.concatenate([d.T] * (P // LOW)),
        "p_sum": np.concatenate([p_sum.reshape(UV, 1) / HW, np.ones((P - UV, 1))]),
        "p_row": np.tile(-p_sum / P, (P, 1)), "rank": row[:, None],
        "mean": np.full((P, 1), 1.0 / POS),
    }
    consts = np.concatenate([np.asarray(wide[n]).astype(f).reshape(P, w) for n, w in CONST_COLS], 1)
    return {"consts": consts, "p_cols": p_cols, "q_cols": q_cols, "r_cols": r_cols, "inter_cols": inter_cols}


def kernel(x, L0_conv_w_down, L0_conv_w_conv, L0_conv_w_up, L1_conv_Wq, L1_conv_Wk, L1_conv_Wv, L1_conv_out_bias,
           L1_conv_gamma):
    import numpy as np
    import concourse.bacc as bacc
    from concourse.bass_utils import run_bass_kernel_spmd

    def by_group(w):
        return np.asarray(w).reshape(-1, T, P, S).transpose(2, 1, 3, 0).reshape(P, TS, -1)

    wv = by_group(L1_conv_Wv).reshape(P, TS, T, P, S).transpose(0, 1, 2, 4, 3).reshape(P, TS, C)
    arrays = {
        "x": x, "w_down": L0_conv_w_down, "w_conv": L0_conv_w_conv, "w_up": L0_conv_w_up,
        "wqk": np.concatenate([by_group(L1_conv_Wq), by_group(L1_conv_Wk)], 2), "wv": wv,
        "bias": np.asarray(L1_conv_out_bias).reshape(T, P, S).transpose(0, 2, 1).reshape(1, C),
        "gamma": L1_conv_gamma, **shape_constants(),
    }
    arrays = {f"in_{n}": np.ascontiguousarray(a) for n, a in arrays.items()}
    nc = bacc.Bacc("TRN2", target_bir_lowering=False, num_devices=1)
    args = {n[3:]: nc.dram_tensor(n, a.shape, mybir.dt.from_np(a.dtype), kind="ExternalInput").ap()
            for n, a in arrays.items()}
    out = nc.dram_tensor("out", (B, C, H, W), F32, kind="ExternalOutput").ap()
    program(nc, out=out, **args)
    r = run_bass_kernel_spmd(nc, [arrays], core_ids=[0])
    return r.results[0]["out"]
```

```python
import concourse.bass as bass
from concourse import mybir
from contextlib import ExitStack

F32 = mybir.dt.float32
ALU = mybir.AluOpType
ACT = mybir.ActivationFunctionType
AX = mybir.AxisListType

B, C, H, W = 8, 512, 128, 128
P = 128
T, S = 2, 2
TS = T * S
HD, WD = H // 2, W // 2
POS = HD * WD
NT = POS // P
K, N = 8, 2
ITERS = 10
EPS = 1e-6
UV, LOW = 64, 8
HW = H * W
BN = B * N
LOG2PI = 1.8378770664093453

CONST_COLS = [("ident", P), ("ones", P), ("dw8", LOW), ("dh_e", H), ("dw_e", W), ("p_sum", 1),
              ("p_row", UV), ("sel_mu", P), ("sel_ex", P), ("mask_x", BN), ("mask_x2", BN),
              ("mask_term", BN), ("block", BN), ("block_k", B), ("is_x2", 1), ("is_x", 1), ("own_rows", B * 2 * B), ("tie", K), ("before", K * K),
              ("pick0", T * K), ("rank", 1)]
CONST_AT, CONST_N = {}, 0
for _name, _width in CONST_COLS:
    CONST_AT[_name] = slice(CONST_N, CONST_N + _width)
    CONST_N += _width


class Chain:

    def __init__(self, eng, sem, start=0):
        self.eng, self.sem, self.n = eng, sem, start

    def link(self, ins):
        self.n = self.n + 1
        ins.then_inc(self.sem, 1)
        self.eng.wait_ge(self.sem, self.n)


FREE = 1


def start_free(eng, sems):
    for sem in sems:
        eng.sem_inc(sem, FREE)


class Scope:

    def __init__(self, nc, name):
        self.nc, self.name, self.ctx, self.sems = nc, name, ExitStack(), []

    def __enter__(self):
        self.ctx.__enter__()
        return self

    def __exit__(self, *e):
        if self.sems:
            self.nc.clear_and_free_semaphores(self.sems)
            self.nc.all_engine_barrier()
        return self.ctx.__exit__(*e)

    def sb(self, name, shape):
        return self.ctx.enter_context(self.nc.sbuf_tensor(f"{self.name}_{name}", shape, F32))

    def ps(self, name, shape):
        return self.ctx.enter_context(self.nc.psum_tensor(f"{self.name}_{name}", shape, F32))

    def sem(self, name):
        self.sems.append(self.nc.alloc_semaphore(f"{self.name}_{name}"))
        return self.sems[-1]


TAPS = [(s, dh, dw) for dw in (0, 1) for dh in (-1, 0, 1) for s in range(S)] + \
       [(s, dh, -1) for dh in (-1, 0, 1) for s in range(S)]
ROWS1 = 32
CH1 = H // ROWS1
TAPS_LEFT = len(TAPS) - 1
OUT1 = ROWS1 // 2
QUADS = S * ROWS1 // 4
SLOTS = 4


def tap_window(buf, tap, rows, row0=0):
    s, dh, dw = tap
    top = 1 + dh + 2 * row0
    left = dw if dw >= 0 else 1
    return buf[:, s, top:top + 2 * rows - 1:2, left:left + 2 * (WD - (dw < 0)) - 1:2]


def first_pass(nc, x, w_down, p_cols, consts, cst, p_sb, xd, xps):
    xv = x.rearrange("b (t g s) h w -> (b t) g s (h w)", t=T, s=S)
    with Scope(nc, "first") as sc:
        xt = [sc.sb(f"x{c}", [P, S, ROWS1 + 1, W]) for c in range(CH1)]
        wd = sc.sb("wd", [P, T, S * 9])
        acc = [sc.sb(f"acc{i}", [P, OUT1, WD]) for i in range(CH1)]
        xT = [sc.sb(f"xT{i}", [P, 4, P]) for i in range(SLOTS)]
        tp = [sc.ps(f"tp{i}", [P, 4, P]) for i in range(SLOTS)]
        freq_ps = [sc.ps(f"freq{s}", [P, 512]) for s in range(S)]
        const_in = sc.sem("const_in")
        x_in = [sc.sem(f"x_in{c}") for c in range(CH1)]
        pe_read = [sc.sem(f"pe_read{c}") for c in range(CH1)]
        top_zero = sc.sem("top_zero")
        started = sc.sem("started")
        tapped = [sc.sem(f"tapped{c}") for c in range(2)]
        chunk_free = [sc.sem(f"chunk_free{c}") for c in range(CH1)]
        xd_out = [sc.sem(f"xd_out{i}") for i in range(CH1)]
        stored = [sc.sem(f"stored{i}") for i in range(CH1)]
        transposed = sc.sem("transposed")
        copied = [sc.sem(f"copied{i}") for i in range(SLOTS)]
        multiplied = [sc.sem(f"multiplied{i}") for i in range(SLOTS)]
        freq_done, freq_read = sc.sem("freq_done"), sc.sem("freq_read")
        ident = cst[:, CONST_AT["ident"]]
        quads = CH1 * QUADS

        with nc.Block() as block:
            @block.sync
            def _(sp):
                sp.dma_start(cst[:, :], consts).then_inc(const_in, 16)
                sp.dma_start(wd[:, :, :], w_down.rearrange("(t g) s a b -> g t (s a b)", t=T)).then_inc(const_in, 16)
                sp.dma_start(p_sb[:, :, :], p_cols.rearrange("w (h k) -> w h k", k=UV)).then_inc(const_in, 16)
                with sp.Fori(0, B * T) as i:
                    for c in range(CH1):
                        sp.wait_ge(pe_read[c], i + FREE)
                        sp.wait_ge(chunk_free[c], i + FREE)
                        above = 1 if c == 0 else 0
                        sp.dma_start(xt[c][:, :, above:, :].rearrange("g s h w -> g s (h w)"),
                                     xv[i, :, :, (c * ROWS1 - 1 + above) * W:(c + 1) * ROWS1 * W]
                                     ).then_inc(x_in[c], 16)

            @block.gpsimd
            def _(pool):
                nc.gpsimd.memset(xt[0][:, :, 0, :], 0.0).then_inc(top_zero, 1)
                start_free(pool, stored)
                with pool.Fori(0, B * T) as i:
                    for c in range(CH1):
                        pool.wait_ge(tapped[c % 2], (i * (CH1 // 2) + c // 2 + 1) * TAPS_LEFT)
                        pool.dma_start(xd.rearrange("b t g n -> (b t) g n")[i, :, c * OUT1 * WD:(c + 1) * OUT1 * WD],
                                       acc[c][:, :, :].rearrange("g h w -> g (h w)")).then_inc(xd_out[c], 16)
                        pool.wait_ge(xd_out[c], i * 16 + 16)
                        pool.sem_inc(stored[c], 1)

            @block.vector
            def _(dve):
                dve.wait_ge(top_zero, 1)
                start_free(dve, chunk_free)
                with dve.Fori(0, B) as b:
                    for t in range(T):
                        for c0 in range(0, CH1, 2):
                            i = b * T + t
                            base = (i * (CH1 // 2) + c0 // 2) * TAPS_LEFT
                            for n, (s, dh, dw) in enumerate(TAPS[1:]):
                                for c in (c0, c0 + 1):
                                    if n == 0:
                                        dve.wait_ge(x_in[c], i * 16 + 16)
                                        dve.wait_ge(started, i * CH1 + c + 1)
                                    else:
                                        dve.wait_ge(tapped[c % 2], base + n)
                                    left = 1 if dw < 0 else 0
                                    k = s * 9 + (dh + 1) * 3 + dw + 1
                                    nc.vector.scalar_tensor_tensor(
                                        out=acc[c][:, :, left:], in0=tap_window(xt[c], (s, dh, dw), OUT1),
                                        scalar=wd[:, t, k:k + 1], in1=acc[c][:, :, left:],
                                        op0=ALU.mult, op1=ALU.add).then_inc(tapped[c % 2], 1)
                            for c in (c0, c0 + 1):
                                dve.wait_ge(tapped[c % 2], base + TAPS_LEFT)
                                dve.sem_inc(chunk_free[c], 1)

            @block.scalar
            def _(act):
                start_free(act, [freq_read, *copied])
                act.wait_ge(const_in, 48)
                act.wait_ge(top_zero, 1)
                s0, dh0, dw0 = TAPS[0]
                first_tap = s0 * 9 + (dh0 + 1) * 3 + dw0 + 1
                with act.Fori(0, B) as b:
                    for t in range(T):
                        i = b * T + t
                        for q in range(quads):
                            slot, c = q % SLOTS, q // QUADS
                            if q % QUADS == 0:
                                act.wait_ge(x_in[c], i * 16 + 16)
                                act.wait_ge(stored[c], i + FREE)
                                nc.scalar.activation(acc[c][:, :, :], tap_window(xt[c], TAPS[0], OUT1), ACT.Copy,
                                                     scale=wd[:, t, first_tap:first_tap + 1]).then_inc(started, 1)
                            act.wait_ge(transposed, i * quads + q + 1)
                            act.wait_ge(multiplied[slot], i * (quads // SLOTS) + q // SLOTS + FREE)
                            nc.scalar.activation(xT[slot][:, :, :], tp[slot][:, :, :],
                                                 ACT.Copy).then_inc(copied[slot], 1)
                        act.wait_ge(freq_done, i + 1)
                        for s in range(S):
                            nc.scalar.activation(xps[:, i, s, :], freq_ps[s][:, 0:UV], ACT.Copy
                                                 ).then_inc(freq_read, 1)

            @block.tensor
            def _(pe):
                pe.wait_ge(const_in, 48)
                pe.wait_ge(top_zero, 1)
                start_free(pe, [*multiplied, *pe_read])
                with pe.Fori(0, B) as b:
                    for t in range(T):
                        i = b * T + t

                        def transpose(q):
                            c, s, r = q // QUADS, q % QUADS // (QUADS // 2), q % (QUADS // 2) * 4
                            slot = q % SLOTS
                            if q % QUADS == 0:
                                pe.wait_ge(x_in[c], i * 16 + 16)
                            pe.wait_ge(copied[slot], i * (quads // SLOTS) + q // SLOTS + FREE)
                            for n in range(4):
                                last = nc.tensor.transpose(tp[slot][:, n, :], xt[c][:, s, 1 + r + n, :], ident)
                            last.then_inc(transposed, 1)

                        def multiply(q):
                            c, s, r = q // QUADS, q % QUADS // (QUADS // 2), q % (QUADS // 2) * 4
                            slot = q % SLOTS
                            if q == 0:
                                pe.wait_ge(freq_read, i * S + FREE)
                            pe.wait_ge(copied[slot], i * (quads // SLOTS) + q // SLOTS + 1 + FREE)
                            for n in range(4):
                                row = c * ROWS1 + r + n
                                last = nc.tensor.matmul(freq_ps[s][:, 0:UV], xT[slot][:, n, :], p_sb[:, row, :],
                                                        start=row == 0, stop=row == H - 1)
                            last.then_inc(multiplied[slot], 1)

                        for q in range(quads + 2):
                            if q < quads:
                                transpose(q)
                                if q % QUADS == QUADS - 1:
                                    pe.wait_ge(transposed, i * quads + q + 1)
                                    pe.sem_inc(pe_read[q // QUADS], 1)
                            if q >= 2:
                                multiply(q - 2)
                        pe.wait_ge(multiplied[(quads - 1) % SLOTS], (i + 1) * (quads // SLOTS) + FREE)
                        pe.sem_inc(freq_done, 1)


def cluster_pass(nc, cst, xd, ohn, oh_t):
    with Scope(nc, "cluster") as sc:
        xx = sc.sb("xx", [P, T, POS])
        xsT = sc.sb("xsT", [P, NT, T, P])
        gram = sc.sb("gram", [P, T, T * P])
        square = sc.sb("square", [P, POS])
        hi, lo, den, inv = (sc.sb(n, [P, T]) for n in ("hi", "lo", "den", "inv"))
        x2 = sc.sb("x2", [P, T])
        wt = sc.sb("wt", [P, T, K])
        prod, dist, near, score, oh = (sc.sb(n, [P, T, K]) for n in ("prod", "dist", "near", "score", "oh"))
        low, best = sc.sb("low", [P, T]), sc.sb("best", [P, T])
        count, rc, empty = sc.sb("count", [P, K]), sc.sb("rc", [P, K]), sc.sb("empty", [P, K])
        rep = sc.sb("rep", [P, T, B * 2, K])
        tp = [sc.ps(f"tp{i}", [P, 4, P]) for i in range(2)]
        gram_ps = [sc.ps(f"gram{t}", [P, 512]) for t in range(T)]
        dot_ps = sc.ps("dot", [P, 512])
        c2_ps = sc.ps("c2", [P, 512])
        cnt_ps = sc.ps("cnt", [P, 512])
        data_in = [sc.sem(f"data_in{t}") for t in range(T)]
        normal, squared, transposed, copied = (
            sc.sem(n) for n in ("normal", "squared", "transposed", "copied"))
        gram_made, gram_copied = sc.sem("gram_made"), sc.sem("gram_copied")
        dots, prods, c2s, labelled, counted, moved, chain_sem = (
            sc.sem(n) for n in ("dots", "prods", "c2s", "labelled", "counted", "moved", "chain"))
        replicated, rep_t, rep_copied = sc.sem("replicated"), sc.sem("rep_t"), sc.sem("rep_copied")
        ident, ones = cst[:, CONST_AT["ident"]], cst[:, CONST_AT["ones"]]
        groups = NT // 2

        with nc.Block() as block:
            @block.sync
            def _(sp):
                for t in range(T):
                    sp.dma_start(xx[:, t, :], xd[0, t, :, :]).then_inc(data_in[t], 16)

            @block.vector
            def _(dve):
                ch = Chain(dve, chain_sem)
                for t in range(T):
                    dve.wait_ge(data_in[t], 16)
                    ch.link(nc.vector.tensor_reduce(hi[:, t:t + 1], xx[:, t, :], AX.X, ALU.max))
                    ch.link(nc.vector.tensor_reduce(lo[:, t:t + 1], xx[:, t, :], AX.X, ALU.min))
                ch.link(nc.vector.tensor_tensor(den[:, :], hi[:, :], lo[:, :], ALU.subtract))
                ch.link(nc.vector.tensor_scalar(den[:, :], den[:, :], 1e-12, None, ALU.max))
                ch.link(nc.vector.reciprocal(inv[:, :], den[:, :]))
                for t in range(T):
                    nc.vector.tensor_scalar(xx[:, t, :], xx[:, t, :], lo[:, t:t + 1], inv[:, t:t + 1],
                                            ALU.subtract, ALU.mult).then_inc(normal, 1)
                nc.vector.tensor_copy(wt[:, :, :].rearrange("p t k -> p (t k)"),
                                      cst[:, CONST_AT["pick0"]]).then_inc(moved, 1)
                dve.wait_ge(moved, 1)
                dve.wait_ge(squared, T)
                first = ch.n
                per = 13
                with dve.Fori(0, ITERS + 1) as i:
                    ch = Chain(dve, chain_sem, i * per + first)
                    dve.wait_ge(dots, i + 1)
                    dv = dot_ps[:, 0:T * K].rearrange("p (t k) -> p t k", t=T)
                    nc.vector.tensor_tensor(prod[:, :, :], wt[:, :, :], dv, ALU.mult).then_inc(prods, 1)
                    for t in range(T):
                        ch.link(nc.vector.tensor_scalar(dist[:, t, :], dv[:, t, :], -2.0, x2[:, t:t + 1],
                                                        ALU.mult, ALU.add))
                    dve.wait_ge(c2s, i + 1)
                    ch.link(nc.vector.tensor_tensor(dist[:, :, :], dist[:, :, :],
                                                    c2_ps[:, 0:K].unsqueeze(1).broadcast_to([P, T, K]), ALU.add))
                    ch.link(nc.vector.tensor_reduce(low[:, :], dist[:, :, :], AX.X, ALU.min))
                    ch.link(nc.vector.tensor_tensor(near[:, :, :], dist[:, :, :],
                                                    low[:, :].unsqueeze(2).broadcast_to([P, T, K]), ALU.is_le))
                    ch.link(nc.vector.tensor_tensor(
                        score[:, :, :], near[:, :, :],
                        cst[:, CONST_AT["tie"]].unsqueeze(1).broadcast_to([P, T, K]), ALU.mult))
                    ch.link(nc.vector.tensor_reduce(best[:, :], score[:, :, :], AX.X, ALU.max))
                    nc.vector.tensor_tensor(oh[:, :, :], score[:, :, :],
                                            best[:, :].unsqueeze(2).broadcast_to([P, T, K]),
                                            ALU.is_equal).then_inc(labelled, 1)
                    dve.wait_ge(labelled, i + 1)
                    dve.wait_ge(counted, i + 1)
                    ch.link(nc.vector.tensor_scalar(count[:, :], cnt_ps[:, 0:K], 1.0, None, ALU.max))
                    ch.link(nc.vector.reciprocal(rc[:, :], count[:, :]))
                    ch.link(nc.vector.tensor_scalar(empty[:, :], cnt_ps[:, 0:K], 0.0, None, ALU.is_equal))
                    ch.link(nc.vector.tensor_tensor(ohn[:, :, :], oh[:, :, :],
                                                    rc[:, :].unsqueeze(1).broadcast_to([P, T, K]), ALU.mult))
                    ch.link(nc.vector.tensor_tensor(wt[:, :, :], wt[:, :, :],
                                                    empty[:, :].unsqueeze(1).broadcast_to([P, T, K]), ALU.mult))
                    ch.link(nc.vector.tensor_tensor(wt[:, :, :], wt[:, :, :], ohn[:, :, :], ALU.add))
                    dve.sem_inc(moved, 1)
                for t in range(T):
                    nc.vector.tensor_copy(rep[:, t, :, :], oh[:, t, :].unsqueeze(1).broadcast_to([P, B * 2, K])
                                          ).then_inc(replicated, 1)

            @block.scalar
            def _(act):
                for t in range(T):
                    act.wait_ge(normal, t + 1)
                    if t:
                        act.wait_ge(squared, t)
                    nc.scalar.activation(square[:, :], xx[:, t, :], ACT.Square,
                                         accum_out=x2[:, t:t + 1]).then_inc(squared, 1)
                for n in range(groups):
                    act.wait_ge(transposed, n + 1)
                    nc.scalar.activation(xsT[:, 2 * n:2 * n + 2, :, :].rearrange("p a t g -> p (a t) g"),
                                         tp[n % 2][:, :, :], ACT.Copy).then_inc(copied, 1)
                for t in range(T):
                    act.wait_ge(gram_made, t + 1)
                    nc.scalar.activation(gram[:, t, :], gram_ps[t][:, 0:T * P], ACT.Copy).then_inc(gram_copied, 1)
                for t in range(T):
                    act.wait_ge(rep_t, t + 1)
                    nc.scalar.activation(oh_t[:, t, :], tp[t][:, 0, :], ACT.Copy).then_inc(rep_copied, 1)
                act.wait_ge(rep_copied, T)

            @block.tensor
            def _(pe):
                pe.wait_ge(normal, T)
                for n in range(groups):
                    if n >= 2:
                        pe.wait_ge(copied, n - 1)
                    for a in range(2):
                        for t in range(T):
                            at = (2 * n + a) * P
                            last = nc.tensor.transpose(tp[n % 2][:, 2 * a + t, :], xx[:, t, at:at + P], ident)
                    last.then_inc(transposed, 1)
                pe.wait_ge(copied, groups)
                for t in range(T):
                    for n in range(NT):
                        last = nc.tensor.matmul(gram_ps[t][:, 0:T * P], xsT[:, n, t, :],
                                                xsT[:, n, :, :].rearrange("p t g -> p (t g)"),
                                                start=n == 0, stop=n == NT - 1)
                    last.then_inc(gram_made, 1)
                pe.wait_ge(gram_copied, T)
                with pe.Fori(0, ITERS + 1) as i:
                    pe.wait_ge(moved, i + 1)
                    for t in range(T):
                        for t2 in range(T):
                            last = nc.tensor.matmul(dot_ps[:, t * K:(t + 1) * K], gram[:, t2, t * P:(t + 1) * P],
                                                    wt[:, t2, :], start=t2 == 0, stop=t2 == T - 1)
                    last.then_inc(dots, 1)
                    pe.wait_ge(prods, i + 1)
                    for t in range(T):
                        last = nc.tensor.matmul(c2_ps[:, 0:K], ones, prod[:, t, :], start=t == 0, stop=t == T - 1)
                    last.then_inc(c2s, 1)
                    pe.wait_ge(labelled, i + 1)
                    for t in range(T):
                        last = nc.tensor.matmul(cnt_ps[:, 0:K], ones, oh[:, t, :], start=t == 0, stop=t == T - 1)
                    last.then_inc(counted, 1)
                for t in range(T):
                    pe.wait_ge(replicated, t + 1)
                    nc.tensor.transpose(tp[t][:, 0, :], rep[:, t, :, :].rearrange("p a k -> p (a k)"),
                                        ident).then_inc(rep_t, 1)


MEAN_CHUNKS = POS // 512
MEAN_LEAD = MEAN_CHUNKS + 1


def average_pass(nc, cst, q_cols, xd, ohn, ft, xpu):
    with Scope(nc, "average") as sc:
        q_sb = sc.sb("q", [P, NT, UV])
        dbuf = [[sc.sb(f"xd{a}_{t}", [P, POS]) for t in range(T)] for a in range(2)]
        dT = [sc.sb(f"dT{i}", [P, 4, P]) for i in range(SLOTS)]
        placed = [sc.sb(f"placed{a}", [P, T, 2 * B, K]) for a in range(2)]
        tp = [sc.ps(f"tp{i}", [P, 4, P]) for i in range(SLOTS)]
        mean_ps = [sc.ps(f"mean{a}", [P, 512]) for a in range(2)]
        freq_ps = [sc.ps(f"freq{a}", [P, T, UV]) for a in range(2)]
        const_in = sc.sem("const_in")
        d_in = [[sc.sem(f"d_in{a}_{t}") for t in range(T)] for a in range(2)]
        transposed, cleared, placed_made, mean_made = (sc.sem(n) for n in (
            "transposed", "cleared", "placed_made", "mean_made"))
        mean_taken, freq_read = ([sc.sem(f"{n}{a}") for a in range(2)] for n in ("mean_taken", "freq_read"))
        copied = [sc.sem(f"copied{i}") for i in range(SLOTS)]
        multiplied = [sc.sem(f"multiplied{i}") for i in range(SLOTS)]
        ident = cst[:, CONST_AT["ident"]]
        per = NT // 4
        quads = T * per
        turns = quads // SLOTS
        chunk_turns = MEAN_CHUNKS // 2
        flat = ft[:, :, :].rearrange("p n k -> p (n k)")

        with nc.Block() as block:
            @block.sync
            def _(sp):
                sp.dma_start(q_sb[:, :, :], q_cols.rearrange("p (n k) -> p n k", k=UV)).then_inc(const_in, 16)
                with sp.Fori(0, B // 2) as h:
                    for a in range(2):
                        sp.wait_ge(mean_made, (h * 2 + a) * MEAN_CHUNKS + MEAN_LEAD - MEAN_CHUNKS)
                        for t in range(T):
                            sp.dma_start(dbuf[a][t][:, :], xd[h * 2 + a, t, :, :]).then_inc(d_in[a][t], 16)

            @block.tensor
            def _(pe):
                start_free(pe, multiplied)
                pe.sem_inc(mean_made, MEAN_LEAD)
                pe.wait_ge(const_in, 16)
                with pe.Fori(0, B // 2) as h:
                    for a in range(2):
                        b = h * 2 + a
                        d = dbuf[a]

                        def transpose(q):
                            t, n0, slot = q // per, q % per * 4, q % SLOTS
                            if q % per == 0:
                                pe.wait_ge(d_in[a][t], h * 16 + 16)
                            pe.wait_ge(copied[slot], b * turns + q // SLOTS + FREE)
                            for n in range(4):
                                last = nc.tensor.transpose(tp[slot][:, n, :], d[t][:, (n0 + n) * P:(n0 + n + 1) * P],
                                                           ident)
                            last.then_inc(transposed, 1)

                        def multiply(q):
                            t, n0, slot = q // per, q % per * 4, q % SLOTS
                            if q == 0:
                                pe.wait_ge(freq_read[a], h + FREE)
                            pe.wait_ge(copied[slot], b * turns + q // SLOTS + 1 + FREE)
                            for n in range(4):
                                last = nc.tensor.matmul(freq_ps[a][:, t, :], dT[slot][:, n, :], q_sb[:, n0 + n, :],
                                                        start=n0 + n == 0, stop=n0 + n == NT - 1)
                            last.then_inc(multiplied[slot], 1)

                        def average(r):
                            if r == 0:
                                pe.wait_ge(placed_made, b + 1)
                            pe.wait_ge(mean_taken[r % 2], b * chunk_turns + r // 2 + FREE)
                            for t in range(T):
                                last = nc.tensor.matmul(mean_ps[r % 2][:, :],
                                                        placed[a][:, t, :, :].rearrange("p b k -> p (b k)"),
                                                        d[t][:, r * 512:(r + 1) * 512], start=t == 0, stop=t == T - 1)
                            last.then_inc(mean_made, 1)

                        for q in range(quads + 2):
                            if q < quads:
                                transpose(q)
                            if q >= 2:
                                multiply(q - 2)
                            if q >= quads + 2 - MEAN_CHUNKS:
                                average(q - (quads + 2 - MEAN_CHUNKS))

            @block.scalar
            def _(act):
                start_free(act, [*freq_read, *copied])
                with act.Fori(0, B // 2) as h:
                    for a in range(2):
                        b = h * 2 + a
                        for q in range(quads):
                            slot = q % SLOTS
                            act.wait_ge(transposed, b * quads + q + 1)
                            act.wait_ge(multiplied[slot], b * turns + q // SLOTS + FREE)
                            nc.scalar.activation(dT[slot][:, :, :], tp[slot][:, :, :], ACT.Copy
                                                 ).then_inc(copied[slot], 1)
                        act.wait_ge(multiplied[SLOTS - 1], b * turns + turns + FREE)
                        nc.scalar.activation(xpu[:, :, :].rearrange("p (b t) k -> p b t k", t=T)[:, b, :, :],
                                             freq_ps[a][:, :, :], ACT.Copy).then_inc(freq_read[a], 1)

            @block.vector
            def _(dve):
                nc.vector.memset(flat, 0.0).then_inc(cleared, 1)
                start_free(dve, mean_taken)
                dve.wait_ge(cleared, 1)
                own = cst[:, CONST_AT["own_rows"]].rearrange("p (b c) -> p b c", b=B)
                with dve.Fori(0, B // 2) as h:
                    for a in range(2):
                        b = h * 2 + a
                        dve.wait_ge(mean_made, b * MEAN_CHUNKS + MEAN_LEAD - MEAN_CHUNKS)
                        nc.vector.tensor_tensor(placed[a][:, :, :, :],
                                                ohn[:, :, :].unsqueeze(2).broadcast_to([P, T, 2 * B, K]),
                                                own[:, b, :].unsqueeze(1).unsqueeze(3).broadcast_to([P, T, 2 * B, K]),
                                                ALU.mult).then_inc(placed_made, 1)
                        for r in range(MEAN_CHUNKS):
                            dve.wait_ge(mean_made, b * MEAN_CHUNKS + r + 1 + MEAN_LEAD)
                            cols = slice(r * 512, (r + 1) * 512)
                            nc.vector.tensor_tensor(flat[:, cols], flat[:, cols], mean_ps[r % 2][:, :], ALU.add
                                                    ).then_inc(mean_taken[r % 2], 1)


def mixture_pass(nc, cst, w_conv, w_up, ft, feat, oh_t, xps, xpu, coef):
    with Scope(nc, "mix") as sc:
        wc = sc.sb("wc", [K, N])
        wu = sc.sb("wu", [P, T, S])
        part = sc.sb("part", [P, UV])
        lift = [sc.sb(f"lift{i}", [P, 4, P]) for i in range(2)]
        diag = sc.sb("diag", [P, P])
        mean_c, square_c, var_c = (sc.sb(n, [P, 1]) for n in ("mean_c", "square_c", "var_c"))
        order, less, rank = sc.sb("order", [P, K, K]), sc.sb("less", [P, K, K]), sc.sb("rank", [P, K])
        var0 = sc.sb("var0", [P, K])
        ranked = sc.sb("ranked", [K, B * 2, K])
        wp = sc.sb("wp", [P, N])
        ms, mu, mu2, var, iv, quad, lnv, w1, w2, wmat, term, lnw, wb, cs, rs, rn = (
            sc.sb(n, [P, BN]) for n in ("ms", "mu", "mu2", "var", "iv", "quad", "lnv", "w1", "w2", "wmat", "term",
                                        "lnw", "wb", "cs", "rs", "rn"))
        logit, resp = sc.sb("logit", [P, NT, BN]), sc.sb("resp", [P, NT, BN])
        top, tot, inv = (sc.sb(n, [P, NT, B]) for n in ("top", "tot", "inv"))
        mud, vard, muc = sc.sb("mud", [P, N]), sc.sb("vard", [P, N]), sc.sb("muc", [P, N])
        c0, c1, box0, box1, ya, yb, ye, y = (sc.sb(n, [P, 1]) for n in ("c0", "c1", "box0", "box1", "ya", "yb",
                                                                      "ye", "y"))
        low = sc.sb("low", [P, B * T, UV])
        ymat, one_gate = sc.sb("ymat", [P, B]), sc.sb("one_gate", [P, T, B])
        tp = [sc.ps(f"tp{i}", [P, 4, P]) for i in range(2)]
        a_ps, b_ps, l_ps, m_ps, n_ps, c_ps = (sc.ps(n, [P, 512]) for n in ("a", "b", "l", "m", "n", "c"))
        const_in, chain_sem = sc.sem("const_in"), sc.sem("chain")
        squared, spread_sum, spread_made, order_made, picked = (
            sc.sem(n) for n in ("squared", "spread_sum", "spread_made", "order_made", "picked"))
        transposed, copied, means, params, weights, logs, logged, terms, scores, shifted, exped, resps, moments, \
            masses, ready = (sc.sem(n) for n in ("transposed", "copied", "means", "params", "weights", "logs",
                                                 "logged", "terms", "scores", "shifted", "exped", "resps",
                                                 "moments", "masses", "ready"))
        gated, sig, sig_in = sc.sem("gated"), sc.sem("sig"), sc.sem("sig_in")
        y_made, act_chain = sc.sem("y_made"), sc.sem("act_chain")

        def k(name):
            return cst[:, CONST_AT[name]]

        groups = NT // 4

        with nc.Block() as block:
            @block.sync
            def _(sp):
                sp.dma_start(wc[:, :], w_conv).then_inc(const_in, 16)
                sp.dma_start(wu[:, :, :], w_up.rearrange("(t g s) -> g t s", t=T, s=S)).then_inc(const_in, 16)

            def parameters(pe, i):
                pe.wait_ge(ready, i + 1)
                nc.tensor.matmul(a_ps[:, 0:BN], k("sel_mu"), ms[:, :], start=True, stop=True)
                nc.tensor.matmul(b_ps[:, 0:BN], k("sel_ex"), ms[:, :], start=True, stop=True).then_inc(means, 1)

            def dve_parameters(dve, ch, i):
                dve.wait_ge(means, i + 1)
                ch.link(nc.vector.tensor_copy(mu[:, :], a_ps[:, 0:BN]))
                ch.link(nc.vector.tensor_tensor(mu2[:, :], mu[:, :], mu[:, :], ALU.mult))
                ch.link(nc.vector.tensor_tensor(var[:, :], b_ps[:, 0:BN], mu2[:, :], ALU.subtract))
                ch.link(nc.vector.tensor_scalar(var[:, :], var[:, :], EPS, EPS, ALU.add, ALU.max))

            @block.tensor
            def _(pe):
                pe.wait_ge(const_in, 32)
                for n in range(groups):
                    pe.wait_ge(squared, n + 1)
                    if n >= 2:
                        pe.wait_ge(copied, n - 1)
                    for j in range(4):
                        last = nc.tensor.transpose(tp[n % 2][:, j, :], ft[:, 4 * n + j, :], k("ident"))
                    last.then_inc(transposed, 1)
                pe.wait_ge(spread_sum, 1)
                nc.tensor.matmul(m_ps[:, 0:P], k("ones"), diag[:, :], start=True, stop=True).then_inc(spread_made, 1)
                pe.wait_ge(order_made, 1)
                nc.tensor.matmul(c_ps[:, 0:N], ranked[:, :, :].rearrange("r a k -> r (a k)"), wc[:, :],
                                 start=True, stop=True).then_inc(picked, 1)
                with pe.Fori(0, ITERS) as i:
                    parameters(pe, i)
                    pe.wait_ge(terms, i + 1)
                    nc.tensor.matmul(c_ps[:, 0:BN], k("ones"), term[:, :], start=True, stop=True).then_inc(logs, 1)
                    pe.wait_ge(weights, i + 1)
                    for n in range(NT):
                        last = nc.tensor.matmul(l_ps[:, n * BN:(n + 1) * BN], ft[:, n, :], wmat[:, :],
                                                start=True, stop=True)
                    last.then_inc(scores, 1)
                    pe.wait_ge(resps, i + 1)
                    nc.tensor.matmul(n_ps[:, 0:BN], k("ones"), rs[:, :], start=True, stop=True).then_inc(masses, 1)
                    for n in range(NT):
                        last = nc.tensor.matmul(m_ps[:, 0:BN], feat[:, n, :], resp[:, n, :],
                                                start=n == 0, stop=n == NT - 1)
                    last.then_inc(moments, 1)
                parameters(pe, ITERS)
                pe.wait_ge(y_made, 1)
                for t in range(T):
                    last = nc.tensor.matmul(l_ps[:, t * B:(t + 1) * B], oh_t[:, t, :], ymat[:, :],
                                            start=True, stop=True)
                last.then_inc(gated, 1)

            @block.scalar
            def _(act):
                for n in range(groups):
                    act.wait_ge(transposed, n + 1)
                    nc.scalar.activation(feat[:, 4 * n:4 * n + 4, :], tp[n % 2][:, :, :], ACT.Copy
                                         ).then_inc(copied, 1)
                with act.Fori(0, ITERS) as i:
                    act.wait_ge(params, i + 1)
                    nc.scalar.activation(lnv[:, :], var[:, :], ACT.Ln).then_inc(act_chain, 1)
                    nc.scalar.activation(lnw[:, :], wb[:, :], ACT.Ln).then_inc(logged, 1)
                    act.wait_ge(shifted, i + 1)
                    nc.scalar.activation(logit[:, :, :], logit[:, :, :], ACT.Exp).then_inc(exped, 1)
                act.wait_ge(sig_in, 1)
                nc.scalar.activation(ye[:, :], yb[:, :], ACT.Exp, scale=-1.0).then_inc(sig, 1)

            @block.vector
            def _(dve):
                ch = Chain(dve, chain_sem)
                dve.wait_ge(const_in, 32)

                def row_sum(out):
                    ch.link(nc.vector.tensor_reduce(
                        part[:, :], ft[:, :, :].rearrange("p n (a c) -> p (n a) c", a=2), AX.X, ALU.add))
                    ch.link(nc.vector.tensor_reduce(out, part[:, :], AX.X, ALU.add))

                row_sum(mean_c[:, :])
                ch.link(nc.vector.tensor_scalar(mean_c[:, :], mean_c[:, :], 1.0 / POS, None, ALU.mult))
                ch.link(nc.vector.tensor_scalar(ft[:, :, :], ft[:, :, :], mean_c[:, 0:1], None, ALU.subtract))
                for n in range(groups):
                    rows = ft[:, 4 * n:4 * n + 4, :]
                    ch.link(nc.vector.tensor_scalar(lift[n % 2][:, :, :], rows, k("is_x2"), k("is_x"),
                                                    ALU.mult, ALU.add))
                    nc.vector.tensor_tensor(rows, rows, lift[n % 2][:, :, :], ALU.mult).then_inc(squared, 1)
                dve.wait_ge(squared, groups)
                row_sum(square_c[:, :])
                ch.link(nc.vector.tensor_scalar(diag[:, :], k("ident"), square_c[:, 0:1], None, ALU.mult))
                dve.sem_inc(spread_sum, 1)
                ch.link(nc.vector.tensor_scalar(var_c[:, :], k("is_x2"), square_c[:, 0:1], 1.0 / POS,
                                                ALU.mult, ALU.mult))
                dve.wait_ge(spread_made, 1)
                mv = m_ps[:, 0:P].rearrange("p (b f k) -> p b f k", b=B, f=2)
                ch.link(nc.vector.tensor_copy(var0[:, :], mv[:, 0, 1, :]))
                mine = var0[:, :].unsqueeze(2).broadcast_to([P, K, K])
                other = var0[:, :].unsqueeze(1).broadcast_to([P, K, K])
                ch.link(nc.vector.tensor_tensor(less[:, :, :], other, mine, ALU.is_lt))
                ch.link(nc.vector.tensor_tensor(order[:, :, :], other, mine, ALU.is_equal))
                ch.link(nc.vector.tensor_tensor(order[:, :, :], order[:, :, :],
                                                k("before").rearrange("p (a c) -> p a c", a=K), ALU.mult))
                ch.link(nc.vector.tensor_tensor(less[:, :, :], less[:, :, :], order[:, :, :], ALU.add))
                ch.link(nc.vector.tensor_reduce(rank[:, :], less[:, :, :], AX.X, ALU.add))
                ch.link(nc.vector.tensor_scalar(ranked[:, :, :],
                                                rank[0:K, :].unsqueeze(1).broadcast_to([K, B * 2, K]),
                                                cst[0:K, CONST_AT["rank"]], None, ALU.is_equal))
                dve.sem_inc(order_made, 1)
                dve.wait_ge(picked, 1)
                ch.link(nc.vector.tensor_copy(wp[:, :], c_ps[:, 0:N]))
                msv = ms[:, :].rearrange("p (b n) -> p b n", n=N)
                for n, (tile, pos) in enumerate(((0, 0), (NT - 1, P - 1))):
                    ch.link(nc.vector.tensor_tensor(msv[:, :, n], ft[:, tile, pos:pos + 1].broadcast_to([P, B]),
                                                    var_c[:, 0:1].broadcast_to([P, B]), ALU.add))
                ch.link(nc.vector.memset(wb[:, :], 1.0 / N))
                dve.sem_inc(ready, 1)
                first = ch.n
                lv = logit[:, :, :].rearrange("p n (b c) -> p n b c", c=N)
                per = 23
                with dve.Fori(0, ITERS) as i:
                    ch = Chain(dve, chain_sem, i * per + first)
                    dve_parameters(dve, ch, i)
                    dve.sem_inc(params, 1)
                    ch.link(nc.vector.reciprocal(iv[:, :], var[:, :]))
                    ch.link(nc.vector.tensor_tensor(w1[:, :], mu[:, :], iv[:, :], ALU.mult))
                    ch.link(nc.vector.tensor_tensor(w2[:, :], iv[:, :], k("mask_x2"), ALU.mult))
                    ch.link(nc.vector.tensor_tensor(wmat[:, :], w1[:, :], k("mask_x"), ALU.mult))
                    ch.link(nc.vector.tensor_tensor(wmat[:, :], wmat[:, :], w2[:, :], ALU.add))
                    dve.sem_inc(weights, 1)
                    ch.link(nc.vector.tensor_tensor(quad[:, :], mu2[:, :], iv[:, :], ALU.mult))
                    dve.wait_ge(act_chain, i + 1)
                    ch.link(nc.vector.tensor_tensor(quad[:, :], quad[:, :], lnv[:, :], ALU.add))
                    ch.link(nc.vector.tensor_tensor(term[:, :], quad[:, :], k("mask_term"), ALU.mult))
                    dve.sem_inc(terms, 1)
                    dve.wait_ge(logs, i + 1)
                    dve.wait_ge(logged, i + 1)
                    ch.link(nc.vector.scalar_tensor_tensor(out=cs[:, :], in0=lnw[:, :], scalar=-0.5 * K * LOG2PI,
                                                           in1=c_ps[:, 0:BN], op0=ALU.add, op1=ALU.add))
                    dve.wait_ge(scores, i + 1)
                    ch.link(nc.vector.tensor_tensor(logit[:, :, :],
                                                    l_ps[:, :].rearrange("p (n c) -> p n c", c=BN),
                                                    cs[:, :].unsqueeze(1).broadcast_to([P, NT, BN]), ALU.add))
                    ch.link(nc.vector.tensor_tensor(top[:, :, :], lv[:, :, :, 0], lv[:, :, :, 1], ALU.max))
                    ch.link(nc.vector.tensor_tensor(lv, lv, top[:, :, :].unsqueeze(3).broadcast_to([P, NT, B, N]),
                                                    ALU.subtract))
                    dve.sem_inc(shifted, 1)
                    dve.wait_ge(exped, i + 1)
                    ch.link(nc.vector.tensor_tensor(tot[:, :, :], lv[:, :, :, 0], lv[:, :, :, 1], ALU.add))
                    ch.link(nc.vector.reciprocal(inv[:, :, :], tot[:, :, :]))
                    ch.link(nc.vector.tensor_tensor(
                        resp[:, :, :].rearrange("p n (b c) -> p n b c", c=N), lv,
                        inv[:, :, :].unsqueeze(3).broadcast_to([P, NT, B, N]), ALU.mult))
                    ch.link(nc.vector.tensor_reduce(rs[:, :], resp[:, :, :].rearrange("p n c -> p c n"),
                                                    AX.X, ALU.add))
                    dve.sem_inc(resps, 1)
                    dve.wait_ge(masses, i + 1)
                    ch.link(nc.vector.reciprocal(rn[:, :], n_ps[:, 0:BN]))
                    ch.link(nc.vector.tensor_scalar(wb[:, :], n_ps[:, 0:BN], 1.0 / POS, None, ALU.mult))
                    dve.wait_ge(moments, i + 1)
                    ch.link(nc.vector.tensor_tensor(ms[:, :], m_ps[:, 0:BN], rn[:, :], ALU.mult))
                    assert isinstance(per, int)
                    dve.sem_inc(ready, 1)
                ch = Chain(dve, chain_sem, ITERS * per + first)
                dve_parameters(dve, ch, ITERS)
                for src, dst in ((mu, mud), (var, vard)):
                    ch.link(nc.vector.tensor_tensor(w1[:, :], src[:, :], k("block"), ALU.mult))
                    ch.link(nc.vector.tensor_reduce(dst[:, :], w1[:, :].rearrange("p (b n) -> p n b", n=N),
                                                    AX.X, ALU.add))
                ch.link(nc.vector.tensor_scalar(muc[:, :], mud[:, :], mean_c[:, 0:1], None, ALU.add))
                ch.link(nc.vector.tensor_tensor(c0[:, :], vard[:, 0:1], vard[:, 1:2], ALU.is_le))
                ch.link(nc.vector.tensor_scalar(c1[:, :], c0[:, :], -1.0, 1.0, ALU.mult, ALU.add))
                for box, a, b in ((box0, c0, c1), (box1, c1, c0)):
                    ch.link(nc.vector.tensor_tensor(ya[:, :], muc[:, 0:1], a[:, :], ALU.mult))
                    ch.link(nc.vector.tensor_tensor(yb[:, :], muc[:, 1:2], b[:, :], ALU.mult))
                    ch.link(nc.vector.tensor_tensor(box[:, :], ya[:, :], yb[:, :], ALU.add))
                ch.link(nc.vector.tensor_tensor(ya[:, :], box0[:, :], wp[:, 0:1], ALU.mult))
                ch.link(nc.vector.tensor_tensor(yb[:, :], box1[:, :], wp[:, 1:2], ALU.mult))
                ch.link(nc.vector.tensor_tensor(yb[:, :], ya[:, :], yb[:, :], ALU.add))
                dve.sem_inc(sig_in, 1)
                dve.wait_ge(sig, 1)
                ch.link(nc.vector.tensor_scalar(ye[:, :], ye[:, :], 1.0, None, ALU.add))
                ch.link(nc.vector.reciprocal(y[:, :], ye[:, :]))
                ch.link(nc.vector.tensor_scalar(ymat[:, :], k("block_k"), y[:, 0:1], None, ALU.mult))
                dve.sem_inc(y_made, 1)
                dve.wait_ge(gated, 1)
                ch.link(nc.vector.tensor_scalar(one_gate[:, :, :].rearrange("p t b -> p (t b)"), l_ps[:, 0:T * B],
                                                1.0, None, ALU.add))
                for t in range(T):
                    ch.link(nc.vector.tensor_tensor(
                        coef[:, :, t, :], one_gate[:, t, :].unsqueeze(2).broadcast_to([P, B, S]),
                        wu[:, t, :].unsqueeze(1).broadcast_to([P, B, S]), ALU.mult))
                cv = coef[:, :, :, :].rearrange("p b t s -> p (b t) s")
                for s in range(S):
                    ch.link(nc.vector.tensor_tensor(low[:, :, :], xpu[:, :, :],
                                                    cv[:, :, s].unsqueeze(2).broadcast_to([P, B * T, UV]), ALU.mult))
                    ch.link(nc.vector.tensor_tensor(xps[:, :, s, :], xps[:, :, s, :], low[:, :, :], ALU.add))


ROWS2 = 8
CH2 = H // ROWS2
DROWS = ROWS2 // 2
HALO = DROWS + 2
HALF = ROWS2 // 2
UNITS = H // HALF
PAIRS = HALF // 2
FILLS = PAIRS + 1
BANKS = TS
XBUF = 8
AHEAD = XBUF - 2
PIECES = 16
PKBUF = 4
SET_UP = 5

CHUNK_LEAD = 2
FILL_LEAD = 2 * FILLS + 1
UNIT_LEAD = BANKS + 1
Y_LEAD = 16


def second_pass(nc, x, cst, p_sb, r_cols, inter_cols, wqk, wv, bias, gamma, xd, xps, coef, out):
    xv = x.rearrange("b (t g s) h w -> b t g s (h w)", t=T, s=S)
    ov = out.rearrange("b (t g s) h w -> b t g s (h w)", t=T, s=S)
    with Scope(nc, "second") as sc:
        inter = sc.sb("inter", [P, W + 4 * HD])
        r_sb = sc.sb("r", [UV, H * LOW])
        wqk_sb, wv_sb = sc.sb("wqk", [P, TS, P]), sc.sb("wv", [P, TS, C])
        gam = sc.sb("gam", [P, 1])
        xt = [sc.sb(f"x{i}", [P, T, S, HALF, W]) for i in range(XBUF)]
        dd = [sc.sb(f"dd{i}", [P, T, HALO, WD]) for i in range(2)]
        mid = [sc.sb(f"mid{i}", [P, T, ROWS2, WD]) for i in range(2)]
        part = sc.sb("part", [P, T, ROWS2, WD])
        scaled_rows = [sc.sb(f"scaled{i}", [P, T, S, ROWS2, WD]) for i in range(2)]
        zt = [sc.sb(f"zt{i}", [P, ROWS2, UV]) for i in range(2)]
        left = [sc.sb(f"left{i}", [P, HALF, TS, P]) for i in range(2)]
        right = [sc.sb(f"right{i}", [P, HALF, W]) for i in range(2)]
        xp = sc.sb("xp", [P, TS, UV])
        qk = sc.sb("qk", [UV, 2, UV])
        vx = sc.sb("vx", [UV + 1, C])
        grams = sc.sb("grams", [UV, 4, UV])
        work, m1 = sc.sb("work", [P, H // 2, LOW]), sc.sb("m1", [UV, H // 2, LOW])
        lam2, lam = sc.sb("lam2", [P, 2, H]), sc.sb("lam", [P, 2, H])
        rk, den, rr = sc.sb("rk", [P, H]), sc.sb("den", [P, H]), sc.sb("rr", [P, H])
        pk = [sc.sb(f"pk{i}", [P, H // PIECES, UV]) for i in range(PKBUF)]
        a_sb, a_free, mx = sc.sb("a", [UV, UV]), sc.sb("a_free", [UV, UV]), sc.sb("mx", [UV, P])
        ms = sc.sb("ms", [UV, H])
        vt = sc.sb("vt", [P, C])
        gain, shift = sc.sb("gain", [P, TS]), sc.sb("shift", [P, TS])
        ob = [sc.ps(f"o{i}", [P, HALF, W]) for i in range(BANKS)]
        tp = [sc.ps(f"tp{i}", [P, 4, P]) for i in range(2)]
        st = sc.ps("st", [P, 1024])

        const_in = sc.sem("const_in")
        x_in = [sc.sem(f"x_in{i}") for i in range(XBUF)]
        y_out = [sc.sem(f"y_out{i}") for i in range(XBUF)]
        dd_in = [sc.sem(f"dd_in{i}") for i in range(2)]
        set_up, weighted, interpolated, scaled = (sc.sem(n) for n in ("set_up", "weighted", "interpolated", "scaled"))
        zt_made, transposed, multiplied = sc.sem("zt_made"), sc.sem("transposed"), sc.sem("multiplied")
        copied = [sc.sem(f"copied{i}") for i in range(2)]
        added = [sc.sem(f"added{i}") for i in range(BANKS)]
        chain_sem = sc.sem("chain")
        (xp_made, qk_made, qk_copied, g_made, g_copied, half_made, half_taken, lam_made, lam2_made, root_made,
         pk_made, pk_used, a_made, a_copied, a_freed, m_made, mx_made, v_made, vt_made, factors_made) = (
            sc.sem(n) for n in (
                "xp_made", "qk_made", "qk_copied", "g_made", "g_copied", "half_made", "half_taken", "lam_made",
                "lam2_made", "root_made", "pk_made", "pk_used", "a_made", "a_copied", "a_freed", "m_made",
                "mx_made", "v_made", "vt_made", "factors_made"))

        def k(name, rows=P):
            return cst[0:rows, CONST_AT[name]]

        half = H * LOW // 2
        rows_pk = H // PIECES
        row_w = inter[:, W:].rearrange("p (k i) -> p k i", k=4)
        hi, lo = slice(UV, P), slice(0, UV)

        def chunk_of(u):
            return u // 2

        def batches(eng, step, prologue=None):
            if prologue:
                prologue()
            with eng.Fori(0, B - 1) as b:
                for u in range(UNITS):
                    step(b, u, True)
            for u in range(UNITS):
                step(B - 1, u, False)

        with nc.Block() as block:
            @block.sync
            def _(sp):
                def load_rows(b, m):
                    slot, n = m % 2, m % CH2
                    sp.wait_ge(weighted, b * CH2 + m + CHUNK_LEAD - 1)
                    batch = b + m // CH2
                    rows = xd[batch].rearrange("t g n -> g t n")
                    first, last = max(n * DROWS - 1, 0), min(n * DROWS + DROWS + 1, HD)
                    at = first - (n * DROWS - 1)
                    if n == 0:
                        sp.dma_start(dd[slot][:, :, 0, :], rows[:, :, 0:WD]).then_inc(dd_in[slot], 16)
                    if n == CH2 - 1:
                        sp.dma_start(dd[slot][:, :, HALO - 1, :], rows[:, :, (HD - 1) * WD:HD * WD]
                                     ).then_inc(dd_in[slot], 16)
                    sp.dma_start(dd[slot][:, :, at:at + last - first, :].rearrange("g t h w -> g t (h w)"),
                                 rows[:, :, first * WD:last * WD]).then_inc(dd_in[slot], 16)

                for dst, src in ((inter[:, :], inter_cols),
                                 (r_sb[:, :], r_cols), (wqk_sb[:, :, :], wqk), (wv_sb[:, :, :], wv),
                                 (vx[UV:UV + 1, :], bias),
                                 (gam[:, :], gamma.rearrange("(a b) -> a b", b=1).broadcast_to([P, 1]))):
                    sp.dma_start(dst, src).then_inc(const_in, 16)

                def load_image(b, u, free=True):
                    i = u % XBUF
                    if free:
                        sp.wait_ge(y_out[i], (b * (UNITS // XBUF) + u // XBUF) * T * 16 + Y_LEAD)
                    for t in range(T):
                        sp.dma_start(xt[i][:, t, :, :, :].rearrange("g s h w -> g s (h w)"),
                                     xv[b + u // UNITS, t, :, :, u % UNITS * HALF * W:(u % UNITS + 1) * HALF * W]
                                     ).then_inc(x_in[i], 16)

                def store(b, u):
                    i = u % XBUF
                    sp.wait_ge(added[BANKS - 1], b * UNITS + u + 1 + FREE)
                    for t in range(T):
                        sp.dma_start(ov[b, t, :, :, u * HALF * W:(u + 1) * HALF * W],
                                     xt[i][:, t, :, :, :].rearrange("g s h w -> g s (h w)")).then_inc(y_out[i], 16)

                def prologue():
                    load_rows(0, 0)
                    load_rows(0, 1)
                    for u in range(AHEAD):
                        load_image(0, u, free=False)
                    load_rows(0, 2)
                    for i in range(XBUF):
                        sp.sem_inc(y_out[i], Y_LEAD)

                def step(b, u, more):
                    if u % 2 == 1 and (more or chunk_of(u) < CH2 - 3):
                        load_rows(b, chunk_of(u) + 3)
                    store(b, u)
                    if more or u + AHEAD < UNITS:
                        load_image(b, u + AHEAD)

                batches(sp, step, prologue)
                for i in range(XBUF):
                    sp.wait_ge(y_out[i], B * UNITS // XBUF * T * 16 + Y_LEAD)

            @block.tensor
            def _(pe):
                pe.wait_ge(const_in, 96)
                pe.wait_ge(set_up, SET_UP)
                pe.sem_inc(transposed, FILL_LEAD)
                pe.sem_inc(multiplied, UNIT_LEAD)

                def qkv(q, first):
                    if not first:
                        pe.wait_ge(vt_made, q)
                        pe.wait_ge(factors_made, q)
                    pe.wait_ge(xp_made, q + 1)
                    for n in range(TS):
                        last = nc.tensor.matmul(st[0:UV, 512:1024], xp[:, n, :], wv_sb[:, n, :],
                                                start=n == 0, stop=n == TS - 1)
                    for j in range(2):
                        for n in range(TS):
                            last = nc.tensor.matmul(st[0:UV, j * UV:(j + 1) * UV], wqk_sb[:, n, j * UV:(j + 1) * UV],
                                                    xp[:, n, :], start=n == 0, stop=n == TS - 1)
                    last.then_inc(qk_made, 1)

                def gram(q):
                    pe.wait_ge(qk_copied, q + 1)
                    nc.tensor.matmul(st[:, UV:2 * UV], qk[:, :, :].rearrange("p a k -> p (a k)"), qk[:, 0, :],
                                     start=True, stop=True)
                    nc.tensor.matmul(st[0:UV, 2 * UV:3 * UV], qk[:, 1, :], qk[:, 1, :], start=True, stop=True)
                    nc.tensor.matmul(st[0:UV, 0:UV], qk[:, 1, :], qk[:, 0, :], start=True, stop=True
                                     ).then_inc(g_made, 1)

                def norm_rows(q, n):
                    j, a = n // 2, n % 2
                    if n == 0:
                        pe.wait_ge(g_copied, q + 1)
                    nc.tensor.matmul(st[:, 0:half], grams[:, j + 1:j + 3, :].rearrange("p a k -> p (a k)"),
                                     r_sb[:, a * half:(a + 1) * half], start=True, stop=True).then_inc(half_made, 1)

                def norm_columns(q, n):
                    pe.wait_ge(half_taken, q * 4 + n + 1)
                    nc.tensor.matmul(st[:, half:2 * half], k("dw_e", UV), m1[:, :, :].rearrange("p h v -> p (h v)"),
                                     start=True, stop=True).then_inc(lam_made, 1)

                def over_positions(q, e):
                    pe.wait_ge(pk_made, q * PIECES + e + 1)
                    for n in range(rows_pk):
                        row = e * rows_pk + n
                        last = nc.tensor.matmul(st[0:UV, 0:UV], p_sb[:, row, :], pk[e % PKBUF][:, n, :],
                                                start=row == 0, stop=row == H - 1)
                    last.then_inc(pk_used, 1)

                def small_products(q):
                    pe.wait_ge(a_freed, q + 1)
                    nc.tensor.matmul(st[:, 512 + UV:512 + UV + 1], grams[:, 0:2, :].rearrange("p a k -> p (a k)"),
                                     a_sb[:, 0:1], start=True, stop=True)
                    nc.tensor.matmul(st[0:UV, 512:512 + UV], a_free[:, :], grams[:, 0, :], start=True, stop=True
                                     ).then_inc(m_made, 1)

                def values(q):
                    pe.wait_ge(mx_made, q + 1)
                    nc.tensor.matmul(st[:, 0:C], mx[:, :], vx[0:UV, :], start=True, stop=True)
                    nc.tensor.matmul(st[:, 512:512 + H], k("dw_e", UV), ms[:, :], start=True, stop=True)
                    for n in range(TS):
                        last = nc.tensor.matmul(st[:, 512 + H + n:512 + H + n + 1], vx[:, n * P:(n + 1) * P],
                                                k("p_sum", UV + 1), start=True, stop=True)
                    last.then_inc(v_made, 1)

                def stage(q, u, first=False):
                    if u == 1:
                        qkv(q, first)
                    elif u == 3:
                        gram(q)
                    elif u in (5, 7, 9, 11, 13):
                        n = (u - 5) // 2
                        if n > 0:
                            norm_columns(q, n - 1)
                        if n < 4:
                            norm_rows(q, n)
                    elif 17 <= u < 17 + PIECES // 2:
                        over_positions(q, 2 * (u - 17))
                        over_positions(q, 2 * (u - 17) + 1)
                    elif u == 27:
                        small_products(q)
                    elif u == 29:
                        values(q)

                def fill(b, u, n):
                    m, a = chunk_of(u), u % 2
                    c, slot = m % 2, (a * FILLS + n) % 2
                    if n == 0 and a == 0:
                        pe.wait_ge(scaled, b * CH2 + m + 1 + CHUNK_LEAD)
                        pe.wait_ge(zt_made, b * CH2 + m + 1)
                    pe.wait_ge(copied[slot], b * CH2 * FILLS + m * FILLS + (a * FILLS + n) // 2 + FREE)
                    for i in range(TS if n < PAIRS else PAIRS):
                        if n < PAIRS:
                            r = a * HALF + 2 * n
                            src = scaled_rows[c][:, i // S, i % S, r:r + 2, :]
                        else:
                            r = a * HALF + 2 * i
                            src = zt[c][:, r:r + 2, :]
                        last = nc.tensor.transpose(tp[slot][:, i, :], src.rearrange("p h w -> p (h w)"), k("ident"))
                    last.then_inc(transposed, 1)

                def multiply(b, u, n):
                    m, a = chunk_of(u), u % 2
                    if n == 0:
                        pe.wait_ge(copied[0], b * CH2 * FILLS + m * FILLS + (a * FILLS + FILLS + 1) // 2 + FREE)
                        pe.wait_ge(copied[1], b * CH2 * FILLS + m * FILLS + (a * FILLS + FILLS) // 2 + FREE)
                    pe.wait_ge(added[n], b * UNITS + u + FREE)
                    for r in range(HALF):
                        last = nc.tensor.matmul(ob[n][:, r, :], left[a][:, r, n, :], right[a][:, r, :],
                                                start=True, stop=True)
                    last.then_inc(multiplied, 1)

                def prologue():
                    for u in range(UNITS):
                        stage(0, u, True)
                    for n in range(FILLS):
                        fill(0, 0, n)

                def step(b, u, more):
                    for n in range(BANKS):
                        multiply(b, u, n)
                        if n < FILLS and (more or u < UNITS - 1):
                            fill(b, u + 1, n)
                    if more:
                        stage(b + 1, u)

                batches(pe, step, prologue)

            @block.scalar
            def _(act):
                act.wait_ge(const_in, 96)
                start_free(act, copied)
                act.sem_inc(scaled, CHUNK_LEAD)

                def stage(q, u):
                    if u == 2:
                        act.wait_ge(qk_made, q + 1)
                        nc.scalar.activation(qk[:, :, :].rearrange("p a k -> p (a k)"), st[0:UV, 0:2 * UV], ACT.Copy)
                        nc.scalar.activation(vx[0:UV, :], st[0:UV, 512:1024], ACT.Copy).then_inc(qk_copied, 1)
                    elif u == 4:
                        act.wait_ge(g_made, q + 1)
                        nc.scalar.activation(grams[:, 0:3, :].rearrange("p a k -> p (a k)"), st[0:UV, 0:3 * UV],
                                             ACT.Copy).then_inc(g_copied, 1)
                    elif u == 15:
                        act.wait_ge(lam2_made, q * 4 + 4)
                        nc.scalar.activation(lam[:, :, :], lam2[:, :, :], ACT.Sqrt).then_inc(root_made, 1)
                    elif u == 25:
                        act.wait_ge(pk_used, q * PIECES + PIECES)
                        nc.scalar.activation(a_sb[:, :], st[0:UV, 0:UV], ACT.Copy).then_inc(a_copied, 1)
                    elif u == 30:
                        act.wait_ge(v_made, q + 1)
                        nc.scalar.activation(vt[:, :], st[:, 0:C], ACT.Copy, scale=gam[:, 0:1]).then_inc(vt_made, 1)

                def scale(b, m, t):
                    c = m % 2
                    if t == 0:
                        act.wait_ge(interpolated, b * CH2 + m + 1)
                        act.wait_ge(transposed, (b * CH2 + m) * 2 * FILLS - 2 * FILLS + FILL_LEAD)
                    for s in range(S):
                        n = t * S + s
                        last = nc.scalar.activation(scaled_rows[c][:, t, s, :, :], mid[c][:, t, :, :], ACT.Identity,
                                                    scale=gain[:, n:n + 1], bias=shift[:, n:n + 1])
                    if t == T - 1:
                        last.then_inc(scaled, 1)

                def copy(b, u, more):
                    m, a = chunk_of(u), u % 2
                    act.wait_ge(multiplied, (b * UNITS + u) * BANKS - BANKS + UNIT_LEAD)
                    if u % UNITS < 2:
                        act.wait_ge(vt_made, b + u // UNITS + 1)
                        for rows, e in ((lo, 0), (hi, 1)):
                            nc.scalar.activation(left[a][rows, e:HALF:2, :, :].rearrange("p h n g -> p h (n g)"),
                                                 vt[rows, :].unsqueeze(1).broadcast_to([UV, PAIRS, C]), ACT.Copy)
                    for n in range(FILLS):
                        slot = (a * FILLS + n) % 2
                        act.wait_ge(transposed, (b * CH2 + m) * 2 * FILLS + a * FILLS + n + 1 + FILL_LEAD)
                        if n < PAIRS:
                            nc.scalar.activation(left[a][lo, 2 * n + 1, :, :], tp[slot][lo, :, :], ACT.Copy)
                            nc.scalar.activation(left[a][hi, 2 * n, :, :], tp[slot][hi, :, :], ACT.Copy
                                                 ).then_inc(copied[slot], 1)
                        else:
                            nc.scalar.activation(right[a][lo, 0:HALF:2, :], tp[slot][lo, 0:PAIRS, :], ACT.Copy)
                            nc.scalar.activation(right[a][hi, 1:HALF:2, :], tp[slot][hi, 0:PAIRS, :], ACT.Copy
                                                 ).then_inc(copied[slot], 1)
                        if a == 1 and n < T and (more or m < CH2 - 1):
                            scale(b, m + 1, n)

                def prologue():
                    for u in range(UNITS):
                        stage(0, u)
                    for t in range(T):
                        scale(0, 0, t)
                    copy(0, 0, True)

                def step(b, u, more):
                    if more:
                        stage(b + 1, u)
                    if more or u < UNITS - 1:
                        copy(b, u + 1, more)

                batches(act, step, prologue)

            @block.vector
            def _(dve):
                nc.vector.memset(grams[:, 3, :], 0.0).then_inc(set_up, 1)
                start_free(dve, added)
                dve.sem_inc(weighted, CHUNK_LEAD)
                dve.wait_ge(const_in, 96)
                for i in range(2):
                    for rows, e in ((hi, 0), (lo, 1)):
                        nc.vector.tensor_copy(right[i][rows, e:HALF:2, :],
                                              inter[rows, 0:W].unsqueeze(1).broadcast_to([UV, PAIRS, W])
                                              ).then_inc(set_up, 1)
                dve.wait_ge(set_up, SET_UP)

                def take_rows(q, n):
                    rows = slice(n % 2 * H // 2, (n % 2 + 1) * H // 2)
                    dve.wait_ge(half_made, q * 4 + n + 1)
                    nc.vector.tensor_tensor(
                        m1[:, :, :], st[0:UV, 0:half].rearrange("p (h v) -> p h v", v=LOW),
                        k("dh_e", UV)[:, rows].unsqueeze(2).broadcast_to([UV, H // 2, LOW]), ALU.mult
                    ).then_inc(half_taken, 1)

                def take_columns(q, n, ch):
                    rows = slice(n % 2 * H // 2, (n % 2 + 1) * H // 2)
                    if n > 0:
                        dve.wait_ge(lam2_made, q * 4 + n)
                    dve.wait_ge(lam_made, q * 4 + n + 1)
                    ch.link(nc.vector.tensor_tensor(
                        work[:, :, :], st[:, half:2 * half].rearrange("p (h v) -> p h v", v=LOW),
                        k("dw8").unsqueeze(1).broadcast_to([P, H // 2, LOW]), ALU.mult))
                    nc.vector.tensor_reduce(lam2[:, n // 2, rows], work[:, :, :], AX.X, ALU.add
                                            ).then_inc(lam2_made, 1)

                def over_lam(q, e):
                    rows = slice(e * rows_pk, (e + 1) * rows_pk)
                    if e >= PKBUF:
                        dve.wait_ge(pk_used, q * PIECES + e - PKBUF + 1)
                    nc.vector.tensor_tensor(pk[e % PKBUF][:, :, :], p_sb[:, rows, :],
                                            rk[:, rows].unsqueeze(2).broadcast_to([P, rows_pk, UV]),
                                            ALU.mult).then_inc(pk_made, 1)

                def stage(b, ahead, u, ch):
                    q = b + ahead
                    if u == 0:
                        if ahead:
                            dve.wait_ge(qk_made, q)
                        nc.vector.tensor_copy(xp[:, :, :].rearrange("p (t s) k -> p t s k", t=T),
                                              xps[:, :, :, :].rearrange("p (b t) s k -> p b t s k", t=T)[:, q, :, :, :]
                                              ).then_inc(xp_made, 1)
                    elif u in (6, 8, 10, 12, 14):
                        n = (u - 6) // 2
                        if n > 0:
                            take_columns(q, n - 1, ch)
                        if n < 4:
                            take_rows(q, n)
                    elif 16 <= u < 16 + PIECES // 2:
                        if u == 16:
                            dve.wait_ge(root_made, q + 1)
                            ch.link(nc.vector.reciprocal(rk[:, :], lam[:, 1, :]))
                        over_lam(q, 2 * (u - 16))
                        over_lam(q, 2 * (u - 16) + 1)
                    elif u == 26:
                        dve.wait_ge(a_copied, q + 1)
                        nc.vector.scalar_tensor_tensor(out=a_free[:, :], in0=k("p_row", UV), scalar=a_sb[:, 0:1],
                                                       in1=a_sb[:, :], op0=ALU.mult, op1=ALU.add
                                                       ).then_inc(a_freed, 1)
                    elif u == 28:
                        dve.wait_ge(m_made, q + 1)
                        nc.vector.tensor_copy(mx[:, :].rearrange("p (e k) -> p e k", e=2),
                                              st[0:UV, 512:512 + UV].unsqueeze(1).broadcast_to([UV, 2, UV]))
                        nc.vector.tensor_scalar(ms[:, :], k("dh_e", UV), st[0:UV, 512 + UV:512 + UV + 1], float(P),
                                                ALU.mult, ALU.mult).then_inc(mx_made, 1)
                    elif u == 30:
                        dve.wait_ge(v_made, q + 1)
                        ch.link(nc.vector.scalar_tensor_tensor(out=den[:, :], in0=lam[:, 0, :], scalar=float(HW),
                                                               in1=st[:, 512:512 + H], op0=ALU.mult, op1=ALU.add))
                        dve.wait_ge(scaled, q * CH2 + CHUNK_LEAD)
                        nc.vector.tensor_copy(gain[:, :].rearrange("p (t s) -> p t s", t=T), coef[:, q, :, :])
                        nc.vector.tensor_scalar(shift[:, :], st[:, 512 + H:512 + H + TS], gam[:, 0:1], None, ALU.mult)
                        ch.link(nc.vector.reciprocal(rr[:, :], den[:, :]))
                        dve.sem_inc(factors_made, 1)

                def weight(b, m, part_n):
                    c, n = m % 2, m % CH2
                    e, r = part_n // 2, part_n % 2
                    if part_n == 0:
                        if c == 0:
                            loads = (m // CH2) * (CH2 // 2 + 1) + n // 2 + 1 + 1
                        else:
                            loads = (m // CH2) * (CH2 // 2 + 1) + n // 2 + 1 + (n == CH2 - 1)
                        dve.wait_ge(dd_in[c], b * (CH2 // 2 + 1) * 16 + loads * 16)
                        dve.wait_ge(scaled, b * CH2 + m + CHUNK_LEAD - 1)
                        if m > 0:
                            dve.wait_ge(interpolated, b * CH2 + m)
                    last = nc.vector.tensor_tensor(
                        (mid[c], part)[r][:, :, :, :].rearrange("p t (i e) w -> p t i e w", e=2)[:, :, :, 1 - e, :],
                        dd[c][:, :, e + r:e + r + DROWS, :],
                        row_w[:, 2 * e + r, n * DROWS:(n + 1) * DROWS].unsqueeze(1).unsqueeze(3)
                        .broadcast_to([P, T, DROWS, WD]), ALU.mult)
                    if part_n == 3:
                        last.then_inc(weighted, 1)

                def interpolate(b, m):
                    c = m % 2
                    dve.wait_ge(weighted, b * CH2 + m + 1 + CHUNK_LEAD)
                    nc.vector.tensor_tensor(mid[c][:, :, :, :], mid[c][:, :, :, :], part[:, :, :, :], ALU.add
                                            ).then_inc(interpolated, 1)

                def frequencies(b, m):
                    c, n = m % 2, m % CH2
                    dve.wait_ge(transposed, (b * CH2 + m) * 2 * FILLS - 2 * FILLS + FILL_LEAD)
                    rows = slice(n * ROWS2, (n + 1) * ROWS2)
                    nc.vector.tensor_tensor(zt[c][:, :, :], p_sb[:, rows, :],
                                            rr[:, rows].unsqueeze(2).broadcast_to([P, ROWS2, UV]),
                                            ALU.mult).then_inc(zt_made, 1)

                def add(b, u, n):
                    i = u % XBUF
                    if n == 0:
                        dve.wait_ge(x_in[i], (b * (UNITS // XBUF) + u // XBUF) * T * 16 + T * 16)
                    dve.wait_ge(multiplied, (b * UNITS + u) * BANKS + n + 1 + UNIT_LEAD)
                    nc.vector.tensor_tensor(xt[i][:, n // S, n % S, :, :], ob[n][:, :, :],
                                            xt[i][:, n // S, n % S, :, :], ALU.add).then_inc(added[n], 1)

                links = 7

                def prologue():
                    ch = Chain(dve, chain_sem)
                    for u in range(UNITS):
                        stage(0, 0, u, ch)
                    assert ch.n == links
                    for n in range(4):
                        weight(0, 0, n)
                    interpolate(0, 0)
                    frequencies(0, 0)
                    for n in range(4):
                        weight(0, 1, n)

                chains = {}

                def step(b, u, more):
                    m = chunk_of(u)
                    if u == 0 and more:
                        chains[0] = Chain(dve, chain_sem, b * links + links)
                    if u == UNITS - 2 and more:
                        stage(b, 1, u, chains[0])
                    if u % 2 == 0 and (more or m + 1 < CH2):
                        interpolate(b, m + 1)
                    for n in range(BANKS):
                        add(b, u, n)
                        if u % 2 == 0 and n == 0 and (more or m + 1 < CH2):
                            frequencies(b, m + 1)
                        if u % 2 == 1 and (more or m + 2 < CH2):
                            weight(b, m + 2, n)
                    if u != UNITS - 2 and more:
                        stage(b, 1, u, chains[0])

                batches(dve, step, prologue)


def program(nc, x, w_down, w_conv, w_up, wqk, wv, bias, gamma, consts, p_cols, q_cols, r_cols, inter_cols, out):
    xd = nc.dram_tensor("downsampled", (B, T, P, POS), F32, kind="Internal").ap()
    with Scope(nc, "all") as sc:
        cst = sc.sb("const", [P, CONST_N])
        p_sb = sc.sb("p", [P, H, UV])
        xps = sc.sb("xps", [P, B * T, S, UV])
        coef = sc.sb("coef", [P, B, T, S])
        first_pass(nc, x, w_down, p_cols, consts, cst, p_sb, xd, xps)
        with Scope(nc, "gates") as sg:
            ohn = sg.sb("ohn", [P, T, K])
            oh_t = sg.sb("oh_t", [P, T, P])
            cluster_pass(nc, cst, xd, ohn, oh_t)
            xpu = sg.sb("xpu", [P, B * T, UV])
            ft = sg.sb("ft", [P, NT, P])
            average_pass(nc, cst, q_cols, xd, ohn, ft, xpu)
            feat = sg.sb("feat", [P, NT, P])
            mixture_pass(nc, cst, w_conv, w_up, ft, feat, oh_t, xps, xpu, coef)
        second_pass(nc, x, cst, p_sb, r_cols, inter_cols, wqk, wv, bias, gamma, xd, xps, coef, out)


def shape_constants():
    import numpy as np

    f = np.float32
    ind = 2.0 * np.arange(H) + 1.0
    d = np.stack([np.sqrt(2.0) / np.sqrt(H) * np.cos(u * ind * np.pi / (2.0 * H)) for u in range(LOW)]).astype(f)
    d[0, :] = 1.0 / np.sqrt(H)
    d = d.T
    p = (d[:, None, :, None] * d[None, :, None, :]).astype(f)
    p_cols = p.transpose(1, 0, 2, 3).reshape(W, H * UV)
    s = np.linspace(0.0, HD - 1.0, H).astype(f)
    i0 = np.floor(s).astype(int)
    i1 = np.minimum(i0 + 1, HD - 1)
    fr = (s - i0.astype(f)).astype(f)
    inter = np.zeros((H, HD), f)
    for h in range(H):
        inter[h, i0[h]] += f(1) - fr[h]
        inter[h, i1[h]] += fr[h]
    du = inter.astype(np.float64).T @ d.astype(np.float64)
    q = (du[:, None, :, None] * du[None, :, None, :]).astype(f).reshape(NT, P, UV)
    q_cols = q.transpose(1, 0, 2).reshape(P, NT * UV)
    above = [0.0] + [inter[2 * i, i - 1] for i in range(1, HD)]
    below = [inter[2 * i, i] for i in range(HD)]
    here = [inter[2 * i + 1, i] for i in range(HD)]
    under = [inter[2 * i + 1, i + 1] for i in range(HD - 1)] + [0.0]
    inter_cols = np.concatenate([np.concatenate([inter.T] * 2)] +
                                [np.tile(np.asarray(v, f), (P, 1)) for v in (above, below, here, under)], 1)
    r = np.zeros((LOW, LOW, H, LOW), f)
    for v in range(LOW):
        r[:, v, :, v] = d.T
    r_cols = r.reshape(UV, H * LOW)

    row = np.arange(P)
    rb, rf, rk = row // 16, row // 8 % 2, row % 8
    col_b = np.arange(BN) // N
    block = (rb[:, None] == col_b[None, :]).astype(f)
    picks = np.round(np.linspace(0.0, C // 2 - 1.0, K)).astype(int)
    p_sum = p.sum((0, 1), dtype=np.float64).reshape(UV)
    wide = {
        "ident": np.eye(P), "ones": np.ones((P, P)),
        "sel_mu": row[:, None] == (rb * 16 + rk)[None, :], "sel_ex": row[:, None] == (rb * 16 + 8 + rk)[None, :],
        "mask_x": block * (rf == 0)[:, None], "mask_x2": -0.5 * block * (rf == 1)[:, None],
        "mask_term": -0.5 * block * (rf == 0)[:, None], "block": block,
        "block_k": (rb[:, None] == np.arange(B)[None, :]) & (rf == 0)[:, None],
        "is_x2": (rf == 1)[:, None], "tie": np.tile(np.arange(K, 0, -1), (P, 1)),
        "before": np.tile((np.arange(K)[None, :] < np.arange(K)[:, None]).reshape(1, -1), (P, 1)),
        "pick0": (row[:, None, None] + P * np.arange(T)[None, :, None] == picks[None, None, :]).reshape(P, T * K),
        "dw8": d, "dh_e": np.concatenate([np.repeat(d.T, LOW, 0)] * 2), "dw_e": np.concatenate([d.T] * (P // LOW)),
        "p_sum": np.concatenate([p_sum.reshape(UV, 1) / HW, np.ones((P - UV, 1))]),
        "p_row": np.tile(-p_sum / P, (P, 1)), "rank": row[:, None],
        "is_x": (rf == 0)[:, None],
        "own_rows": np.tile((np.arange(2 * B)[None, :] // 2 == np.arange(B)[:, None]).reshape(1, -1), (P, 1)),
    }
    consts = np.concatenate([np.asarray(wide[n]).astype(f).reshape(P, w) for n, w in CONST_COLS], 1)
    return {"consts": consts, "p_cols": p_cols, "q_cols": q_cols, "r_cols": r_cols, "inter_cols": inter_cols}


def kernel(x, L0_conv_w_down, L0_conv_w_conv, L0_conv_w_up, L1_conv_Wq, L1_conv_Wk, L1_conv_Wv, L1_conv_out_bias,
           L1_conv_gamma):
    import numpy as np
    import concourse.bacc as bacc
    from concourse.bass_utils import run_bass_kernel_spmd

    def by_group(w):
        return np.asarray(w).reshape(-1, T, P, S).transpose(2, 1, 3, 0).reshape(P, TS, -1)

    wv = by_group(L1_conv_Wv).reshape(P, TS, T, P, S).transpose(0, 1, 2, 4, 3).reshape(P, TS, C)
    arrays = {
        "x": x, "w_down": L0_conv_w_down, "w_conv": L0_conv_w_conv, "w_up": L0_conv_w_up,
        "wqk": np.concatenate([by_group(L1_conv_Wq), by_group(L1_conv_Wk)], 2), "wv": wv,
        "bias": np.asarray(L1_conv_out_bias).reshape(T, P, S).transpose(0, 2, 1).reshape(1, C),
        "gamma": L1_conv_gamma, **shape_constants(),
    }
    arrays = {f"in_{n}": np.ascontiguousarray(a) for n, a in arrays.items()}
    nc = bacc.Bacc("TRN2", target_bir_lowering=False, num_devices=1)
    args = {n[3:]: nc.dram_tensor(n, a.shape, mybir.dt.from_np(a.dtype), kind="ExternalInput").ap()
            for n, a in arrays.items()}
    out = nc.dram_tensor("out", (B, C, H, W), F32, kind="ExternalOutput").ap()
    program(nc, out=out, **args)
    r = run_bass_kernel_spmd(nc, [arrays], core_ids=[0])
    return r.results[0]["out"]
```
